# Optimizing a Trainium2 kernel written in Bass

```python
import numpy as np
import jax
import jax.numpy as jnp

def _softmax(x, axis=-1):
    return jax.nn.softmax(x, axis=axis)

def _gelu(x):
    return jax.nn.gelu(x, approximate=True)

def _silu(x):
    return jax.nn.silu(x)

def _sigmoid(x):
    return jax.nn.sigmoid(x)

def _layernorm(x, axis=-1, eps=1e-05):
    m = jnp.mean(x, axis=axis, keepdims=True)
    v = jnp.var(x, axis=axis, keepdims=True)
    return (x - m) / jnp.sqrt(v + eps)

def _scatter_add(tgt, idx, src, axis=0):
    return tgt.at[idx].add(src)

def _segment_sum(src, seg, n):
    return jax.ops.segment_sum(src, seg, n)
kernel_name = 'mk_adj_preln_d2_adj_r2_e2577a'

def setup_inputs(seed: int=0):
    np.random.seed(seed)
    _w = jnp.asarray

    def _rec_inputs():
        import jax
        import jax.numpy as jnp
        _gk = jax.random.key(seed)
        x = -0.0004776 + 1.001 * jax.random.normal(jax.random.fold_in(_gk, 1), (2048, 512), jnp.float32)
        _w = (1.0 + jnp.arange(2048, dtype=jnp.float32)) ** (-0.5)
        _w = _w / _w.mean()
        _pij = jnp.clip(0.000976562 * _w[:, None] * _w[None, :], 0.0, 1.0)
        _a = jax.random.uniform(jax.random.fold_in(_gk, 2), (2048, 2048)) < _pij
        _a = jnp.logical_or(_a, jnp.eye(2048, dtype=bool))
        _af = _a.astype(jnp.float32)
        adj = _af
        return (x, adj)
    x, adj = _rec_inputs()

    def _L0_gnn_setup():
        import jax, jax.numpy as jnp
        import numpy as np
        N, H, E, HEADS = (1500, 512, 10000, 8)
        DK = H // HEADS
        key = jax.random.key(seed)
        k1, k2, k3, k4 = jax.random.split(key, 4)
        inst_feature = jax.random.normal(k1, (N, H), dtype=jnp.float32)
        rel_pair_index = jax.random.randint(k2, (E, 2), 0, N, dtype=jnp.int64)
        agg = jnp.zeros((N, N), dtype=jnp.float32)
        agg = agg.at[rel_pair_index[:, 0], rel_pair_index[:, 1]].set(1.0)
        agg = agg.at[jnp.arange(N), jnp.arange(N)].set(1.0)
        std = float(np.sqrt(2.0 / (H + DK)))
        Wq = jax.random.normal(k3, (H, H), dtype=jnp.float32) * std
        Wk = jax.random.normal(k4, (H, H), dtype=jnp.float32) * std
        bq = jnp.zeros((H,), dtype=jnp.float32)
        bk = jnp.zeros((H,), dtype=jnp.float32)
        return {'inst_feature': inst_feature, 'aggregator_matrix': agg, 'rel_pair_index': rel_pair_index, 'Wq': Wq, 'bq': bq, 'Wk': Wk, 'bk': bk}
    _L0_gnn_all = _L0_gnn_setup()
    _L0_gnn_in = {k: v for k, v in _L0_gnn_all.items() if k in ('rel_pair_index', 'Wq', 'bq', 'Wk', 'bk')}
    del _L0_gnn_all

    def _L1_gnn_setup():
        import jax, jax.numpy as jnp
        import numpy as np
        N = 2048
        D_IN = 512
        H = 16
        DH = D_IN // H
        ALPHA = 0.2
        MASK_VAL = -65500.0
        key = jax.random.key(seed)
        ks = jax.random.split(key, 7)
        x = jax.random.normal(ks[0], (N, D_IN), dtype=jnp.float32)
        adj = jax.random.randint(ks[1], (N, N), 0, 2).astype(jnp.float32)
        s = 1.0 / np.sqrt(D_IN)
        W_seq = jax.random.normal(ks[2], (D_IN, D_IN), dtype=jnp.float32) * s
        a1 = jax.random.normal(ks[3], (DH,), dtype=jnp.float32) / np.sqrt(DH)
        a2 = jax.random.normal(ks[4], (DH,), dtype=jnp.float32) / np.sqrt(DH)
        W_out = jax.random.normal(ks[5], (D_IN, D_IN), dtype=jnp.float32) * s
        b_out = jax.random.normal(ks[6], (D_IN,), dtype=jnp.float32) * 0.01
        return {'x': x, 'adj': adj, 'W_seq': W_seq, 'a1': a1, 'a2': a2, 'W_out': W_out, 'b_out': b_out}
    _L1_gnn_all = _L1_gnn_setup()
    _L1_gnn_in = {k: v for k, v in _L1_gnn_all.items() if k in ('W_seq', 'a1', 'a2', 'W_out', 'b_out')}
    del _L1_gnn_all
    return {'x': x, 'adj': adj, 'L0_gnn_rel_pair_index': _L0_gnn_in['rel_pair_index'], 'L0_gnn_Wq': _L0_gnn_in['Wq'], 'L0_gnn_bq': _L0_gnn_in['bq'], 'L0_gnn_Wk': _L0_gnn_in['Wk'], 'L0_gnn_bk': _L0_gnn_in['bk'], 'L1_gnn_W_seq': _L1_gnn_in['W_seq'], 'L1_gnn_a1': _L1_gnn_in['a1'], 'L1_gnn_a2': _L1_gnn_in['a2'], 'L1_gnn_W_out': _L1_gnn_in['W_out'], 'L1_gnn_b_out': _L1_gnn_in['b_out']}

def reference(x, adj, L0_gnn_rel_pair_index, L0_gnn_Wq, L0_gnn_bq, L0_gnn_Wk, L0_gnn_bk, L1_gnn_W_seq, L1_gnn_a1, L1_gnn_a2, L1_gnn_W_out, L1_gnn_b_out):
    import jax
    import jax.numpy as jnp

    def _L0_gnn_ref(inst_feature, aggregator_matrix, rel_pair_index, Wq, bq, Wk, bk):
        import jax, jax.numpy as jnp
        import numpy as np
        N, H, E, HEADS = (1500, 512, 10000, 8)
        DK = H // HEADS
        n = inst_feature.shape[0]
        sub = rel_pair_index[:, 0]
        obj = rel_pair_index[:, 1]
        q = (inst_feature[sub] @ Wq.T + bq).reshape(-1, HEADS, DK)
        k = (inst_feature[obj] @ Wk.T + bk).reshape(-1, HEADS, DK)
        att = ((q * k).sum(-1) / np.sqrt(DK)).T.astype(inst_feature.dtype)
        scores = jnp.zeros((HEADS, n, n), dtype=inst_feature.dtype)
        scores = scores.at[:, sub, obj].set(att)
        mask = (1.0 - aggregator_matrix).astype(bool)
        scores = jnp.where(mask[None], -jnp.inf, scores)
        di = jnp.arange(n)
        scores = scores.at[:, di, di].set(1e-07)
        attn = jax.nn.softmax(scores, axis=2)
        aggregator_factor = attn.sum(axis=0) / HEADS
        return aggregator_factor @ inst_feature

    def _L1_gnn_ref(x, adj, W_seq, a1, a2, W_out, b_out):
        import jax, jax.numpy as jnp
        import numpy as np
        N = 2048
        D_IN = 512
        H = 16
        DH = D_IN // H
        ALPHA = 0.2
        MASK_VAL = -65500.0
        seq = (x @ W_seq).reshape(N, H, DH)
        score1 = jnp.einsum('nhd,d->hn', seq, a1)
        score2 = jnp.einsum('nhd,d->hn', seq, a2)
        scores = score1[:, :, None] + score2[:, None, :]
        scores = jax.nn.leaky_relu(scores, negative_slope=ALPHA)
        scores = scores + (1.0 - adj)[None, :, :] * MASK_VAL
        attn = jax.nn.softmax(scores, axis=-1)
        hidden = jnp.einsum('hij,jhd->ihd', attn, seq).reshape(N, D_IN)
        hidden = hidden @ W_out + b_out
        return jax.nn.elu(hidden)
    h = jnp.maximum(_layernorm(x, axis=-1), 0.0)
    x = x + _L0_gnn_ref(h, adj, L0_gnn_rel_pair_index, L0_gnn_Wq, L0_gnn_bq, L0_gnn_Wk, L0_gnn_bk)
    h = jnp.maximum(_layernorm(x, axis=-1), 0.0)
    x = x + _L1_gnn_ref(h, adj, L1_gnn_W_seq, L1_gnn_a1, L1_gnn_a2, L1_gnn_W_out, L1_gnn_b_out)
    return x

_drawn_inputs = setup_inputs


def setup_inputs(seed=0):
    import zlib

    import numpy as np

    out = dict(_drawn_inputs(seed))
    spreads = {'L0_gnn_bq': (0.0, 2.0), 'L0_gnn_bk': (0.0, 2.0)}
    factors = {'L0_gnn_Wq': 200.0, 'L0_gnn_Wk': 200.0, 'L1_gnn_a1': 2.745, 'L1_gnn_b_out': 8.0}
    for name, (base, spread) in spreads.items():
        noise = np.random.default_rng([zlib.crc32(name.encode()), seed]).standard_normal(out[name].shape)
        drawn = base * np.exp(spread * noise) if base else spread * noise
        out[name] = jnp.asarray(drawn.astype(out[name].dtype))
    for name, factor in factors.items():
        out[name] = (out[name] * factor).astype(out[name].dtype)
    return out
```

```python
from contextlib import ExitStack

import concourse.bass as bass
from concourse import mybir

F32 = mybir.dt.float32
BF16 = mybir.dt.bfloat16
I32 = mybir.dt.int32
U32 = mybir.dt.uint32
ALU = mybir.AluOpType
ACT = mybir.ActivationFunctionType
AX = mybir.AxisListType

P = 128
N = 2048
D = 512
NT = N // P
KT = D // P
EPS = 1e-5

NREL = 1500
ET = -(-NREL // P)
NE = ET * P
E = 10000
EP = 125
EC = E // EP
HA = 8
DK = D // HA
CH = NE // 512
BIG = float(2.0 ** 100)
DIAG = 1e-7

HB = 16
DH = D // HB
DZ = DH + 1
GH = 8
NG = HB // GH
SLOPE = 0.2
SHIFT = 40.0


def make_constants(nc, t, s):
    with nc.Block() as block:
        @block.gpsimd
        def _(pool):
            pool.memset(t["ident"][:, :], 0.0).then_inc(s["zeroed"], 1)
            pool.memset(t["identb"][:, :], 0.0).then_inc(s["zeroed"], 1)
            pool.memset(t["offdiag"][:, :], 1.0).then_inc(s["zeroed"], 1)
            pool.wait_ge(s["zeroed"], 3)
            for m, fill in ((t["ident"], 1.0), (t["identb"], 1.0), (t["offdiag"], 0.0)):
                pool.affine_select(out=m[:, :], in_=m[:, :], compare_op=ALU.not_equal, fill=fill, base=0,
                                   pattern=[[-1, P]], channel_multiplier=1).then_inc(s["const"], 1)


def stage1(nc, c, io, t, s, ps):
    sb = lambda name, shape, dt=F32: c.enter_context(nc.sbuf_tensor(name, shape, dt))
    sem = lambda name: c.enter_context(nc.semaphore(name))
    xs = sb("s1_x", [P, NT, D])
    wnat = [sb(f"s1_w{i}", [P, KT, D]) for i in range(2)]
    wT = [sb(f"s1_wT{i}", [P, KT, D]) for i in range(2)]
    bias = sb("s1_bias", [P, 2, KT])
    bias8 = sb("s1_bias8", [P, KT])
    hT = sb("s1_hT", [P, KT, NE])
    stats = sb("s1_stats", [P, NT, 6])
    mv = sb("s1_mv", [P, NT, 2])
    std = sb("s1_std", [P, NT])
    rstd = sb("s1_rstd", [P, NT])
    nmr = sb("s1_nmr", [P, NT])
    full = sb("s1_full", [P, 2, 512])
    parts = sb("s1_parts", [P, 2, 3, 512], BF16)
    zero = sb("s1_zero", [P, NE], BF16)
    ones = sb("s1_ones", [P, 1], BF16)
    rel = sb("s1_rel", [P, EC, 2], I32)
    flat = sb("s1_flat", [P, EC], U32)
    h = t["h"]

    x_in = [sem(f"s1_x_in{i}") for i in range(4)]
    w_in, bias_in, rel_in = sem("s1_w_in"), sem("s1_bias_in"), sem("s1_rel_in")
    zero_set, table_zero, flat_ready = sem("s1_zero_set"), sem("s1_table_zero"), sem("s1_flat")
    related = [sem(f"s1_related{i}") for i in range(2)]
    stat, var_ready, std_ready, norm_ready, h_ready = (sem("s1_stat"), sem("s1_var"), sem("s1_std"), sem("s1_norm"),
                                                       sem("s1_h"))
    wT_psum, wT_ready, hT_psum, hT_ready = sem("s1_wTp"), sem("s1_wT"), sem("s1_hTp"), sem("s1_hT")
    bias_ready, proj, full_ready, split_step, parts_ready = (sem("s1_b8"), sem("s1_proj"), sem("s1_full"),
                                                             sem("s1_split"), sem("s1_parts"))
    parts_out = [sem(f"s1_parts_out{i}") for i in range(2)]
    groups = [(w, dt, ch) for w in (1, 0) for dt in range(KT) for ch in range(CH)]
    G = len(groups)

    with nc.Block() as block:
        @block.sync
        def _(sp):
            for i, w in enumerate((io["L0_gnn_Wq"], io["L0_gnn_Wk"])):
                sp.dma_start(wnat[i][:, :, :], w.rearrange("(t p) k -> p t k", p=P)).then_inc(w_in, 16)
            for i in range(4):
                sp.dma_start(xs[:, 4 * i:4 * i + 4, :],
                             io["x"][512 * i:512 * i + 512, :].rearrange("(t p) k -> p t k", p=P)).then_inc(x_in[i], 16)
            for g, (w, dt, ch) in enumerate(groups):
                sp.wait_ge(parts_ready, g + 1)
                dst = t["q_parts" if w == 0 else "k_parts"]
                sp.dma_start(dst[:, dt * P:(dt + 1) * P, ch * 512:(ch + 1) * 512].rearrange("s p i -> p s i"),
                             parts[:, g % 2, :, :]).then_inc(parts_out[g % 2], 16)
            for i in range(2):
                sp.wait_ge(parts_out[i], 16 * G // 2)

        @block.gpsimd
        def _(pool):
            pool.memset(zero[:, :], 0.0).then_inc(zero_set, 1)
            pool.memset(ones[:, :], 1.0).then_inc(zero_set, 1)
            pool.dma_start(rel[0:EP, :, :], io["L0_gnn_rel_pair_index"].rearrange("(p c) s -> p c s", p=EP)).then_inc(rel_in, 16)
            pool.wait_ge(zero_set, 2)
            for i in range(2):
                pool.dma_start(t["rel_table"][i].rearrange("(t p) j -> p t j", p=P),
                               zero[:, None, :].to_broadcast([P, ET, NE])).then_inc(table_zero, 16)
            for i, b in enumerate((io["L0_gnn_bq"], io["L0_gnn_bk"])):
                pool.dma_start(bias[:, i, :], b.rearrange("(t p) -> p t", p=P),
                               allow_slow_non_contiguous=True).then_inc(bias_in, 16)
            pool.wait_ge(table_zero, 32)
            pool.wait_ge(flat_ready, 1)
            for e in range(EC):
                if e >= 2:
                    pool.wait_ge(related[e % 2], 16 * (e // 2))
                pool.indirect_dma_start(t["rel_table"][e % 2].rearrange("i (j o) -> (i j) o", o=1),
                                        bass.IndirectOffsetOnAxis(ap=flat[0:EP, e:e + 1], axis=0),
                                        ones[0:EP, 0:1], None).then_inc(related[e % 2], 16)
            for i in range(2):
                pool.wait_ge(related[i], 16 * EC // 2)

        @block.vector
        def _(dve):
            dve.wait_ge(rel_in, 16)
            dve.scalar_tensor_tensor(flat[0:EP, :], rel[0:EP, :, 0], float(NE), rel[0:EP, :, 1], ALU.mult,
                                     ALU.add).then_inc(flat_ready, 1)
            dve.wait_ge(bias_in, 32)
            dve.tensor_scalar(bias8[:, :], bias[:, 0, :], DK ** -0.5, None, ALU.mult).then_inc(bias_ready, 1)
            for k in range(8):
                dve.wait_ge(wT_psum, k + 1)
                dve.tensor_copy(wT[k // KT][:, k % KT, :], ps[:, k, :]).then_inc(wT_ready, 1)
            for i in range(NT):
                if i % 4 == 0:
                    dve.wait_ge(x_in[i // 4], 16)
                dve.bn_stats(stats[:, i, :], xs[:, i, :]).then_inc(stat, 1)
            dve.wait_ge(stat, NT)
            for i in range(NT):
                dve.bn_aggr(mv[:, i, :], stats[:, i, :]).then_inc(stat, 1)
            dve.wait_ge(stat, 2 * NT)
            dve.tensor_scalar(rstd[:, :], mv[:, :, 1], EPS, None, ALU.add).then_inc(var_ready, 1)
            dve.wait_ge(std_ready, 1)
            dve.reciprocal(rstd[:, :], std[:, :]).then_inc(var_ready, 1)
            dve.wait_ge(var_ready, 2)
            dve.scalar_tensor_tensor(nmr[:, :], mv[:, :, 0], -1.0, rstd[:, :], ALU.mult, ALU.mult).then_inc(norm_ready, 1)
            for i in range(ET):
                dve.wait_ge(hT_psum, i + 1)
                dve.tensor_copy(hT[:, :, i * P:(i + 1) * P],
                                ps[:, i % 4, :].rearrange("p (k i) -> p k i", k=KT)).then_inc(hT_ready, 1)
            for g in range(G):
                v, q = full[:, g % 2, :], parts[:, g % 2, :, :]
                dve.wait_ge(full_ready, g + 1)
                if g >= 2:
                    dve.wait_ge(parts_out[g % 2], 16 * (g // 2))
                dve.tensor_copy(q[:, 0, :], v).then_inc(split_step, 1)
                dve.wait_ge(split_step, 3 * g + 1)
                dve.tensor_tensor(v, v, q[:, 0, :], ALU.subtract).then_inc(split_step, 1)
                dve.wait_ge(split_step, 3 * g + 2)
                dve.tensor_copy(q[:, 1, :], v).then_inc(split_step, 1)
                dve.wait_ge(split_step, 3 * g + 3)
                dve.tensor_tensor(q[:, 2, :], v, q[:, 1, :], ALU.subtract).then_inc(parts_ready, 1)

        @block.scalar
        def _(act):
            act.wait_ge(var_ready, 1)
            act.activation(std[:, :], rstd[:, :], ACT.Sqrt).then_inc(std_ready, 1)
            act.wait_ge(norm_ready, 1)
            for i in range(NT):
                act.activation(h[:, i, :], xs[:, i, :], ACT.Relu, bias=nmr[:, i:i + 1],
                               scale=rstd[:, i:i + 1]).then_inc(h_ready, 1)
            act.wait_ge(bias_ready, 1)
            for g, (w, dt, ch) in enumerate(groups):
                act.wait_ge(proj, g + 1)
                if g >= 2:
                    act.wait_ge(parts_ready, g - 1)
                b = bias8[:, dt:dt + 1] if w == 0 else bias[:, 1, dt:dt + 1]
                act.activation(full[:, g % 2, :], ps[:, 4 + g % 4, :], ACT.Identity, bias=b,
                               scale=DK ** -0.5 if w == 0 else 1.0).then_inc(full_ready, 1)

        @block.tensor
        def _(pe):
            pe.wait_ge(s["const"], 3)
            pe.wait_ge(w_in, 32)
            for k in range(8):
                for dt in range(KT):
                    last = pe.transpose(ps[:, k, dt * P:(dt + 1) * P],
                                        wnat[k // KT][:, dt, (k % KT) * P:(k % KT + 1) * P], t["ident"][:, :])
                last.then_inc(wT_psum, 1)
            for i in range(ET):
                pe.wait_ge(h_ready, i + 1)
                pe.wait_ge(wT_ready, 8)
                if i >= 4:
                    pe.wait_ge(hT_ready, i - 3)
                for k in range(KT):
                    last = pe.transpose(ps[:, i % 4, k * P:(k + 1) * P], h[:, i, k * P:(k + 1) * P], t["ident"][:, :])
                last.then_inc(hT_psum, 1)
            pe.wait_ge(hT_ready, ET)
            for g, (w, dt, ch) in enumerate(groups):
                if g >= 4:
                    pe.wait_ge(full_ready, g - 3)
                for k in range(KT):
                    last = pe.matmul(ps[:, 4 + g % 4, :], wT[w][:, k, dt * P:(dt + 1) * P],
                                     hT[:, k, ch * 512:(ch + 1) * 512], start=(k == 0), stop=(k == KT - 1))
                last.then_inc(proj, 1)



class At:

    def __init__(self, pair, n):
        self.pair, self.n = pair, n

    def at(self, off=0):
        return 2 * self.pair + (self.n + off)

    def half(self, off=0):
        return self.pair + (self.n + off) // 2

    def par(self, off=0):
        return (self.n + off) % 2

    def rows(self, off=0):
        return bass.ds(self.at(off) * P, P)


def stage2(nc, c, io, t, s, ps):
    sb = lambda name, shape, dt=F32: c.enter_context(nc.sbuf_tensor(name, shape, dt))
    sem = lambda name: c.enter_context(nc.semaphore(name))
    h = t["h"]
    k1 = sb("s2_k1", [P, HA, NE], BF16)
    k2 = sb("s2_k2", [P, HA, NE], BF16)
    qs = [sb(f"s2_q{i}", [P, 3, HA, P], BF16) for i in range(2)]
    adjn = sb("s2_adj", [P, 4, N], BF16)
    rel = [sb(f"s2_rel{i}", [P, 2, NE], BF16) for i in range(2)]
    low = [sb(f"s2_low{i}", [P, NE], BF16) for i in range(2)]
    ex = sb("s2_exp", [P, HA, NE])
    W = [sb(f"s2_W{i}", [P, N]) for i in range(2)]
    WT = [sb(f"s2_WT{i}", [P, 2, P]) for i in range(2)]
    xt = [sb(f"s2_x{i}", [P, D]) for i in range(2)]
    junk = sb("s2_junk", [P, N], BF16)
    junkv = sb("s2_junkv", [P, NE], BF16)
    negm = sb("s2_negm", [P, 2, HA])
    negd = sb("s2_negd", [P, HA])
    zs = sb("s2_zs", [P, 2, HA])
    n0 = sb("s2_n0", [P, 2])
    e0 = sb("s2_e0", [P, 3, HA])
    e1 = sb("s2_e1", [P, 3, HA])
    z = sb("s2_z", [P, HA])
    rz = sb("s2_rz", [P, HA])
    r8 = sb("s2_r8", [P, HA])
    re = sb("s2_re", [P, 2, HA])
    cd = sb("s2_cd", [P, 2])
    diag = sb("s2_diag", [P, 1])

    k_in = sem("s2_k_in")
    q_in = [sem(f"s2_q_in{i}") for i in range(2)]
    rel_in = [sem(f"s2_rel_in{i}") for i in range(2)]
    adj_in = [sem(f"s2_adj_in{i}") for i in range(2)]
    x_in = [sem(f"s2_x_in{i}") for i in range(2)]
    y_out = [sem(f"s2_y_out{i}") for i in range(2)]
    mask_step, unrelated, low_ready, adjn_ready = (sem("s2_mask_step"), sem("s2_unrelated"), sem("s2_low"),
                                                   sem("s2_adjn"))
    consts, consts_e = sem("s2_consts"), sem("s2_consts_e")
    scores, negmax, exped, rowsum, efac = sem("s2_scores"), sem("s2_negmax"), sem("s2_exped"), sem("s2_rowsum"), sem("s2_efac")
    fac, added, tail, w_ready = sem("s2_fac"), sem("s2_added"), sem("s2_tail"), sem("s2_w_ready")
    turned, turned_out, agg, summed = sem("s2_turned"), sem("s2_turned_out"), sem("s2_agg"), sem("s2_summed")

    def steps(eng, step, has):
        for it in (-2, -1, 0, 1):
            step(At(0, it), lambda off, lo, hi, it=it: lo <= it + off < hi)
        with eng.Fori(0, (ET - 4) // 2) as pair:
            for n in (2, 3):
                step(At(pair, n), lambda off, lo, hi: True)
        for it in range(ET - 2, NT + 1):
            step(At(0, it), lambda off, lo, hi, it=it: lo <= it + off < hi)

    with nc.Block() as block:
        @block.sync
        def _(sp):
            def rows(parts, n):
                return parts[n, :, :].rearrange("(h p) j -> p h j", p=DK)
            for dst, a, b in ((k1, 0, 1), (k2, 2, 0)):
                sp.dma_start(dst[0:DK, :, :], rows(t["k_parts"], a)).then_inc(k_in, 16)
                sp.dma_start(dst[DK:P, :, :], rows(t["k_parts"], b)).then_inc(k_in, 16)

            def step(it, has):
                if has(2, 0, ET):
                    q, b = it.par(2), it.par(2)
                    if has(0, 0, ET):
                        sp.wait_ge(scores, HA * it.at(1))
                    for lo, kind, part in ((0, 0, 0), (DK, 0, 0), (0, 1, 1), (DK, 1, 1), (0, 2, 0), (DK, 2, 2)):
                        sp.dma_start(qs[q][lo:lo + DK, kind, :, :],
                                     rows(t["q_parts"], part)[:, :, it.rows(2)]).then_inc(q_in[q], 16)
                    if has(0, 0, ET):
                        sp.wait_ge(adjn_ready, it.at(1))
                    for i in range(2):
                        sp.dma_start(rel[b][:, i, :], t["rel_table"][i][it.rows(2), :]).then_inc(rel_in[b], 16)
                if has(-1, 0, NT):
                    b = it.par(-1)
                    if has(-3, 0, NT):
                        sp.wait_ge(y_out[b], 16 * it.half(-1))
                    sp.dma_start(xt[b][:, :], io["x"][it.rows(-1), :]).then_inc(x_in[b], 16)
                    sp.wait_ge(summed, it.at(0))
                    sp.dma_start(t["x1"][it.rows(-1), :], xt[b][:, :]).then_inc(y_out[b], 16)
            steps(sp, step, None)
            for i in range(2):
                sp.wait_ge(y_out[i], 16 * NT // 2)

        @block.gpsimd
        def _(pool):
            pool.memset(negd[:, :], -DIAG).then_inc(consts, 1)
            pool.memset(diag[:, :], DIAG).then_inc(consts, 1)

            def step(it, has):
                if not has(2, 0, NT):
                    return
                b, slot, cols = it.par(2), it.at(2) % 4, it.rows(2)
                if has(-2, 0, NT):
                    pool.wait_ge(w_ready, it.at(-1))
                pool.dma_start(adjn[:, slot, :], io["adj"][cols, :]).then_inc(adj_in[b], 16)
                pool.wait_ge(adj_in[b], 16 * (it.half(2) + 1))
                if not has(2, 0, ET):
                    pool.tensor_tensor(adjn[:, slot, cols], adjn[:, slot, cols], t["offdiag"][:, :],
                                       ALU.mult).then_inc(adjn_ready, 1)
                    return
                pool.tensor_tensor(adjn[:, slot, cols], adjn[:, slot, cols], t["offdiag"][:, :],
                                   ALU.mult).then_inc(mask_step, 1)
                pool.wait_ge(rel_in[b], 32 * (it.half(2) + 1))
                pool.tensor_tensor(rel[b][:, 0, :], rel[b][:, 0, :], rel[b][:, 1, :], ALU.add).then_inc(mask_step, 1)
                pool.wait_ge(mask_step, 3 * it.at(2) + 2)
                pool.tensor_tensor(rel[b][:, 0, :], rel[b][:, 0, :], adjn[:, it.at(6) % 4, 0:NE], ALU.mult).then_inc(mask_step, 1)
                pool.wait_ge(unrelated, it.at(3))
                pool.tensor_tensor(adjn[:, it.at(10) % 4, 0:NE], adjn[:, it.at(10) % 4, 0:NE], rel[b][:, 1, :],
                                   ALU.mult).then_inc(adjn_ready, 1)
            steps(pool, step, None)

        @block.tensor
        def _(pe):
            pe.wait_ge(k_in, 64)

            def turn(it, m):
                n = HA * it.at(-1) + m
                if m == 0:
                    pe.wait_ge(w_ready, it.at(0))
                if not (it.n == 1 and m == 0):
                    pe.wait_ge(turned_out, n)
                for b in range(2):
                    last = pe.transpose(ps[:, 6, b * P:(b + 1) * P],
                                        W[it.par(-1)][:, (2 * m + b) * P:(2 * m + b + 1) * P], t["ident"][:, :])
                last.then_inc(turned, 1)

            def aggregate(it, m, has):
                if m == 0 and has(-2, 0, NT):
                    pe.wait_ge(summed, it.at(-1))
                pe.wait_ge(turned_out, HA * it.at(-1) + m + 1)
                for b in range(2):
                    last = pe.matmul(ps[:, 7, :], WT[m % 2][:, b, :], h[:, 2 * m + b, :],
                                     start=(m == 0 and b == 0), stop=(m == HA - 1 and b == 1))
                last.then_inc(agg, 1)

            def step(it, has):
                nxt, prev = has(1, 0, ET), has(-1, 0, NT)
                for hd in range(HA):
                    if nxt:
                        q = it.par(1)
                        if hd == 0:
                            pe.wait_ge(q_in[q], 96 * (it.half(1) + 1))
                            pe.wait_ge(low_ready, it.at(2))
                        if not (it.n == -1 and hd < 2):
                            pe.wait_ge(exped, HA * it.at(1) + hd - 1)
                        for ch in range(CH):
                            cols = slice(ch * 512, ch * 512 + 512)
                            out = ps[:, 3 * (hd % 2) + ch, :]
                            pe.matmul(out, qs[q][:, 0, hd, :], k1[:, hd, cols], start=True, stop=False)
                            pe.matmul(out, qs[q][:, 1, hd, :], k1[:, hd, cols], start=False, stop=False)
                            pe.matmul(out, qs[q][:, 2, hd, :], k2[:, hd, cols], start=False, stop=False)
                            last = pe.matmul(out, t["identb"][:, :], low[q][:, cols], start=False, stop=True)
                        last.then_inc(scores, 1)
                    if prev:
                        turn(it, hd)
                        if hd:
                            aggregate(it, hd - 1, has)
                if prev:
                    aggregate(it, HA - 1, has)
            steps(pe, step, None)

        @block.scalar
        def _(act):
            act.wait_ge(consts, 2)
            act.activation(e0[:, 2, :], negd[:, :], ACT.Exp).then_inc(consts_e, 1)
            act.activation(e1[:, 2, :], negd[:, :], ACT.Exp, bias=diag[:, 0:1]).then_inc(consts_e, 1)

            def step(it, has):
                nxt, prev, b = has(1, 0, ET), has(-1, 0, NT), it.par(1)
                if has(1, 0, NT):
                    act.wait_ge(adjn_ready, it.at(2))
                    if not it.n == -1:
                        act.wait_ge(rowsum, it.at(1))
                    if has(-1, 0, NT):
                        act.wait_ge(fac, 6 * it.at(0))
                    act.activation(junk[:, :], adjn[:, it.at(1) % 4, :], ACT.Copy,
                                   accum_out=n0[:, b:b + 1]).then_inc(rowsum, 1)
                for hd in range(HA):
                    if hd == 5 and has(2, 0, ET):
                        m = it.par(2)
                        act.wait_ge(unrelated, it.at(3))
                        if has(0, 0, ET):
                            act.wait_ge(scores, HA * it.at(1))
                        act.activation(low[m][:, :], rel[m][:, 1, :], ACT.Copy, scale=-BIG).then_inc(low_ready, 1)
                    if prev:
                        n = HA * it.at(-1) + hd
                        act.wait_ge(turned, n + 1)
                        if not (it.n == 1 and hd < 2):
                            act.wait_ge(agg, n - 1)
                        act.activation(WT[hd % 2][:, :, :],
                                       ps[:, 6, 0:2 * P].rearrange("p (b i) -> p b i", b=2),
                                       ACT.Copy).then_inc(turned_out, 1)
                    if nxt:
                        act.wait_ge(negmax, HA * it.at(1) + hd + 1)
                        if has(0, 0, ET):
                            act.wait_ge(added, HA * it.at(0) + hd + 1)
                        act.activation(ex[:, hd, :], ps[:, 3 * (hd % 2):3 * (hd % 2) + 3, :].rearrange("p c j -> p (c j)"),
                                       ACT.Exp, bias=negm[:, b, hd:hd + 1], accum_out=zs[:, b, hd:hd + 1]).then_inc(exped, 1)
                if nxt:
                    act.activation(e0[:, b, :], negm[:, b, :], ACT.Exp).then_inc(efac, 1)
                    act.activation(e1[:, b, :], negm[:, b, :], ACT.Exp, bias=diag[:, 0:1]).then_inc(efac, 1)
            steps(act, step, None)

        @block.vector
        def _(dve):
            dve.wait_ge(consts_e, 2)

            def step(it, has):
                nxt, cur, related, prev = has(1, 0, ET), has(0, 0, NT), has(0, 0, ET), has(-1, 0, NT)
                b, bn = it.par(0), it.par(1)
                w = W[b]
                if cur:
                    f = 6 * it.at(0)
                    k = b if related else 2
                    dve.wait_ge(rowsum, it.at(1))
                    if related:
                        dve.wait_ge(exped, HA * it.at(1))
                        dve.wait_ge(efac, 2 * it.at(1))
                        dve.scalar_tensor_tensor(z[:, :], e0[:, k, :], n0[:, b:b + 1], zs[:, b, :], ALU.mult,
                                                 ALU.add).then_inc(fac, 1)
                        dve.wait_ge(fac, f + 1)
                        dve.tensor_tensor(z[:, :], z[:, :], e1[:, k, :], ALU.add).then_inc(fac, 1)
                    else:
                        dve.scalar_tensor_tensor(z[:, :], e0[:, k, :], n0[:, b:b + 1], e1[:, k, :], ALU.mult,
                                                 ALU.add).then_inc(fac, 2)
                    dve.wait_ge(fac, f + 2)
                    dve.reciprocal(rz[:, :], z[:, :]).then_inc(fac, 1)
                    dve.wait_ge(fac, f + 3)
                    dve.tensor_scalar(r8[:, :], rz[:, :], 1.0 / HA, None, ALU.mult).then_inc(fac, 1)
                    dve.scalar_tensor_tensor(re[:, 0, :], rz[:, :], 1.0 / HA, e0[:, k, :], ALU.mult, ALU.mult,
                                             accum_out=cd[:, 0:1]).then_inc(fac, 1)
                    dve.scalar_tensor_tensor(re[:, 1, :], rz[:, :], 1.0 / HA, e1[:, k, :], ALU.mult, ALU.mult,
                                             accum_out=cd[:, 1:2]).then_inc(fac, 1)
                    if has(-2, 0, NT):
                        dve.wait_ge(turned, HA * it.at(-1))
                    dve.wait_ge(fac, f + 6)
                for hd in range(HA):
                    if hd == 4 and has(2, 0, ET):
                        dve.wait_ge(mask_step, 3 * it.at(3))
                        m = rel[it.par(2)]
                        dve.tensor_scalar(m[:, 1, :], m[:, 0, :], 0.0, None, ALU.is_equal).then_inc(unrelated, 1)
                    if nxt:
                        dve.wait_ge(scores, HA * it.at(1) + hd + 1)
                        if not (it.n == -1 and hd == 0):
                            dve.wait_ge(negmax, HA * it.at(1) + hd)
                        dve.tensor_scalar(junkv[:, :], ps[:, 3 * (hd % 2):3 * (hd % 2) + 3, :].rearrange("p c j -> p (c j)"),
                                          -1.0, -DIAG, ALU.mult, ALU.min,
                                          accum_out=negm[:, bn, hd:hd + 1]).then_inc(negmax, 1)
                    if related:
                        if hd == 0:
                            dve.tensor_scalar(w[:, 0:NE], ex[:, 0, :], r8[:, 0:1], None, ALU.mult).then_inc(added, 1)
                        else:
                            dve.wait_ge(added, HA * it.at(0) + hd)
                            dve.scalar_tensor_tensor(w[:, 0:NE], ex[:, hd, :], r8[:, hd:hd + 1], w[:, 0:NE], ALU.mult,
                                                     ALU.add).then_inc(added, 1)
                if cur:
                    nbr = adjn[:, it.at(0) % 4, :]
                    if related:
                        dve.wait_ge(added, HA * it.at(1))
                        dve.scalar_tensor_tensor(w[:, 0:NE], adjn[:, it.at(0) % 4, 0:NE], cd[:, 0:1], w[:, 0:NE], ALU.mult,
                                                 ALU.add).then_inc(tail, 1)
                        dve.tensor_scalar(w[:, NE:N], adjn[:, it.at(0) % 4, NE:N], cd[:, 0:1], None, ALU.mult).then_inc(tail, 1)
                    else:
                        dve.tensor_scalar(w[:, :], nbr, cd[:, 0:1], None, ALU.mult).then_inc(tail, 2)
                    dve.wait_ge(tail, 2 * it.at(1))
                    dve.scalar_tensor_tensor(w[:, it.rows()], t["ident"][:, :], cd[:, 1:2], w[:, it.rows()], ALU.mult,
                                             ALU.add).then_inc(w_ready, 1)
                if prev:
                    p = it.par(-1)
                    dve.wait_ge(agg, HA * it.at(0))
                    dve.wait_ge(x_in[p], 16 * (it.half(-1) + 1))
                    dve.tensor_tensor(xt[p][:, :], xt[p][:, :], ps[:, 7, :], ALU.add).then_inc(summed, 1)
            steps(dve, step, None)


def stage3(nc, c, io, t, s, ps):
    sb = lambda name, shape, dt=F32: c.enter_context(nc.sbuf_tensor(name, shape, dt))
    sem = lambda name: c.enter_context(nc.semaphore(name))
    seq, adjT = t["seq"], t["adjT"]
    xs = sb("s3_x", [P, NT, D])
    wseq = sb("s3_w", [P, KT, D])
    a12 = sb("s3_a", [P, 2, DH])
    stats = sb("s3_stats", [P, NT, 6])
    mv = sb("s3_mv", [P, NT, 2])
    std = sb("s3_std", [P, NT])
    rstd = sb("s3_rstd", [P, NT])
    nmr = sb("s3_nmr", [P, NT])
    hb = [sb(f"s3_h{i}", [P, D]) for i in range(2)]
    hT = [sb(f"s3_hT{i}", [P, KT, P]) for i in range(2)]
    adjb = [sb(f"s3_adj{i}", [P, N], BF16) for i in range(2)]
    prod = [sb(f"s3_prod{i}", [P, 2, D]) for i in range(2)]
    sc = sb("s3_sc", [P, 2, HB, NT])
    top = sb("s3_top", [P, HB])
    topa = sb("s3_topa", [P, HB])
    d = sb("s3_d", [P, HB, NT])
    u = sb("s3_u", [P, HB, NT])
    m = sb("s3_m", [P, HB, NT])
    shift = sb("s3_shift", [P, 1])
    s1T = sb("s3_s1T", [P, 2, P])

    x_in = [sem(f"s3_x_in{i}") for i in range(4)]
    w_in, a_in = sem("s3_w_in"), sem("s3_a_in")
    adj_in = [sem(f"s3_adj_in{i}") for i in range(2)]
    consts, stat, var_ready, std_ready, norm_ready = (sem("s3_consts"), sem("s3_stat"), sem("s3_var"), sem("s3_std"),
                                                      sem("s3_norm"))
    h_ready, h_turned, hT_ready, adj_turned, adj_out_a, adj_out_v, seq_psum, seq_ready, prods, scored = (
        sem("s3_h"), sem("s3_h_turned"), sem("s3_hT"), sem("s3_adj_turned"), sem("s3_adj_out_a"), sem("s3_adj_out_v"),
        sem("s3_seq_psum"), sem("s3_seq"), sem("s3_prods"), sem("s3_scored"))
    topped, top_all, chain, expd, sT_psum, sT_ready, rows_out = (sem("s3_topped"), sem("s3_top_all"), sem("s3_chain"),
                                                                sem("s3_expd"), sem("s3_sT_psum"), sem("s3_sT"),
                                                                sem("s3_rows_out"))

    def steps(eng, step):
        for it in (0, 1):
            step(At(0, it), True)
        with eng.Fori(0, (NT - 2) // 2) as pair:
            for n in (2, 3):
                step(At(pair, n), False)

    with nc.Block() as block:
        @block.sync
        def _(sp):
            for i in range(4):
                sp.dma_start(xs[:, 4 * i:4 * i + 4, :],
                             t["x1"][512 * i:512 * i + 512, :].rearrange("(t p) k -> p t k", p=P)).then_inc(x_in[i], 16)
            sp.dma_start(wseq[:, :, :], io["L1_gnn_W_seq"].rearrange("(t p) n -> p t n", p=P)).then_inc(w_in, 16)
            for i, a in enumerate((io["L1_gnn_a1"], io["L1_gnn_a2"])):
                sp.dma_start(a12[:, i, :], a.rearrange("(o d) -> o d", o=1).to_broadcast([P, DH])).then_inc(a_in, 16)
            sp.wait_ge(sT_ready, 2)
            for g in range(2):
                sp.dma_start(t["s1_rows"].rearrange("h (t i) -> (h t) i", i=P)[g * P:(g + 1) * P, :],
                             s1T[:, g, :]).then_inc(rows_out, 16)
            sp.wait_ge(rows_out, 32)

        @block.gpsimd
        def _(pool):
            pool.memset(shift[:, :], SHIFT).then_inc(consts, 1)
            for i in range(2):
                pool.dma_start(adjb[i][:, :], io["adj"][i * P:(i + 1) * P, :]).then_inc(adj_in[i], 16)
            pool.wait_ge(a_in, 32)

            def step(it, first):
                b = it.par()
                pool.wait_ge(seq_ready, it.at(1))
                if not first:
                    pool.wait_ge(scored, 2 * it.at(-1))
                for i in range(2):
                    pool.tensor_tensor(prod[b][:, i, :].rearrange("p (h d) -> p h d", h=HB),
                                       seq[:, it.at(), :].rearrange("p (h d) -> p h d", h=HB),
                                       a12[:, i, None, :].to_broadcast([P, HB, DH]), ALU.mult).then_inc(prods, 1)

            def load_adj(it):
                pool.wait_ge(adj_turned, 2 * it.at(-1))
                pool.dma_start(adjb[it.par()][:, :], io["adj"][it.rows(), :]).then_inc(adj_in[it.par()], 16)
            for it in (0, 1):
                load_adj(At(0, it + 2))
                step(At(0, it), True)
            with pool.Fori(0, (NT - 4) // 2) as pair:
                for n in (2, 3):
                    load_adj(At(pair, n + 2))
                    step(At(pair, n), False)
            for it in (NT - 2, NT - 1):
                step(At(0, it), False)
            pool.wait_ge(topped, 1)
            pool.partition_all_reduce(topa[:, :], top[:, :], P, bass.bass_isa.ReduceOp.max).then_inc(top_all, 1)

        @block.vector
        def _(dve):
            for i in range(NT):
                if i % 4 == 0:
                    dve.wait_ge(x_in[i // 4], 16)
                dve.bn_stats(stats[:, i, :], xs[:, i, :]).then_inc(stat, 1)
            dve.wait_ge(stat, NT)
            for i in range(NT):
                dve.bn_aggr(mv[:, i, :], stats[:, i, :]).then_inc(stat, 1)
            dve.wait_ge(stat, 2 * NT)
            dve.tensor_scalar(rstd[:, :], mv[:, :, 1], EPS, None, ALU.add).then_inc(var_ready, 1)
            dve.wait_ge(std_ready, 1)
            dve.reciprocal(rstd[:, :], std[:, :]).then_inc(var_ready, 1)
            dve.wait_ge(var_ready, 2)
            dve.scalar_tensor_tensor(nmr[:, :], mv[:, :, 0], -1.0, rstd[:, :], ALU.mult, ALU.mult).then_inc(norm_ready, 1)

            def step(it, first):
                b = it.par()
                dve.wait_ge(h_turned, it.at(1))
                if not first:
                    dve.wait_ge(seq_psum, it.at(-1))
                dve.tensor_copy(hT[b][:, :, :], ps[:, b, :].rearrange("p (k i) -> p k i", k=KT)).then_inc(hT_ready, 1)
                dve.wait_ge(adj_turned, 2 * it.at() + 2)
                dve.tensor_copy(adjT[:, 8:16, it.rows()],
                                ps[:, 3, :].bitcast(BF16).rearrange("p (j i) -> p j i", j=8)).then_inc(adj_out_v, 1)

            def score(it):
                for i in range(2):
                    dve.wait_ge(prods, 2 * it.at() + i + 1)
                    dve.reduce_sum(sc[:, i, :, it.at()], prod[it.par()][:, i, :].rearrange("p (h d) -> p h d", h=HB),
                                   AX.X).then_inc(scored, 1)
            step(At(0, 0), True)
            step(At(0, 1), True)
            with dve.Fori(0, (NT - 2) // 2) as pair:
                for n in (2, 3):
                    step(At(pair, n), False)
                    score(At(pair, n - 2))
            score(At(0, NT - 2))
            score(At(0, NT - 1))

            steps_done = [0]

            def link(ins):
                steps_done[0] += 1
                ins.then_inc(chain, 1)
                dve.wait_ge(chain, steps_done[0])
            dve.wait_ge(scored, 2 * NT)
            s1, s2 = sc[:, 0, :, :], sc[:, 1, :, :]
            dve.reduce_max(top[:, :], s2, AX.X).then_inc(topped, 1)
            dve.tensor_scalar(t["ns2"][:, :, :], s2, -1.0, None, ALU.mult)\
                .then_inc(t["lasting"], 1)
            for g in range(2):
                dve.wait_ge(sT_psum, g + 1)
                dve.tensor_copy(s1T[:, g, :], ps[:, 6, g * P:(g + 1) * P]).then_inc(sT_ready, 1)
            dve.wait_ge(top_all, 1)
            tops = topa[:, :, None].to_broadcast([P, HB, NT])
            link(dve.tensor_tensor(d[:, :, :], s2, tops, ALU.subtract))
            link(dve.tensor_tensor(u[:, :, :], s1, tops, ALU.add))
            link(dve.scalar_tensor_tensor(m[:, :, :], u[:, :, :], SLOPE, u[:, :, :], ALU.mult, ALU.max))
            link(dve.scalar_tensor_tensor(t["wb"][:, :, :], u[:, :, :], SLOPE, m[:, :, :], ALU.mult, ALU.subtract))
            link(dve.tensor_tensor(t["wa"][:, :, :], u[:, :, :], m[:, :, :], ALU.subtract))

        @block.scalar
        def _(act):
            act.wait_ge(var_ready, 1)
            act.activation(std[:, :], rstd[:, :], ACT.Sqrt).then_inc(std_ready, 1)
            act.wait_ge(norm_ready, 1)

            def relu(it, first):
                if not first:
                    act.wait_ge(h_turned, it.at(-1))
                act.activation(hb[it.par()][:, :], xs[:, it.at(), :], ACT.Relu, bias=nmr[:, bass.ds(it.at(), 1)],
                               scale=rstd[:, bass.ds(it.at(), 1)]).then_inc(h_ready, 1)

            def step(it):
                act.wait_ge(adj_turned, 2 * it.at() + 1)
                act.activation(adjT[:, 0:8, it.rows()], ps[:, 2, :].bitcast(BF16).rearrange("p (j i) -> p j i", j=8),
                               ACT.Copy).then_inc(adj_out_a, 1)
                act.wait_ge(seq_psum, it.at(1))
                act.activation(seq[:, it.at(), :], ps[:, 4 + it.par(), :], ACT.Copy).then_inc(seq_ready, 1)
            relu(At(0, 0), True)
            relu(At(0, 1), True)
            with act.Fori(0, (NT - 2) // 2) as pair:
                for n in (0, 1):
                    step(At(pair, n))
                    relu(At(pair, n + 2), False)
            step(At(0, NT - 2))
            step(At(0, NT - 1))
            act.wait_ge(consts, 1)
            act.wait_ge(chain, 1)
            act.activation(t["ea"][:, :, :], d[:, :, :], ACT.Exp, bias=shift[:, 0:1]).then_inc(expd, 1)
            act.activation(t["eb"][:, :, :], d[:, :, :], ACT.Exp, bias=shift[:, 0:1], scale=SLOPE).then_inc(expd, 1)
            act.wait_ge(chain, 5)
            for w in ("wa", "wb"):
                act.activation(t[w][:, :, :], t[w][:, :, :], ACT.Exp).then_inc(expd, 1)

        @block.tensor
        def _(pe):
            pe.wait_ge(w_in, 16)

            def turn(it, first):
                b = it.par()
                pe.wait_ge(h_ready, it.at(1))
                if not first:
                    pe.wait_ge(hT_ready, it.at(-1))
                for k in range(KT):
                    last = pe.transpose(ps[:, b, k * P:(k + 1) * P], hb[b][:, k * P:(k + 1) * P], t["ident"][:, :])
                last.then_inc(h_turned, 1)

            def step(it, first, last_tile=False):
                b = it.par()
                pe.wait_ge(adj_in[b], 16 * (it.half() + 1))
                for half, out in ((0, adj_out_a), (1, adj_out_v)):
                    if not (first and b == 0):
                        pe.wait_ge(out, it.at())
                    for j in range(8):
                        last = pe.transpose(ps[:, 2 + half, :].bitcast(BF16)[:, j * P:(j + 1) * P],
                                            adjb[b][:, (8 * half + j) * P:(8 * half + j + 1) * P], t["identb"][:, :])
                    last.then_inc(adj_turned, 1)
                if not last_tile:
                    turn(At(it.pair, it.n + 1), first and b == 0)
                pe.wait_ge(hT_ready, it.at(1))
                if not first:
                    pe.wait_ge(seq_ready, it.at(-1))
                for k in range(KT):
                    last = pe.matmul(ps[:, 4 + b, :], hT[b][:, k, :], wseq[:, k, :], start=(k == 0), stop=(k == KT - 1))
                last.then_inc(seq_psum, 1)
            turn(At(0, 0), True)
            step(At(0, 0), True)
            step(At(0, 1), True)
            with pe.Fori(0, (NT - 4) // 2) as pair:
                for n in (2, 3):
                    step(At(pair, n), False)
            step(At(0, NT - 2), False)
            step(At(0, NT - 1), False, last_tile=True)
            pe.wait_ge(scored, 2 * NT)
            for g in range(2):
                if g:
                    pe.wait_ge(sT_ready, g)
                pe.transpose(ps[:, 6, g * P:(g + 1) * P],
                             sc[:, 0, 8 * g:8 * g + 8, :].rearrange("p h t -> p (h t)"), t["ident"][:, :]).then_inc(sT_psum, 1)


RING = 8
HALF = N // 2
HT = HALF // P
VECTOR_ONLY = (5, 10, 15)


def stage4(nc, c, io, t, s, ps, g):
    sb = lambda name, shape, dt=F32: c.enter_context(nc.sbuf_tensor(f"s4_{g}_{name}", shape, dt))
    sem = lambda name: c.enter_context(nc.semaphore(f"s4_{g}_{name}"))
    seq, adjT = t["seq"], t["adjT"]
    V = sb("V", [P, NT, 3, 2, GH, DZ], BF16)
    A2 = sb("A2", [P, NT, GH, DZ])
    masks = sb("masks", [P, RING, HALF], BF16)
    s1b = [sb(f"s1b{i}", [P, HALF]) for i in range(2)]
    tmp = [sb(f"tmp{i}", [P, 2, GH, DZ]) for i in range(2)]
    sums = [sb(f"sums{i}", [P, HT, 2, DZ]) for i in range(2)]
    hid = [sb(f"hid{i}", [P, HT, DZ]) for i in range(2)]
    bs2 = [sb(f"bs2{i}", [P, NT]) for i in range(2)]
    bs2_ready = sem("bs2_ready")
    hs = slice(g * GH, (g + 1) * GH)
    fs = slice(g * GH * DH, (g + 1) * GH * DH)

    value, hi_out, rest, mid_out, split = sem("value"), sem("hi"), sem("rest"), sem("mid"), sem("split")
    a2_psum, a2_ready = sem("a2_psum"), sem("a2")
    s1_in = [sem(f"s1_in{i}") for i in range(2)]
    hid_out = [sem(f"hid_out{i}") for i in range(2)]
    signs, mask_ready, mask_used, summed, comb, hid_ready = (
        sem("signs"), sem("mask"), sem("mask_used"), sem("summed"), sem("comb"), sem("hid"))
    NS = NT - len(VECTOR_ONLY)

    with nc.Block() as block:
        @block.sync
        def _(sp):
            def load(hh, half):
                sp.dma_start(s1b[half][:, :],
                             t["s1_rows"][bass.ds(hh + g * GH, 1), half * HALF:(half + 1) * HALF].to_broadcast([P, HALF])
                             ).then_inc(s1_in[half], 16)

            def store(hh, half):
                sp.wait_ge(hid_ready, 2 * hh + half + 1)
                sp.dma_start(t["hidden"][half * HALF:(half + 1) * HALF, hh + g * GH, :].rearrange("(t p) d -> p t d", p=P),
                             hid[half][:, :, :]).then_inc(hid_out[half], 16)
            load(0, 0)
            load(0, 1)
            with sp.Fori(0, GH - 1) as hh:
                for half in range(2):
                    sp.wait_ge(mask_ready, 2 * NT * hh + NT * (half + 1))
                    load(hh + 1, half)
                for half in range(2):
                    store(hh, half)
            for half in range(2):
                store(GH - 1, half)
            for half in range(2):
                sp.wait_ge(hid_out[half], 16 * GH)

        @block.gpsimd
        def _(pool):
            def value_of(it, first):
                b = it.par()
                if not first:
                    pool.wait_ge(split, it.at(-1))
                for k, e in enumerate((t["ea"], t["eb"])):
                    w = e[:, hs, it.at()]
                    pool.tensor_tensor(tmp[b][:, k, :, 0:DH], seq[:, it.at(), fs].rearrange("p (h d) -> p h d", h=GH),
                                       w[:, :, None].to_broadcast([P, GH, DH]), ALU.mult).then_inc(value, 1)
                    pool.tensor_copy(tmp[b][:, k, :, DH], w).then_inc(value, 1)
            value_of(At(0, 0), True)
            value_of(At(0, 1), True)
            with pool.Fori(0, (NT - 2) // 2) as pair:
                for n in (2, 3):
                    value_of(At(pair, n), False)

            def combine_all(hh, first):
                for half in range(2):
                    n = 2 * hh + half
                    q, out, rows = sums[half], hid[half], slice(half * HT, (half + 1) * HT)
                    wa = t["wa"][:, hh + g * GH, rows].rearrange("p (t o) -> p t o", o=1).to_broadcast([P, HT, DZ])
                    wb = t["wb"][:, hh + g * GH, rows].rearrange("p (t o) -> p t o", o=1).to_broadcast([P, HT, DZ])
                    pool.wait_ge(summed, n + 1)
                    if not first:
                        pool.wait_ge(hid_out[half], 16 * hh)
                    pool.tensor_tensor(out[:, :, :], A2[:, rows, hh, :], q[:, :, 1, :], ALU.subtract).then_inc(comb, 1)
                    pool.tensor_tensor(q[:, :, 0, :], q[:, :, 0, :], wa, ALU.mult).then_inc(comb, 1)
                    pool.wait_ge(comb, 3 * n + 2)
                    pool.tensor_tensor(out[:, :, :], out[:, :, :], wb, ALU.mult).then_inc(comb, 1)
                    pool.wait_ge(comb, 3 * n + 3)
                    pool.tensor_tensor(out[:, :, :], out[:, :, :], q[:, :, 0, :], ALU.add).then_inc(hid_ready, 1)
            combine_all(0, True)
            with pool.Fori(1, GH) as hh:
                combine_all(hh, False)

        @block.scalar
        def _(act):
            def parts(it):
                b = it.par()
                act.wait_ge(value, 4 * it.at(1))
                act.activation(V[:, it.at(), 0, :, :, :], tmp[b][:, :, :, :], ACT.Copy).then_inc(hi_out, 1)
                act.wait_ge(rest, it.at(1))
                act.activation(V[:, it.at(), 1, :, :, :], tmp[b][:, :, :, :], ACT.Copy).then_inc(mid_out, 1)
            with act.Fori(0, NT // 2) as pair:
                for n in (0, 1):
                    parts(At(pair, n))

            def head(hh, first):
                for half in range(2):
                    act.wait_ge(s1_in[half], 16 * hh + 16)
                    act.wait_ge(bs2_ready, 2 * hh + half + 1)
                    for j in range(NT):
                        if j in VECTOR_ONLY:
                            continue
                        n = 2 * NT * hh + NT * half + j
                        if not (first and NT * half + j < RING):
                            act.wait_ge(mask_used, n - RING + 1)
                        act.activation(masks[:, j % RING, :], s1b[half][:, :], ACT.Relu,
                                       bias=bs2[half][:, j:j + 1], scale=BIG).then_inc(signs, 1)
            head(0, True)
            with act.Fori(1, GH) as hh:
                head(hh, False)

        @block.vector
        def _(dve):
            def parts(it):
                b = it.par()
                dve.wait_ge(hi_out, it.at(1))
                dve.tensor_tensor(tmp[b][:, :, :, :].rearrange("p k h d -> p (k h d)"),
                                  tmp[b][:, :, :, :].rearrange("p k h d -> p (k h d)"),
                                  V[:, it.at(), 0, :, :, :].rearrange("p k h d -> p (k h d)"), ALU.subtract).then_inc(rest, 1)
                dve.wait_ge(mid_out, it.at(1))
                dve.tensor_tensor(V[:, it.at(), 2, :, :, :].rearrange("p k h d -> p (k h d)"),
                                  tmp[b][:, :, :, :].rearrange("p k h d -> p (k h d)"),
                                  V[:, it.at(), 1, :, :, :].rearrange("p k h d -> p (k h d)"), ALU.subtract).then_inc(split, 1)
            with dve.Fori(0, NT // 2) as pair:
                for n in (0, 1):
                    parts(At(pair, n))

            with dve.Fori(0, NT // 2) as pair:
                for n in (0, 1):
                    it = At(pair, n)
                    dve.wait_ge(a2_psum, it.at(1))
                    dve.reduce_sum(A2[:, it.at(), :, :].rearrange("p (q h) d -> p q (h d)", q=2),
                                   ps[:, 2 * n:2 * n + 2, 0:3 * GH * DZ // 2].rearrange("p q (s c) -> p q c s", s=3),
                                   AX.X).then_inc(a2_ready, 1)

            dve.tensor_scalar(bs2[0][:, :], t["ns2"][:, g * GH, :], -BIG, None, ALU.mult).then_inc(bs2_ready, 1)

            def head(hh, first):
                for half in range(2):
                    dve.wait_ge(s1_in[half], 16 * hh + 16)
                    for j in range(NT):
                        if j == 3:
                            if not (first and half == 0):
                                dve.wait_ge(signs, 2 * NS * hh + NS * half)
                            at = hh + g * GH if half == 0 else (hh + 1) % GH + g * GH
                            dve.tensor_scalar(bs2[1 - half][:, :], t["ns2"][:, at, :], -BIG, None,
                                              ALU.mult).then_inc(bs2_ready, 1)
                        n = 2 * NT * hh + NT * half + j
                        out, near = masks[:, j % RING, :], adjT[:, j, half * HALF:(half + 1) * HALF]
                        if j in VECTOR_ONLY:
                            if not (first and NT * half + j < RING):
                                dve.wait_ge(mask_used, n - RING + 1)
                            dve.scalar_tensor_tensor(out, s1b[half][:, :], t["ns2"][:, hh + g * GH, j:j + 1], near,
                                                     ALU.is_gt, ALU.mult).then_inc(mask_ready, 1)
                        else:
                            before = sum(x not in VECTOR_ONLY for x in range(j))
                            dve.wait_ge(signs, 2 * NS * hh + NS * half + before + 1)
                            dve.tensor_tensor(out, out, near, ALU.min).then_inc(mask_ready, 1)
                    k = 2 * hh + half
                    dve.wait_ge(mask_used, NT * (k + 1))
                    if not first:
                        dve.wait_ge(hid_ready, k - 1)
                    dve.reduce_sum(sums[half][:, :, :, :].rearrange("p t k d -> p t (k d)"),
                                   ps[:, 4 * half:4 * half + 4, :].rearrange("p b (u c) -> p (b u) c", u=2)[:, :, 0:6 * DZ]
                                   .rearrange("p t (s c) -> p t c s", s=3), AX.X).then_inc(summed, 1)
            head(0, True)
            with dve.Fori(1, GH) as hh:
                head(hh, False)

        @block.tensor
        def _(pe):
            pe.wait_ge(split, NT)

            def near(it, first):
                b = it.par()
                if not first:
                    pe.wait_ge(a2_ready, it.at(-1))
                for j in range(NT):
                    for q in range(2):
                        last = pe.matmul(ps[:, 2 * b + q, 0:3 * GH * DZ // 2].rearrange("p (s c) -> p s c", s=3),
                                         adjT[:, j, it.rows()],
                                         V[:, j, :, 1, 4 * q:4 * q + 4, :].rearrange("p s h d -> p s (h d)"),
                                         start=(j == 0), stop=(j == NT - 1))
                last.then_inc(a2_psum, 1)
            near(At(0, 0), True)
            near(At(0, 1), True)
            with pe.Fori(0, (NT - 2) // 2) as pair:
                for n in (2, 3):
                    near(At(pair, n), False)
            pe.wait_ge(a2_ready, NT)

            def head(hh, first):
                for half in range(2):
                    if not first:
                        pe.wait_ge(summed, 2 * hh + half - 1)
                    for j in range(NT):
                        pe.wait_ge(mask_ready, 2 * NT * hh + NT * half + j + 1)
                        for i in range(HT):
                            last = pe.matmul(ps[:, 4 * half + i // 2, 256 * (i % 2):256 * (i % 2) + 6 * DZ]
                                             .rearrange("p (s d) -> p s d", s=6),
                                             masks[:, j % RING, i * P:(i + 1) * P],
                                             V[:, j, :, :, hh, :].rearrange("p s k d -> p (s k) d"),
                                             start=(j == 0 and i % 2 == 0), stop=(j == NT - 1), skip_group_check=True)
                        last.then_inc(mask_used, 1)
            head(0, True)
            with pe.Fori(1, GH) as hh:
                head(hh, False)


def stage5(nc, c, io, out, t, s, ps):
    sb = lambda name, shape, dt=F32: c.enter_context(nc.sbuf_tensor(name, shape, dt))
    sem = lambda name: c.enter_context(nc.semaphore(name))
    wout = sb("s5_w", [P, KT, D])
    bout = sb("s5_b", [P, D])
    hid = [sb(f"s5_hid{i}", [P, HB, DZ]) for i in range(2)]
    x1 = [sb(f"s5_x{i}", [P, D]) for i in range(2)]
    rz = [sb(f"s5_rz{i}", [P, HB]) for i in range(2)]
    hn = [sb(f"s5_hn{i}", [P, D]) for i in range(2)]
    hT = [sb(f"s5_hT{i}", [P, KT, P]) for i in range(2)]
    v = [sb(f"s5_v{i}", [P, D]) for i in range(2)]
    e = [sb(f"s5_e{i}", [P, D]) for i in range(2)]
    w_in = sem("s5_w_in")
    hid_in = [sem(f"s5_hid_in{i}") for i in range(2)]
    x_in = [sem(f"s5_x_in{i}") for i in range(2)]
    y_out = [sem(f"s5_y_out{i}") for i in range(2)]
    inv, normed, turned, turned_out, proj, biased, low, expd, added, done = (
        sem("s5_inv"), sem("s5_normed"), sem("s5_turned"), sem("s5_turned_out"), sem("s5_proj"), sem("s5_biased"),
        sem("s5_low"), sem("s5_expd"), sem("s5_added"), sem("s5_done"))

    def steps(eng, step):
        for it in (0, 1):
            step(At(0, it), True)
        with eng.Fori(0, (NT - 2) // 2) as pair:
            for n in (2, 3):
                step(At(pair, n), False)

    with nc.Block() as block:
        @block.sync
        def _(sp):
            sp.dma_start(wout[:, :, :], io["L1_gnn_W_out"].rearrange("(t p) n -> p t n", p=P)).then_inc(w_in, 16)
            sp.dma_start(bout[:, :], io["L1_gnn_b_out"].rearrange("(o d) -> o d", o=1).to_broadcast([P, D])).then_inc(w_in, 16)

            def step(it, first):
                b = it.par()
                if not first:
                    sp.wait_ge(normed, it.at(-1))
                sp.dma_start(hid[b][:, :, :], t["hidden"][it.rows(), :, :]).then_inc(hid_in[b], 16)
                if not first:
                    sp.wait_ge(y_out[b], 16 * it.half())
                sp.dma_start(x1[b][:, :], t["x1"][it.rows(), :]).then_inc(x_in[b], 16)
            steps(sp, step)

        @block.vector
        def _(dve):
            def norm(it, first):
                b = it.par()
                dve.wait_ge(hid_in[b], 16 * (it.half() + 1))
                dve.reciprocal(rz[b][:, :], hid[b][:, :, DH]).then_inc(inv, 1)
                dve.wait_ge(inv, it.at(1))
                if not first:
                    dve.wait_ge(turned, it.at(-1))
                dve.tensor_tensor(hn[b][:, :].rearrange("p (h d) -> p h d", h=HB), hid[b][:, :, 0:DH],
                                  rz[b][:, :, None].to_broadcast([P, HB, DH]), ALU.mult).then_inc(normed, 1)

            def finish(it, first):
                b = it.par()
                dve.wait_ge(proj, it.at(1))
                dve.wait_ge(w_in, 32)
                dve.tensor_tensor(v[b][:, :], ps[:, 2 + b, :], bout[:, :], ALU.add).then_inc(biased, 1)
                dve.wait_ge(biased, it.at(1))
                if not first:
                    dve.wait_ge(added, it.at(-1))
                dve.tensor_scalar(e[b][:, :], v[b][:, :], 0.0, None, ALU.min).then_inc(low, 1)
                dve.wait_ge(x_in[b], 16 * (it.half() + 1))
                dve.wait_ge(expd, it.at(1))
                dve.scalar_tensor_tensor(e[b][:, :], e[b][:, :], -1.0, x1[b][:, :], ALU.add, ALU.add).then_inc(added, 1)
                dve.wait_ge(added, it.at(1))
                dve.scalar_tensor_tensor(x1[b][:, :], v[b][:, :], 0.0, e[b][:, :], ALU.max, ALU.add).then_inc(done, 1)
            norm(At(0, 0), True)
            norm(At(0, 1), True)
            finish(At(0, 0), True)
            norm(At(0, 2), False)
            finish(At(0, 1), True)
            norm(At(0, 3), False)
            with dve.Fori(0, (NT - 4) // 2) as pair:
                for n in (2, 3):
                    finish(At(pair, n), False)
                    norm(At(pair, n + 2), False)
            for it in (NT - 2, NT - 1):
                finish(At(0, it), False)

        @block.tensor
        def _(pe):
            pe.wait_ge(w_in, 32)

            def turn(it, first):
                b = it.par()
                pe.wait_ge(normed, it.at(1))
                if not first:
                    pe.wait_ge(turned_out, it.at(-1))
                for k in range(KT):
                    last = pe.transpose(ps[:, b, k * P:(k + 1) * P], hn[b][:, k * P:(k + 1) * P], t["ident"][:, :])
                last.then_inc(turned, 1)

            def project(it, first):
                b = it.par()
                pe.wait_ge(turned_out, it.at(1))
                if not first:
                    pe.wait_ge(biased, it.at(-1))
                for k in range(KT):
                    last = pe.matmul(ps[:, 2 + b, :], hT[b][:, k, :], wout[:, k, :], start=(k == 0), stop=(k == KT - 1))
                last.then_inc(proj, 1)
            turn(At(0, 0), True)
            turn(At(0, 1), True)
            project(At(0, 0), True)
            turn(At(0, 2), False)
            project(At(0, 1), True)
            turn(At(0, 3), False)
            with pe.Fori(0, (NT - 4) // 2) as pair:
                for n in (2, 3):
                    project(At(pair, n), False)
                    turn(At(pair, n + 2), False)
            for it in (NT - 2, NT - 1):
                project(At(0, it), False)

        @block.scalar
        def _(act):
            def copy(it, first):
                b = it.par()
                act.wait_ge(turned, it.at(1))
                if not first:
                    act.wait_ge(proj, it.at(-1))
                act.activation(hT[b][:, :, :], ps[:, b, :].rearrange("p (k i) -> p k i", k=KT), ACT.Copy).then_inc(turned_out, 1)

            def exp(it):
                b = it.par()
                act.wait_ge(low, it.at(1))
                act.activation(e[b][:, :], e[b][:, :], ACT.Exp).then_inc(expd, 1)
            copy(At(0, 0), True)
            copy(At(0, 1), True)
            with act.Fori(0, (NT - 2) // 2) as pair:
                for n in (0, 1):
                    exp(At(pair, n))
                    copy(At(pair, n + 2), False)
            for it in (NT - 2, NT - 1):
                exp(At(0, it))

        @block.gpsimd
        def _(pool):
            with pool.Fori(0, NT // 2) as pair:
                for n in (0, 1):
                    it = At(pair, n)
                    pool.wait_ge(done, it.at(1))
                    pool.dma_start(out[it.rows(), :], x1[n][:, :]).then_inc(y_out[n], 16)
            for i in range(2):
                pool.wait_ge(y_out[i], 16 * NT // 2)


INS = ["x", "adj", "L0_gnn_rel_pair_index", "L0_gnn_Wq", "L0_gnn_bq", "L0_gnn_Wk", "L0_gnn_bk", "L1_gnn_W_seq",
       "L1_gnn_a1", "L1_gnn_a2", "L1_gnn_W_out", "L1_gnn_b_out"]


def build(nc, io, out, kind="Internal", upto=5):
    dram = lambda name, shape, dt=F32: nc.dram_tensor(name, shape, dt, kind=kind).ap()
    t = {
        "q_parts": dram("q_parts", [3, D, NE], BF16), "k_parts": dram("k_parts", [3, D, NE], BF16),
        "rel_table": [dram(f"rel_table{i}", [NE, NE], BF16) for i in range(2)], "x1": dram("x1", [N, D]),
        "s1_rows": dram("s1_rows", [HB, N]), "hidden": dram("hidden", [N, HB, DZ]),
    }
    with ExitStack() as c:
        t["ident"] = c.enter_context(nc.sbuf_tensor("ident", [P, P], F32))
        t["identb"] = c.enter_context(nc.sbuf_tensor("identb", [P, P], BF16))
        t["offdiag"] = c.enter_context(nc.sbuf_tensor("offdiag", [P, P], BF16))
        ps = c.enter_context(nc.psum_tensor("psum", [P, 8, 512], F32))
        s = {n: c.enter_context(nc.semaphore(n)) for n in ("zeroed", "const", "lasting")}
        make_constants(nc, t, s)
        with ExitStack() as first:
            t["h"] = first.enter_context(nc.sbuf_tensor("h", [P, NT, D], F32))
            with ExitStack() as part:
                stage1(nc, part, io, t, s, ps)
            if upto >= 2:
                with ExitStack() as part:
                    stage2(nc, part, io, t, s, ps)
        if upto >= 3:
            with ExitStack() as second:
                sb = lambda name, shape, dt=F32: second.enter_context(nc.sbuf_tensor(name, shape, dt))
                t["seq"] = sb("seq", [P, NT, D])
                t["adjT"] = sb("adjT", [P, NT, N], BF16)
                for name in ("ns2", "ea", "eb", "wa", "wb"):
                    t[name] = sb(name, [P, HB, NT])
                t["lasting"] = s["lasting"]
                with ExitStack() as part:
                    stage3(nc, part, io, t, s, ps)
                for g in range(NG if upto >= 4 else 0):
                    with ExitStack() as part:
                        stage4(nc, part, io, t, s, ps, g)
        if upto >= 5:
            with ExitStack() as part:
                stage5(nc, part, io, out, t, s, ps)


def kernel(**inputs):
    import numpy as np
    import concourse.bacc as bacc
    from concourse.bass_utils import run_bass_kernel_spmd as run

    nc = bacc.Bacc("TRN2", target_bir_lowering=False, num_devices=1)
    arrays, io = {}, {}
    for name in INS:
        a = np.ascontiguousarray(inputs[name])
        arrays[f"in_{name}"] = a
        io[name] = nc.dram_tensor(f"in_{name}", a.shape, mybir.dt.from_np(a.dtype), kind="ExternalInput").ap()
    out = nc.dram_tensor("out", [N, D], F32, kind="ExternalOutput").ap()
    build(nc, io, out)
    return run(nc, [arrays], core_ids=[0]).results[0]["out"]
```

```python
from contextlib import ExitStack

import concourse.bass as bass
from concourse import mybir

F32 = mybir.dt.float32
BF16 = mybir.dt.bfloat16
I32 = mybir.dt.int32
U32 = mybir.dt.uint32
ALU = mybir.AluOpType
ACT = mybir.ActivationFunctionType
AX = mybir.AxisListType

P = 128
N = 2048
D = 512
NT = N // P
KT = D // P
EPS = 1e-5

NREL = 1500
ET = -(-NREL // P)
NE = ET * P
E = 10000
EP = 125
EC = E // EP
HA = 8
DK = D // HA
CH = NE // 512
BIG = float(2.0 ** 100)
DIAG = 1e-7

HB = 16
DH = D // HB
DZ = DH + 1
GH = 2
NG = HB // GH
SLOPE = 0.2
SHIFT = 40.0


def make_constants(nc, t, s):
    with nc.Block() as block:
        @block.gpsimd
        def _(pool):
            pool.memset(t["ident"][:, :], 0.0).then_inc(s["zeroed"], 1)
            pool.memset(t["identb"][:, :], 0.0).then_inc(s["zeroed"], 1)
            pool.memset(t["offdiag"][:, :], 1.0).then_inc(s["zeroed"], 1)
            pool.wait_ge(s["zeroed"], 3)
            for m, fill in ((t["ident"], 1.0), (t["identb"], 1.0), (t["offdiag"], 0.0)):
                pool.affine_select(out=m[:, :], in_=m[:, :], compare_op=ALU.not_equal, fill=fill, base=0,
                                   pattern=[[-1, P]], channel_multiplier=1).then_inc(s["const"], 1)


def stage1(nc, c, io, t, s, ps):
    sb = lambda name, shape, dt=F32: c.enter_context(nc.sbuf_tensor(name, shape, dt))
    sem = lambda name: c.enter_context(nc.semaphore(name))
    xs = sb("s1_x", [P, NT, D])
    wnat = [sb(f"s1_w{i}", [P, KT, D]) for i in range(2)]
    wT = [sb(f"s1_wT{i}", [P, KT, D]) for i in range(2)]
    bias = sb("s1_bias", [P, 2, KT])
    bias8 = sb("s1_bias8", [P, KT])
    hT = sb("s1_hT", [P, KT, NE])
    stats = sb("s1_stats", [P, NT, 6])
    mv = sb("s1_mv", [P, NT, 2])
    std = sb("s1_std", [P, NT])
    rstd = sb("s1_rstd", [P, NT])
    nmr = sb("s1_nmr", [P, NT])
    full = sb("s1_full", [P, 2, 512])
    parts = sb("s1_parts", [P, 2, 3, 512], BF16)
    zero = sb("s1_zero", [P, NE], BF16)
    ones = sb("s1_ones", [P, 1], BF16)
    rel = sb("s1_rel", [P, EC, 2], I32)
    flat = sb("s1_flat", [P, EC], U32)
    h = t["h"]

    x_in = [sem(f"s1_x_in{i}") for i in range(4)]
    w_in, bias_in, rel_in = sem("s1_w_in"), sem("s1_bias_in"), sem("s1_rel_in")
    zero_set, table_zero, flat_ready = sem("s1_zero_set"), sem("s1_table_zero"), sem("s1_flat")
    related = [sem(f"s1_related{i}") for i in range(2)]
    stat, var_ready, std_ready, norm_ready, h_ready = (sem("s1_stat"), sem("s1_var"), sem("s1_std"), sem("s1_norm"),
                                                       sem("s1_h"))
    wT_psum, wT_ready, hT_psum, hT_ready = sem("s1_wTp"), sem("s1_wT"), sem("s1_hTp"), sem("s1_hT")
    bias_ready, proj, full_ready, split_step, parts_ready = (sem("s1_b8"), sem("s1_proj"), sem("s1_full"),
                                                             sem("s1_split"), sem("s1_parts"))
    parts_out = [sem(f"s1_parts_out{i}") for i in range(2)]
    groups = [(w, dt, ch) for w in (1, 0) for dt in range(KT) for ch in range(CH)]
    G = len(groups)

    with nc.Block() as block:
        @block.sync
        def _(sp):
            for i, w in enumerate((io["L0_gnn_Wq"], io["L0_gnn_Wk"])):
                sp.dma_start(wnat[i][:, :, :], w.rearrange("(t p) k -> p t k", p=P)).then_inc(w_in, 16)
            for i in range(4):
                sp.dma_start(xs[:, 4 * i:4 * i + 4, :],
                             io["x"][512 * i:512 * i + 512, :].rearrange("(t p) k -> p t k", p=P)).then_inc(x_in[i], 16)
            for g, (w, dt, ch) in enumerate(groups):
                sp.wait_ge(parts_ready, g + 1)
                dst = t["q_parts" if w == 0 else "k_parts"]
                sp.dma_start(dst[:, dt * P:(dt + 1) * P, ch * 512:(ch + 1) * 512].rearrange("s p i -> p s i"),
                             parts[:, g % 2, :, :]).then_inc(parts_out[g % 2], 16)
            for i in range(2):
                sp.wait_ge(parts_out[i], 16 * G // 2)

        @block.gpsimd
        def _(pool):
            pool.memset(zero[:, :], 0.0).then_inc(zero_set, 1)
            pool.memset(ones[:, :], 1.0).then_inc(zero_set, 1)
            pool.dma_start(rel[0:EP, :, :], io["L0_gnn_rel_pair_index"].rearrange("(p c) s -> p c s", p=EP)).then_inc(rel_in, 16)
            pool.wait_ge(zero_set, 2)
            for i in range(2):
                pool.dma_start(t["rel_table"][i].rearrange("(t p) j -> p t j", p=P),
                               zero[:, None, :].to_broadcast([P, ET, NE])).then_inc(table_zero, 16)
            for i, b in enumerate((io["L0_gnn_bq"], io["L0_gnn_bk"])):
                pool.dma_start(bias[:, i, :], b.rearrange("(t p) -> p t", p=P),
                               allow_slow_non_contiguous=True).then_inc(bias_in, 16)
            pool.wait_ge(table_zero, 32)
            pool.wait_ge(flat_ready, 1)
            for e in range(EC):
                if e >= 2:
                    pool.wait_ge(related[e % 2], 16 * (e // 2))
                pool.indirect_dma_start(t["rel_table"][e % 2].rearrange("i (j o) -> (i j) o", o=1),
                                        bass.IndirectOffsetOnAxis(ap=flat[0:EP, e:e + 1], axis=0),
                                        ones[0:EP, 0:1], None).then_inc(related[e % 2], 16)
            for i in range(2):
                pool.wait_ge(related[i], 16 * EC // 2)

        @block.vector
        def _(dve):
            dve.wait_ge(rel_in, 16)
            dve.scalar_tensor_tensor(flat[0:EP, :], rel[0:EP, :, 0], float(NE), rel[0:EP, :, 1], ALU.mult,
                                     ALU.add).then_inc(flat_ready, 1)
            dve.wait_ge(bias_in, 32)
            dve.tensor_scalar(bias8[:, :], bias[:, 0, :], DK ** -0.5, None, ALU.mult).then_inc(bias_ready, 1)
            for k in range(8):
                dve.wait_ge(wT_psum, k + 1)
                dve.tensor_copy(wT[k // KT][:, k % KT, :], ps[:, k, :]).then_inc(wT_ready, 1)
            for i in range(NT):
                if i % 4 == 0:
                    dve.wait_ge(x_in[i // 4], 16)
                dve.bn_stats(stats[:, i, :], xs[:, i, :]).then_inc(stat, 1)
            dve.wait_ge(stat, NT)
            for i in range(NT):
                dve.bn_aggr(mv[:, i, :], stats[:, i, :]).then_inc(stat, 1)
            dve.wait_ge(stat, 2 * NT)
            dve.tensor_scalar(rstd[:, :], mv[:, :, 1], EPS, None, ALU.add).then_inc(var_ready, 1)
            dve.wait_ge(std_ready, 1)
            dve.reciprocal(rstd[:, :], std[:, :]).then_inc(var_ready, 1)
            dve.wait_ge(var_ready, 2)
            dve.scalar_tensor_tensor(nmr[:, :], mv[:, :, 0], -1.0, rstd[:, :], ALU.mult, ALU.mult).then_inc(norm_ready, 1)
            for i in range(ET):
                dve.wait_ge(hT_psum, i + 1)
                dve.tensor_copy(hT[:, :, i * P:(i + 1) * P],
                                ps[:, i % 4, :].rearrange("p (k i) -> p k i", k=KT)).then_inc(hT_ready, 1)
            for g in range(G):
                v, q = full[:, g % 2, :], parts[:, g % 2, :, :]
                dve.wait_ge(full_ready, g + 1)
                if g >= 2:
                    dve.wait_ge(parts_out[g % 2], 16 * (g // 2))
                dve.tensor_copy(q[:, 0, :], v).then_inc(split_step, 1)
                dve.wait_ge(split_step, 3 * g + 1)
                dve.tensor_tensor(v, v, q[:, 0, :], ALU.subtract).then_inc(split_step, 1)
                dve.wait_ge(split_step, 3 * g + 2)
                dve.tensor_copy(q[:, 1, :], v).then_inc(split_step, 1)
                dve.wait_ge(split_step, 3 * g + 3)
                dve.tensor_tensor(q[:, 2, :], v, q[:, 1, :], ALU.subtract).then_inc(parts_ready, 1)

        @block.scalar
        def _(act):
            act.wait_ge(var_ready, 1)
            act.activation(std[:, :], rstd[:, :], ACT.Sqrt).then_inc(std_ready, 1)
            act.wait_ge(norm_ready, 1)
            for i in range(NT):
                act.activation(h[:, i, :], xs[:, i, :], ACT.Relu, bias=nmr[:, i:i + 1],
                               scale=rstd[:, i:i + 1]).then_inc(h_ready, 1)
            act.wait_ge(bias_ready, 1)
            for g, (w, dt, ch) in enumerate(groups):
                act.wait_ge(proj, g + 1)
                if g >= 2:
                    act.wait_ge(parts_ready, g - 1)
                b = bias8[:, dt:dt + 1] if w == 0 else bias[:, 1, dt:dt + 1]
                act.activation(full[:, g % 2, :], ps[:, 4 + g % 4, :], ACT.Identity, bias=b,
                               scale=DK ** -0.5 if w == 0 else 1.0).then_inc(full_ready, 1)

        @block.tensor
        def _(pe):
            pe.wait_ge(s["const"], 3)
            pe.wait_ge(w_in, 32)
            for k in range(8):
                for dt in range(KT):
                    last = pe.transpose(ps[:, k, dt * P:(dt + 1) * P],
                                        wnat[k // KT][:, dt, (k % KT) * P:(k % KT + 1) * P], t["ident"][:, :])
                last.then_inc(wT_psum, 1)
            for i in range(ET):
                pe.wait_ge(h_ready, i + 1)
                pe.wait_ge(wT_ready, 8)
                if i >= 4:
                    pe.wait_ge(hT_ready, i - 3)
                for k in range(KT):
                    last = pe.transpose(ps[:, i % 4, k * P:(k + 1) * P], h[:, i, k * P:(k + 1) * P], t["ident"][:, :])
                last.then_inc(hT_psum, 1)
            pe.wait_ge(hT_ready, ET)
            for g, (w, dt, ch) in enumerate(groups):
                if g >= 4:
                    pe.wait_ge(full_ready, g - 3)
                for k in range(KT):
                    last = pe.matmul(ps[:, 4 + g % 4, :], wT[w][:, k, dt * P:(dt + 1) * P],
                                     hT[:, k, ch * 512:(ch + 1) * 512], start=(k == 0), stop=(k == KT - 1))
                last.then_inc(proj, 1)



class At:

    def __init__(self, pair, n):
        self.pair, self.n = pair, n

    def at(self, off=0):
        return 2 * self.pair + (self.n + off)

    def half(self, off=0):
        return self.pair + (self.n + off) // 2

    def par(self, off=0):
        return (self.n + off) % 2

    def rows(self, off=0):
        return bass.ds(self.at(off) * P, P)


def stage2(nc, c, io, t, s, ps):
    sb = lambda name, shape, dt=F32: c.enter_context(nc.sbuf_tensor(name, shape, dt))
    sem = lambda name: c.enter_context(nc.semaphore(name))
    h = t["h"]
    k1 = sb("s2_k1", [P, HA, NE], BF16)
    k2 = sb("s2_k2", [P, HA, NE], BF16)
    qs = [sb(f"s2_q{i}", [P, 3, HA, P], BF16) for i in range(2)]
    adjn = sb("s2_adj", [P, 4, N], BF16)
    rel = [sb(f"s2_rel{i}", [P, 2, NE], BF16) for i in range(2)]
    low = [sb(f"s2_low{i}", [P, NE], BF16) for i in range(2)]
    ex = sb("s2_exp", [P, HA, NE])
    W = [sb(f"s2_W{i}", [P, N]) for i in range(2)]
    WT = [sb(f"s2_WT{i}", [P, 2, P]) for i in range(2)]
    xt = [sb(f"s2_x{i}", [P, D]) for i in range(2)]
    junk = sb("s2_junk", [P, N], BF16)
    junkv = sb("s2_junkv", [P, NE], BF16)
    negm = sb("s2_negm", [P, 2, HA])
    negd = sb("s2_negd", [P, HA])
    zs = sb("s2_zs", [P, 2, HA])
    n0 = sb("s2_n0", [P, 2])
    e0 = sb("s2_e0", [P, 3, HA])
    e1 = sb("s2_e1", [P, 3, HA])
    z = sb("s2_z", [P, HA])
    rz = sb("s2_rz", [P, HA])
    r8 = sb("s2_r8", [P, HA])
    re = sb("s2_re", [P, 2, HA])
    cd = sb("s2_cd", [P, 2])
    diag = sb("s2_diag", [P, 1])

    k_in = sem("s2_k_in")
    q_in = [sem(f"s2_q_in{i}") for i in range(2)]
    rel_in = [sem(f"s2_rel_in{i}") for i in range(2)]
    adj_in = [sem(f"s2_adj_in{i}") for i in range(2)]
    x_in = [sem(f"s2_x_in{i}") for i in range(2)]
    y_out = [sem(f"s2_y_out{i}") for i in range(2)]
    mask_step, unrelated, low_ready, adjn_ready = (sem("s2_mask_step"), sem("s2_unrelated"), sem("s2_low"),
                                                   sem("s2_adjn"))
    consts, consts_e = sem("s2_consts"), sem("s2_consts_e")
    scores, negmax, exped, rowsum, efac = sem("s2_scores"), sem("s2_negmax"), sem("s2_exped"), sem("s2_rowsum"), sem("s2_efac")
    fac, added, tail, w_ready = sem("s2_fac"), sem("s2_added"), sem("s2_tail"), sem("s2_w_ready")
    turned, turned_out, agg, summed = sem("s2_turned"), sem("s2_turned_out"), sem("s2_agg"), sem("s2_summed")

    def steps(eng, step):
        for it in (-2, -1, 0, 1):
            step(At(0, it), lambda off, lo, hi, it=it: lo <= it + off < hi)
        with eng.Fori(0, (ET - 4) // 2) as pair:
            for n in (2, 3):
                step(At(pair, n), lambda off, lo, hi: True)
        for it in range(ET - 2, NT + 1):
            step(At(0, it), lambda off, lo, hi, it=it: lo <= it + off < hi)

    with nc.Block() as block:
        @block.sync
        def _(sp):
            def rows(parts, n):
                return parts[n, :, :].rearrange("(h p) j -> p h j", p=DK)
            for dst, a, b in ((k1, 0, 1), (k2, 2, 0)):
                sp.dma_start(dst[0:DK, :, :], rows(t["k_parts"], a)).then_inc(k_in, 16)
                sp.dma_start(dst[DK:P, :, :], rows(t["k_parts"], b)).then_inc(k_in, 16)

            def step(it, has):
                if has(2, 0, ET):
                    q, b = it.par(2), it.par(2)
                    if has(0, 0, ET):
                        sp.wait_ge(scores, HA * it.at(1))
                    for lo, kind, part in ((0, 0, 0), (DK, 0, 0), (0, 1, 1), (DK, 1, 1), (0, 2, 0), (DK, 2, 2)):
                        sp.dma_start(qs[q][lo:lo + DK, kind, :, :],
                                     rows(t["q_parts"], part)[:, :, it.rows(2)]).then_inc(q_in[q], 16)
                    if has(0, 0, ET):
                        sp.wait_ge(adjn_ready, it.at(1))
                    for i in range(2):
                        sp.dma_start(rel[b][:, i, :], t["rel_table"][i][it.rows(2), :]).then_inc(rel_in[b], 16)
                if has(-1, 0, NT):
                    b = it.par(-1)
                    sp.wait_ge(y_out[b], 16 * (it.half(-1) + 1))
                    sp.dma_start(xt[b][:, :], io["x"][it.rows(-1), :]).then_inc(x_in[b], 16)
                    sp.wait_ge(summed, it.at(0))
                    sp.dma_start(t["x1"][it.rows(-1), :], xt[b][:, :]).then_inc(y_out[b], 16)
            for i in range(2):
                sp.sem_inc(y_out[i], 16)
            steps(sp, step)
            for i in range(2):
                sp.wait_ge(y_out[i], 16 * (NT // 2 + 1))

        @block.gpsimd
        def _(pool):
            pool.memset(negd[:, :], -DIAG).then_inc(consts, 1)
            pool.memset(diag[:, :], DIAG).then_inc(consts, 1)

            def step(it, has):
                if not has(2, 0, NT):
                    return
                b, slot, cols = it.par(2), it.at(2) % 4, it.rows(2)
                if has(-2, 0, NT):
                    pool.wait_ge(w_ready, it.at(-1))
                pool.dma_start(adjn[:, slot, :], io["adj"][cols, :]).then_inc(adj_in[b], 16)
                pool.wait_ge(adj_in[b], 16 * (it.half(2) + 1))
                if not has(2, 0, ET):
                    pool.tensor_tensor(adjn[:, slot, cols], adjn[:, slot, cols], t["offdiag"][:, :],
                                       ALU.mult).then_inc(adjn_ready, 1)
                    return
                pool.tensor_tensor(adjn[:, slot, cols], adjn[:, slot, cols], t["offdiag"][:, :],
                                   ALU.mult).then_inc(mask_step, 1)
                pool.wait_ge(rel_in[b], 32 * (it.half(2) + 1))
                pool.tensor_tensor(rel[b][:, 0, :], rel[b][:, 0, :], rel[b][:, 1, :], ALU.add).then_inc(mask_step, 1)
                pool.wait_ge(mask_step, 3 * it.at(2) + 2)
                pool.tensor_tensor(rel[b][:, 0, :], rel[b][:, 0, :], adjn[:, it.at(6) % 4, 0:NE], ALU.mult).then_inc(mask_step, 1)
                pool.wait_ge(unrelated, it.at(3))
                pool.tensor_tensor(adjn[:, it.at(10) % 4, 0:NE], adjn[:, it.at(10) % 4, 0:NE], rel[b][:, 1, :],
                                   ALU.mult).then_inc(adjn_ready, 1)
            steps(pool, step)

        @block.tensor
        def _(pe):
            pe.wait_ge(k_in, 64)

            def turn(it, m):
                n = HA * it.at(-1) + m
                if m == 0:
                    pe.wait_ge(w_ready, it.at(0))
                if not (it.n == 1 and m == 0):
                    pe.wait_ge(turned_out, n)
                for b in range(2):
                    last = pe.transpose(ps[:, 6, b * P:(b + 1) * P],
                                        W[it.par(-1)][:, (2 * m + b) * P:(2 * m + b + 1) * P], t["ident"][:, :])
                last.then_inc(turned, 1)

            def aggregate(it, m, has):
                if m == 0 and has(-2, 0, NT):
                    pe.wait_ge(summed, it.at(-1))
                pe.wait_ge(turned_out, HA * it.at(-1) + m + 1)
                for b in range(2):
                    last = pe.matmul(ps[:, 7, :], WT[m % 2][:, b, :], h[:, 2 * m + b, :],
                                     start=(m == 0 and b == 0), stop=(m == HA - 1 and b == 1))
                last.then_inc(agg, 1)

            def step(it, has):
                nxt, prev = has(1, 0, ET), has(-1, 0, NT)
                for hd in range(HA):
                    if nxt:
                        q = it.par(1)
                        if hd == 0:
                            pe.wait_ge(q_in[q], 96 * (it.half(1) + 1))
                            pe.wait_ge(low_ready, it.at(2))
                        if not (it.n == -1 and hd < 2):
                            pe.wait_ge(exped, HA * it.at(1) + hd - 1)
                        for ch in range(CH):
                            cols = slice(ch * 512, ch * 512 + 512)
                            out = ps[:, 3 * (hd % 2) + ch, :]
                            pe.matmul(out, qs[q][:, 0, hd, :], k1[:, hd, cols], start=True, stop=False)
                            pe.matmul(out, qs[q][:, 1, hd, :], k1[:, hd, cols], start=False, stop=False)
                            pe.matmul(out, qs[q][:, 2, hd, :], k2[:, hd, cols], start=False, stop=False)
                            last = pe.matmul(out, t["identb"][:, :], low[q][:, cols], start=False, stop=True)
                        last.then_inc(scores, 1)
                    if prev:
                        turn(it, hd)
                        if hd:
                            aggregate(it, hd - 1, has)
                if prev:
                    aggregate(it, HA - 1, has)
            steps(pe, step)

        @block.scalar
        def _(act):
            act.wait_ge(consts, 2)
            act.activation(e0[:, 2, :], negd[:, :], ACT.Exp).then_inc(consts_e, 1)
            act.activation(e1[:, 2, :], negd[:, :], ACT.Exp, bias=diag[:, 0:1]).then_inc(consts_e, 1)

            def step(it, has):
                nxt, prev, b = has(1, 0, ET), has(-1, 0, NT), it.par(1)
                if has(1, 0, NT):
                    act.wait_ge(adjn_ready, it.at(2))
                    if not it.n == -1:
                        act.wait_ge(rowsum, it.at(1))
                    if has(-1, 0, NT):
                        act.wait_ge(fac, 6 * it.at(0))
                    act.activation(junk[:, :], adjn[:, it.at(1) % 4, :], ACT.Copy,
                                   accum_out=n0[:, b:b + 1]).then_inc(rowsum, 1)
                for hd in range(HA):
                    if hd == 5 and has(2, 0, ET):
                        m = it.par(2)
                        act.wait_ge(unrelated, it.at(3))
                        if has(0, 0, ET):
                            act.wait_ge(scores, HA * it.at(1))
                        act.activation(low[m][:, :], rel[m][:, 1, :], ACT.Copy, scale=-BIG).then_inc(low_ready, 1)
                    if prev:
                        n = HA * it.at(-1) + hd
                        act.wait_ge(turned, n + 1)
                        if not (it.n == 1 and hd < 2):
                            act.wait_ge(agg, n - 1)
                        act.activation(WT[hd % 2][:, :, :],
                                       ps[:, 6, 0:2 * P].rearrange("p (b i) -> p b i", b=2),
                                       ACT.Copy).then_inc(turned_out, 1)
                    if nxt:
                        act.wait_ge(negmax, HA * it.at(1) + hd + 1)
                        if has(0, 0, ET):
                            act.wait_ge(added, HA * it.at(0) + hd + 1)
                        act.activation(ex[:, hd, :], ps[:, 3 * (hd % 2):3 * (hd % 2) + 3, :].rearrange("p c j -> p (c j)"),
                                       ACT.Exp, bias=negm[:, b, hd:hd + 1], accum_out=zs[:, b, hd:hd + 1]).then_inc(exped, 1)
                if nxt:
                    act.activation(e0[:, b, :], negm[:, b, :], ACT.Exp).then_inc(efac, 1)
                    act.activation(e1[:, b, :], negm[:, b, :], ACT.Exp, bias=diag[:, 0:1]).then_inc(efac, 1)
            steps(act, step)

        @block.vector
        def _(dve):
            dve.wait_ge(consts_e, 2)

            def step(it, has):
                nxt, cur, related, prev = has(1, 0, ET), has(0, 0, NT), has(0, 0, ET), has(-1, 0, NT)
                b, bn = it.par(0), it.par(1)
                w = W[b]
                if cur:
                    f = 6 * it.at(0)
                    k = b if related else 2
                    dve.wait_ge(rowsum, it.at(1))
                    if related:
                        dve.wait_ge(exped, HA * it.at(1))
                        dve.wait_ge(efac, 2 * it.at(1))
                        dve.scalar_tensor_tensor(z[:, :], e0[:, k, :], n0[:, b:b + 1], zs[:, b, :], ALU.mult,
                                                 ALU.add).then_inc(fac, 1)
                        dve.wait_ge(fac, f + 1)
                        dve.tensor_tensor(z[:, :], z[:, :], e1[:, k, :], ALU.add).then_inc(fac, 1)
                    else:
                        dve.scalar_tensor_tensor(z[:, :], e0[:, k, :], n0[:, b:b + 1], e1[:, k, :], ALU.mult,
                                                 ALU.add).then_inc(fac, 2)
                    dve.wait_ge(fac, f + 2)
                    dve.reciprocal(rz[:, :], z[:, :]).then_inc(fac, 1)
                    dve.wait_ge(fac, f + 3)
                    dve.tensor_scalar(r8[:, :], rz[:, :], 1.0 / HA, None, ALU.mult).then_inc(fac, 1)
                    dve.scalar_tensor_tensor(re[:, 0, :], rz[:, :], 1.0 / HA, e0[:, k, :], ALU.mult, ALU.mult,
                                             accum_out=cd[:, 0:1]).then_inc(fac, 1)
                    dve.scalar_tensor_tensor(re[:, 1, :], rz[:, :], 1.0 / HA, e1[:, k, :], ALU.mult, ALU.mult,
                                             accum_out=cd[:, 1:2]).then_inc(fac, 1)
                    if has(-2, 0, NT):
                        dve.wait_ge(turned, HA * it.at(-1))
                    dve.wait_ge(fac, f + 6)
                for hd in range(HA):
                    if hd == 4 and has(2, 0, ET):
                        dve.wait_ge(mask_step, 3 * it.at(3))
                        m = rel[it.par(2)]
                        dve.tensor_scalar(m[:, 1, :], m[:, 0, :], 0.0, None, ALU.is_equal).then_inc(unrelated, 1)
                    if nxt:
                        dve.wait_ge(scores, HA * it.at(1) + hd + 1)
                        if not (it.n == -1 and hd == 0):
                            dve.wait_ge(negmax, HA * it.at(1) + hd)
                        dve.tensor_scalar(junkv[:, :], ps[:, 3 * (hd % 2):3 * (hd % 2) + 3, :].rearrange("p c j -> p (c j)"),
                                          -1.0, -DIAG, ALU.mult, ALU.min,
                                          accum_out=negm[:, bn, hd:hd + 1]).then_inc(negmax, 1)
                    if related:
                        if hd == 0:
                            dve.tensor_scalar(w[:, 0:NE], ex[:, 0, :], r8[:, 0:1], None, ALU.mult).then_inc(added, 1)
                        else:
                            dve.wait_ge(added, HA * it.at(0) + hd)
                            dve.scalar_tensor_tensor(w[:, 0:NE], ex[:, hd, :], r8[:, hd:hd + 1], w[:, 0:NE], ALU.mult,
                                                     ALU.add).then_inc(added, 1)
                if cur:
                    nbr = adjn[:, it.at(0) % 4, :]
                    if related:
                        dve.wait_ge(added, HA * it.at(1))
                        dve.scalar_tensor_tensor(w[:, 0:NE], adjn[:, it.at(0) % 4, 0:NE], cd[:, 0:1], w[:, 0:NE], ALU.mult,
                                                 ALU.add).then_inc(tail, 1)
                        dve.tensor_scalar(w[:, NE:N], adjn[:, it.at(0) % 4, NE:N], cd[:, 0:1], None, ALU.mult).then_inc(tail, 1)
                    else:
                        dve.tensor_scalar(w[:, :], nbr, cd[:, 0:1], None, ALU.mult).then_inc(tail, 2)
                    dve.wait_ge(tail, 2 * it.at(1))
                    dve.scalar_tensor_tensor(w[:, it.rows()], t["ident"][:, :], cd[:, 1:2], w[:, it.rows()], ALU.mult,
                                             ALU.add).then_inc(w_ready, 1)
                if prev:
                    p = it.par(-1)
                    dve.wait_ge(agg, HA * it.at(0))
                    dve.wait_ge(x_in[p], 16 * (it.half(-1) + 1))
                    dve.tensor_tensor(xt[p][:, :], xt[p][:, :], ps[:, 7, :], ALU.add).then_inc(summed, 1)
            steps(dve, step)


def stage3(nc, c, io, t, s, ps):
    sb = lambda name, shape, dt=F32: c.enter_context(nc.sbuf_tensor(name, shape, dt))
    sem = lambda name: c.enter_context(nc.semaphore(name))
    seq, adjT = t["seq"], t["adjT"]
    xs = sb("s3_x", [P, NT, D])
    wseq = sb("s3_w", [P, KT, D])
    a12 = sb("s3_a", [P, 2, DH])
    stats = sb("s3_stats", [P, NT, 6])
    mv = sb("s3_mv", [P, NT, 2])
    std = sb("s3_std", [P, NT])
    rstd = sb("s3_rstd", [P, NT])
    nmr = sb("s3_nmr", [P, NT])
    hb = [sb(f"s3_h{i}", [P, D]) for i in range(2)]
    hT = [sb(f"s3_hT{i}", [P, KT, P]) for i in range(2)]
    adjb = [sb(f"s3_adj{i}", [P, N], BF16) for i in range(2)]
    prod = [sb(f"s3_prod{i}", [P, 2, D]) for i in range(2)]
    sc = sb("s3_sc", [P, 2, HB, NT])
    top = sb("s3_top", [P, HB])
    topa = sb("s3_topa", [P, HB])
    d = sb("s3_d", [P, HB, NT])
    u = sb("s3_u", [P, HB, NT])
    m = sb("s3_m", [P, HB, NT])
    shift = sb("s3_shift", [P, 1])
    s1T = sb("s3_s1T", [P, 2, P])

    x_in = [sem(f"s3_x_in{i}") for i in range(4)]
    w_in, a_in = sem("s3_w_in"), sem("s3_a_in")
    adj_in = [sem(f"s3_adj_in{i}") for i in range(2)]
    consts, stat, var_ready, std_ready, norm_ready = (sem("s3_consts"), sem("s3_stat"), sem("s3_var"), sem("s3_std"),
                                                      sem("s3_norm"))
    h_ready, h_turned, hT_ready, adj_turned, adj_out_a, adj_out_v, seq_psum, seq_ready, prods, scored = (
        sem("s3_h"), sem("s3_h_turned"), sem("s3_hT"), sem("s3_adj_turned"), sem("s3_adj_out_a"), sem("s3_adj_out_v"),
        sem("s3_seq_psum"), sem("s3_seq"), sem("s3_prods"), sem("s3_scored"))
    topped, top_all, chain, expd, sT_psum, sT_ready, rows_out = (sem("s3_topped"), sem("s3_top_all"), sem("s3_chain"),
                                                                sem("s3_expd"), sem("s3_sT_psum"), sem("s3_sT"),
                                                                sem("s3_rows_out"))

    def steps(eng, step):
        for it in (0, 1):
            step(At(0, it), True)
        with eng.Fori(0, (NT - 2) // 2) as pair:
            for n in (2, 3):
                step(At(pair, n), False)

    with nc.Block() as block:
        @block.sync
        def _(sp):
            for i in range(4):
                sp.dma_start(xs[:, 4 * i:4 * i + 4, :],
                             t["x1"][512 * i:512 * i + 512, :].rearrange("(t p) k -> p t k", p=P)).then_inc(x_in[i], 16)
            sp.dma_start(wseq[:, :, :], io["L1_gnn_W_seq"].rearrange("(t p) n -> p t n", p=P)).then_inc(w_in, 16)
            for i, a in enumerate((io["L1_gnn_a1"], io["L1_gnn_a2"])):
                sp.dma_start(a12[:, i, :], a.rearrange("(o d) -> o d", o=1).to_broadcast([P, DH])).then_inc(a_in, 16)
            sp.wait_ge(sT_ready, 2)
            for g in range(2):
                sp.dma_start(t["s1_rows"].rearrange("h (t i) -> (h t) i", i=P)[g * P:(g + 1) * P, :],
                             s1T[:, g, :]).then_inc(rows_out, 16)
            sp.wait_ge(rows_out, 32)

        @block.gpsimd
        def _(pool):
            pool.memset(shift[:, :], SHIFT).then_inc(consts, 1)
            for i in range(2):
                pool.dma_start(adjb[i][:, :], io["adj"][i * P:(i + 1) * P, :]).then_inc(adj_in[i], 16)
            pool.wait_ge(a_in, 32)

            def step(it, first):
                b = it.par()
                pool.wait_ge(seq_ready, it.at(1))
                if not first:
                    pool.wait_ge(scored, 2 * it.at(-1))
                for i in range(2):
                    pool.tensor_tensor(prod[b][:, i, :].rearrange("p (h d) -> p h d", h=HB),
                                       seq[:, it.at(), :].rearrange("p (h d) -> p h d", h=HB),
                                       a12[:, i, None, :].to_broadcast([P, HB, DH]), ALU.mult).then_inc(prods, 1)

            def load_adj(it):
                pool.wait_ge(adj_turned, 2 * it.at(-1))
                pool.dma_start(adjb[it.par()][:, :], io["adj"][it.rows(), :]).then_inc(adj_in[it.par()], 16)
            for it in (0, 1):
                load_adj(At(0, it + 2))
                step(At(0, it), True)
            with pool.Fori(0, (NT - 4) // 2) as pair:
                for n in (2, 3):
                    load_adj(At(pair, n + 2))
                    step(At(pair, n), False)
            for it in (NT - 2, NT - 1):
                step(At(0, it), False)
            pool.wait_ge(topped, 1)
            pool.partition_all_reduce(topa[:, :], top[:, :], P, bass.bass_isa.ReduceOp.max).then_inc(top_all, 1)

        @block.vector
        def _(dve):
            for i in range(NT):
                if i % 4 == 0:
                    dve.wait_ge(x_in[i // 4], 16)
                dve.bn_stats(stats[:, i, :], xs[:, i, :]).then_inc(stat, 1)
            dve.wait_ge(stat, NT)
            for i in range(NT):
                dve.bn_aggr(mv[:, i, :], stats[:, i, :]).then_inc(stat, 1)
            dve.wait_ge(stat, 2 * NT)
            dve.tensor_scalar(rstd[:, :], mv[:, :, 1], EPS, None, ALU.add).then_inc(var_ready, 1)
            dve.wait_ge(std_ready, 1)
            dve.reciprocal(rstd[:, :], std[:, :]).then_inc(var_ready, 1)
            dve.wait_ge(var_ready, 2)
            dve.scalar_tensor_tensor(nmr[:, :], mv[:, :, 0], -1.0, rstd[:, :], ALU.mult, ALU.mult).then_inc(norm_ready, 1)

            def step(it, first):
                b = it.par()
                dve.wait_ge(h_turned, it.at(1))
                if not first:
                    dve.wait_ge(seq_psum, it.at(-1))
                dve.tensor_copy(hT[b][:, :, :], ps[:, b, :].rearrange("p (k i) -> p k i", k=KT)).then_inc(hT_ready, 1)
                dve.wait_ge(adj_turned, 2 * it.at() + 2)
                dve.tensor_copy(adjT[:, 8:16, it.rows()],
                                ps[:, 3, :].bitcast(BF16).rearrange("p (j i) -> p j i", j=8)).then_inc(adj_out_v, 1)

            def score(it):
                for i in range(2):
                    dve.wait_ge(prods, 2 * it.at() + i + 1)
                    dve.reduce_sum(sc[:, i, :, it.at()], prod[it.par()][:, i, :].rearrange("p (h d) -> p h d", h=HB),
                                   AX.X).then_inc(scored, 1)
            step(At(0, 0), True)
            step(At(0, 1), True)
            with dve.Fori(0, (NT - 2) // 2) as pair:
                for n in (2, 3):
                    step(At(pair, n), False)
                    score(At(pair, n - 2))
            score(At(0, NT - 2))
            score(At(0, NT - 1))

            steps_done = [0]

            def link(ins):
                steps_done[0] += 1
                ins.then_inc(chain, 1)
                dve.wait_ge(chain, steps_done[0])
            dve.wait_ge(scored, 2 * NT)
            s1, s2 = sc[:, 0, :, :], sc[:, 1, :, :]
            dve.reduce_max(top[:, :], s2, AX.X).then_inc(topped, 1)
            dve.tensor_scalar(t["ns2"][:, :, :], s2, -1.0, None, ALU.mult)\
                .then_inc(t["lasting"], 1)
            for g in range(2):
                dve.wait_ge(sT_psum, g + 1)
                dve.tensor_copy(s1T[:, g, :], ps[:, 6, g * P:(g + 1) * P]).then_inc(sT_ready, 1)
            dve.wait_ge(top_all, 1)
            tops = topa[:, :, None].to_broadcast([P, HB, NT])
            link(dve.tensor_tensor(d[:, :, :], s2, tops, ALU.subtract))
            link(dve.tensor_tensor(u[:, :, :], s1, tops, ALU.add))
            link(dve.scalar_tensor_tensor(m[:, :, :], u[:, :, :], SLOPE, u[:, :, :], ALU.mult, ALU.max))
            link(dve.scalar_tensor_tensor(t["wb"][:, :, :], u[:, :, :], SLOPE, m[:, :, :], ALU.mult, ALU.subtract))
            link(dve.tensor_tensor(t["wa"][:, :, :], u[:, :, :], m[:, :, :], ALU.subtract))

        @block.scalar
        def _(act):
            act.wait_ge(var_ready, 1)
            act.activation(std[:, :], rstd[:, :], ACT.Sqrt).then_inc(std_ready, 1)
            act.wait_ge(norm_ready, 1)

            def relu(it, first):
                if not first:
                    act.wait_ge(h_turned, it.at(-1))
                act.activation(hb[it.par()][:, :], xs[:, it.at(), :], ACT.Relu, bias=nmr[:, bass.ds(it.at(), 1)],
                               scale=rstd[:, bass.ds(it.at(), 1)]).then_inc(h_ready, 1)

            def step(it):
                act.wait_ge(adj_turned, 2 * it.at() + 1)
                act.activation(adjT[:, 0:8, it.rows()], ps[:, 2, :].bitcast(BF16).rearrange("p (j i) -> p j i", j=8),
                               ACT.Copy).then_inc(adj_out_a, 1)
                act.wait_ge(seq_psum, it.at(1))
                act.activation(seq[:, it.at(), :], ps[:, 4 + it.par(), :], ACT.Copy).then_inc(seq_ready, 1)
            relu(At(0, 0), True)
            relu(At(0, 1), True)
            with act.Fori(0, (NT - 2) // 2) as pair:
                for n in (0, 1):
                    step(At(pair, n))
                    relu(At(pair, n + 2), False)
            step(At(0, NT - 2))
            step(At(0, NT - 1))
            act.wait_ge(consts, 1)
            act.wait_ge(chain, 1)
            act.activation(t["ea"][:, :, :].rearrange("p t h -> p h t"), d[:, :, :], ACT.Exp, bias=shift[:, 0:1]).then_inc(expd, 1)
            act.activation(t["eb"][:, :, :].rearrange("p t h -> p h t"), d[:, :, :], ACT.Exp, bias=shift[:, 0:1],
                           scale=SLOPE).then_inc(expd, 1)
            act.wait_ge(chain, 5)
            for w in ("wa", "wb"):
                act.activation(t[w][:, :, :], t[w][:, :, :], ACT.Exp).then_inc(expd, 1)

        @block.tensor
        def _(pe):
            pe.wait_ge(w_in, 16)

            def turn(it, first):
                b = it.par()
                pe.wait_ge(h_ready, it.at(1))
                if not first:
                    pe.wait_ge(hT_ready, it.at(-1))
                for k in range(KT):
                    last = pe.transpose(ps[:, b, k * P:(k + 1) * P], hb[b][:, k * P:(k + 1) * P], t["ident"][:, :])
                last.then_inc(h_turned, 1)

            def step(it, first, last_tile=False):
                b = it.par()
                pe.wait_ge(adj_in[b], 16 * (it.half() + 1))
                for half, out in ((0, adj_out_a), (1, adj_out_v)):
                    if not (first and b == 0):
                        pe.wait_ge(out, it.at())
                    for j in range(8):
                        last = pe.transpose(ps[:, 2 + half, :].bitcast(BF16)[:, j * P:(j + 1) * P],
                                            adjb[b][:, (8 * half + j) * P:(8 * half + j + 1) * P], t["identb"][:, :])
                    last.then_inc(adj_turned, 1)
                if not last_tile:
                    turn(At(it.pair, it.n + 1), first and b == 0)
                pe.wait_ge(hT_ready, it.at(1))
                if not first:
                    pe.wait_ge(seq_ready, it.at(-1))
                for k in range(KT):
                    last = pe.matmul(ps[:, 4 + b, :], hT[b][:, k, :], wseq[:, k, :], start=(k == 0), stop=(k == KT - 1))
                last.then_inc(seq_psum, 1)
            turn(At(0, 0), True)
            step(At(0, 0), True)
            step(At(0, 1), True)
            with pe.Fori(0, (NT - 4) // 2) as pair:
                for n in (2, 3):
                    step(At(pair, n), False)
            step(At(0, NT - 2), False)
            step(At(0, NT - 1), False, last_tile=True)
            pe.wait_ge(scored, 2 * NT)
            for g in range(2):
                if g:
                    pe.wait_ge(sT_ready, g)
                pe.transpose(ps[:, 6, g * P:(g + 1) * P],
                             sc[:, 0, 8 * g:8 * g + 8, :].rearrange("p h t -> p (h t)"), t["ident"][:, :]).then_inc(sT_psum, 1)


RING = 8
HALF = N // 2
HT = HALF // P
VECTOR_ONLY = (4, 9, 14)
NS = NT - len(VECTOR_ONLY)
UG = 2 * GH
VB = NT // UG
AT = NT // UG
HEAD_START = 6
BANK_START = 2


def stage4(nc, c, io, t, s, ps):
    sb = lambda name, shape, dt=F32: c.enter_context(nc.sbuf_tensor(f"s4_{name}", shape, dt))
    sem = lambda name: c.enter_context(nc.semaphore(f"s4_{name}"))
    seq, adjT = t["seq"], t["adjT"]
    GZ = GH * DZ
    V = sb("V", [P, 3, NT, 3, 2, GZ], BF16)
    A2 = sb("A2", [P, 3, NT, GZ])
    masks = sb("masks", [P, RING, HALF], BF16)
    s1b = [sb(f"s1b{i}", [P, HALF]) for i in range(2)]
    bs2 = [sb(f"bs2{i}", [P, NT]) for i in range(2)]
    tmp = [sb(f"tmp{i}", [P, VB, 2, GZ]) for i in range(2)]
    sums = [sb(f"sums{i}", [P, HT, 2, DZ]) for i in range(2)]
    hid = [sb(f"hid{i}", [P, HT, DZ]) for i in range(2)]

    value, hi_out, rest, mid_out, split = sem("value"), sem("hi"), sem("rest"), sem("mid"), sem("split")
    near_psum, near_out = sem("near_psum"), sem("near_out")
    s1_in = [sem(f"s1_in{i}") for i in range(2)]
    hid_out = [sem(f"hid_out{i}") for i in range(2)]
    bs2_ready, signs, mask_ready, mask_used = sem("bs2_ready"), sem("signs"), sem("mask"), sem("mask_used")
    bank_free, summed, sums_free, comb, hid_ready = (sem("bank_free"), sem("summed"), sem("sums_free"), sem("comb"),
                                                     sem("hid"))

    with nc.Block() as block:
        @block.sync
        def _(sp):
            def load(k, half):
                sp.dma_start(s1b[half][:, :],
                             t["s1_rows"][bass.ds(k, 1), half * HALF:(half + 1) * HALF].to_broadcast([P, HALF])
                             ).then_inc(s1_in[half], 16)

            def store(k, half):
                sp.wait_ge(hid_ready, 2 * k + half + 1)
                sp.dma_start(t["hidden"][half * HALF:(half + 1) * HALF, k, :].rearrange("(t p) d -> p t d", p=P),
                             hid[half][:, :, :]).then_inc(hid_out[half], 16)
            load(0, 0)
            load(0, 1)
            with sp.Fori(0, HB - 1) as k:
                for half in range(2):
                    sp.wait_ge(mask_ready, NT * (2 * k + half + 1))
                    load(k + 1, half)
                    if half:
                        store(k, 0)
                store(k, 1)
            for half in range(2):
                store(HB - 1, half)
            for half in range(2):
                sp.wait_ge(hid_out[half], 16 * (HB + 1))

        @block.gpsimd
        def _(pool):
            for half in range(2):
                pool.sem_inc(hid_out[half], 16)
            pool.sem_inc(sums_free, 2)

            def values(g, u, first=False):
                b, n = u % 2, UG * g + u
                js = slice(VB * u, VB * u + VB)
                if not first:
                    pool.wait_ge(split, n - 1)
                for k, e in enumerate((t["ea"], t["eb"])):
                    for hh in range(GH):
                        head = GH * g + hh
                        w = e[:, js, head]
                        pool.tensor_tensor(tmp[b][:, :, k, hh * DZ:hh * DZ + DH], seq[:, js, bass.ds(head * DH, DH)],
                                           w[:, :, None].to_broadcast([P, VB, DH]), ALU.mult).then_inc(value, 1)
                        pool.tensor_copy(tmp[b][:, :, k, hh * DZ + DH], w).then_inc(value, 1)

            def combine(g, u):
                n, hh, half = UG * g + u, u // 2, u % 2
                q, out, rows = sums[half], hid[half], slice(half * HT, (half + 1) * HT)
                wa, wb = (t[w][:, GH * g + hh, rows].rearrange("p (t o) -> p t o", o=1).to_broadcast([P, HT, DZ])
                          for w in ("wa", "wb"))
                pool.wait_ge(summed, n + 1)
                pool.wait_ge(hid_out[half], 16 * (GH * g + hh + 1))
                pool.tensor_tensor(out[:, :, :], A2[:, g % 3, rows, hh * DZ:(hh + 1) * DZ], q[:, :, 1, :],
                                   ALU.subtract).then_inc(comb, 1)
                pool.tensor_tensor(q[:, :, 0, :], q[:, :, 0, :], wa, ALU.mult).then_inc(comb, 1)
                pool.wait_ge(comb, 3 * n + 1)
                pool.tensor_tensor(out[:, :, :], out[:, :, :], wb, ALU.mult).then_inc(comb, 1)
                pool.wait_ge(comb, 3 * n + 3)
                pool.tensor_tensor(out[:, :, :], out[:, :, :], q[:, :, 0, :], ALU.add).then_inc(hid_ready, 1)
                pool.wait_ge(hid_ready, n + 1)
                pool.sem_inc(sums_free, 1)
            for n in range(2 * UG):
                values(n // UG, n % UG, first=n < 2)
            with pool.Fori(0, NG - 2) as g:
                for u in range(UG):
                    values(g + 2, u)
                    combine(g, u)
            for g in (NG - 2, NG - 1):
                for u in range(UG):
                    combine(g, u)

        @block.scalar
        def _(act):
            def part(g, u, p):
                n = UG * g + u
                act.wait_ge(*((value, 4 * GH * (n + 1)) if p == 0 else (rest, n + 1)))
                act.activation(V[:, g % 3, VB * u:VB * u + VB, p, :, :], tmp[u % 2][:, :, :, :],
                               ACT.Copy).then_inc(hi_out if p == 0 else mid_out, 1)

            def unit(g, u, build=True):
                n, half = UG * g + u, u % 2
                act.wait_ge(s1_in[half], 16 * (GH * g + u // 2 + 1))
                act.wait_ge(bs2_ready, n + 1)
                for j in range(NT):
                    if j not in VECTOR_ONLY:
                        act.wait_ge(mask_used, NT * n + j + 1)
                        act.activation(masks[:, j % RING, :], s1b[half][:, :], ACT.Relu,
                                       bias=bs2[half][:, j:j + 1], scale=BIG).then_inc(signs, 1)
                    if build and j == 13:
                        part(g + 2, u, 0)
                if build:
                    part(g + 2, u, 1)
            for n in range(2 * UG):
                part(n // UG, n % UG, 0)
                part(n // UG, n % UG, 1)
            with act.Fori(0, NG - 2) as g:
                for u in range(UG):
                    unit(g, u)
            for g in (NG - 2, NG - 1):
                for u in range(UG):
                    unit(g, u, build=False)

        @block.vector
        def _(dve):
            dve.sem_inc(bank_free, 1)

            def take_off(g, u, p):
                n = UG * g + u
                dve.wait_ge(hi_out if p == 0 else mid_out, n + 1)
                left = tmp[u % 2][:, :, :, :].rearrange("p j k c -> p j (k c)")
                js = slice(VB * u, VB * u + VB)
                out = left if p == 0 else V[:, g % 3, js, 2, :, :].rearrange("p j k c -> p j (k c)")
                dve.tensor_tensor(out, left, V[:, g % 3, js, p, :, :].rearrange("p j k c -> p j (k c)"),
                                  ALU.subtract).then_inc(rest if p == 0 else split, 1)

            def scaled_scores(g, u):
                n = UG * g + u
                head = GH * g + u // 2
                if not isinstance(n, int) or n:
                    dve.wait_ge(signs, NS * (n - 1) + 1)
                dve.tensor_scalar(bs2[u % 2][:, :], t["ns2"][:, head, :], -BIG, None, ALU.mult).then_inc(bs2_ready, 1)

            def mask(g, u, j):
                n, half = UG * g + u, u % 2
                out, near = masks[:, j % RING, :], adjT[:, j, half * HALF:(half + 1) * HALF]
                if j in VECTOR_ONLY:
                    dve.wait_ge(mask_used, NT * n + j + 1)
                    dve.wait_ge(s1_in[half], 16 * (GH * g + u // 2 + 1))
                    dve.scalar_tensor_tensor(out, s1b[half][:, :], t["ns2"][:, GH * g + u // 2, j:j + 1], near,
                                             ALU.is_gt, ALU.mult).then_inc(mask_ready, 1)
                else:
                    before = sum(x not in VECTOR_ONLY for x in range(j))
                    dve.wait_ge(signs, NS * n + before + 1)
                    dve.tensor_tensor(out, out, near, ALU.min).then_inc(mask_ready, 1)

            def mask_sums(g, u):
                n = UG * g + u
                dve.wait_ge(mask_used, RING + NT * (n + 1))
                dve.wait_ge(sums_free, n + 1)
                dve.reduce_sum(sums[u % 2][:, :, :, :].rearrange("p t k d -> p t (k d)"),
                               ps[:, 0:4, :].rearrange("p b (u c) -> p (b u) c", u=2)[:, :, 0:6 * DZ]
                               .rearrange("p t (s c) -> p t c s", s=3), AX.X).then_inc(summed, 1)
                dve.wait_ge(summed, n + 1)
                dve.sem_inc(bank_free, 1)

            def near_sums(g, u):
                n = UG * g + u
                dve.wait_ge(near_psum, n + 1)
                b = 4 + 2 * (u % 2)
                dve.reduce_sum(A2[:, g % 3, AT * u:AT * u + AT, :],
                               ps[:, b:b + 2, :].rearrange("p b (u c) -> p (b u) c", u=2)[:, :, 0:3 * GZ]
                               .rearrange("p t (s c) -> p t c s", s=3), AX.X).then_inc(near_out, 1)

            def unit(g, u, build=True, ahead=True, last=False):
                nxt = (g, u + 1) if u + 1 < UG else (g + 1, 0)
                for j in range(HEAD_START, NT):
                    if j == HEAD_START + 1 and not last:
                        scaled_scores(*nxt)
                    if build and j == 10:
                        take_off(g + 2, u, 0)
                    if build and j == 14:
                        take_off(g + 2, u, 1)
                    mask(g, u, j)
                if not last:
                    for j in range(BANK_START):
                        mask(*nxt, j)
                mask_sums(g, u)
                if not last:
                    for j in range(BANK_START, HEAD_START):
                        mask(*nxt, j)
                if ahead:
                    near_sums(g + 1, u)
            for n in range(2 * UG):
                for p in range(2):
                    take_off(n // UG, n % UG, p)
                if n == 0:
                    scaled_scores(0, 0)
                if n >= UG:
                    near_sums(0, n - UG)
            for j in range(HEAD_START):
                mask(0, 0, j)
            with dve.Fori(0, NG - 2) as g:
                for u in range(UG):
                    unit(g, u)
            for u in range(UG):
                unit(NG - 2, u, build=False)
            for u in range(UG):
                unit(NG - 1, u, build=False, ahead=False, last=u == UG - 1)

        @block.tensor
        def _(pe):
            pe.sem_inc(mask_used, RING)

            def near(g, u, first=False):
                n, b = UG * g + u, 4 + 2 * (u % 2)
                if not first:
                    pe.wait_ge(near_out, n - 1)
                pe.wait_ge(split, UG * (g + 1))
                for i in range(AT):
                    it = AT * u + i
                    for j in range(NT):
                        last = pe.matmul(ps[:, b + i // 2, 256 * (i % 2):256 * (i % 2) + 3 * GZ]
                                         .rearrange("p (s c) -> p s c", s=3),
                                         adjT[:, j, it * P:(it + 1) * P], V[:, g % 3, j, :, 1, :],
                                         start=(j == 0 and i % 2 == 0), stop=(j == NT - 1), skip_group_check=True)
                last.then_inc(near_psum, 1)

            def unit(g, u, ahead=True):
                n = UG * g + u
                hh = u // 2
                pe.wait_ge(bank_free, n + 1)
                for j in range(NT):
                    pe.wait_ge(mask_ready, NT * n + j + 1)
                    for i in range(HT):
                        last = pe.matmul(ps[:, i // 2, 256 * (i % 2):256 * (i % 2) + 6 * DZ]
                                         .rearrange("p (s d) -> p s d", s=6),
                                         masks[:, j % RING, i * P:(i + 1) * P],
                                         V[:, g % 3, j, :, :, hh * DZ:(hh + 1) * DZ].rearrange("p s k d -> p (s k) d"),
                                         start=(j == 0 and i % 2 == 0), stop=(j == NT - 1), skip_group_check=True)
                    last.then_inc(mask_used, 1)
                if ahead:
                    near(g + 1, u)
            for u in range(UG):
                near(0, u, first=u < 2)
            with pe.Fori(0, NG - 1) as g:
                for u in range(UG):
                    unit(g, u)
            for u in range(UG):
                unit(NG - 1, u, ahead=False)


def stage5(nc, c, io, out, t, s, ps):
    sb = lambda name, shape, dt=F32: c.enter_context(nc.sbuf_tensor(name, shape, dt))
    sem = lambda name: c.enter_context(nc.semaphore(name))
    wout = sb("s5_w", [P, KT, D])
    bout = sb("s5_b", [P, D])
    hid = [sb(f"s5_hid{i}", [P, HB, DZ]) for i in range(2)]
    x1 = [sb(f"s5_x{i}", [P, D]) for i in range(2)]
    rz = [sb(f"s5_rz{i}", [P, HB]) for i in range(2)]
    hn = [sb(f"s5_hn{i}", [P, D]) for i in range(2)]
    hT = [sb(f"s5_hT{i}", [P, KT, P]) for i in range(2)]
    v = [sb(f"s5_v{i}", [P, D]) for i in range(2)]
    e = [sb(f"s5_e{i}", [P, D]) for i in range(2)]
    w_in = sem("s5_w_in")
    hid_in = [sem(f"s5_hid_in{i}") for i in range(2)]
    x_in = [sem(f"s5_x_in{i}") for i in range(2)]
    y_out = [sem(f"s5_y_out{i}") for i in range(2)]
    inv, normed, turned, turned_out, proj, biased, low, expd, added, done = (
        sem("s5_inv"), sem("s5_normed"), sem("s5_turned"), sem("s5_turned_out"), sem("s5_proj"), sem("s5_biased"),
        sem("s5_low"), sem("s5_expd"), sem("s5_added"), sem("s5_done"))

    def steps(eng, step):
        for it in (0, 1):
            step(At(0, it), True)
        with eng.Fori(0, (NT - 2) // 2) as pair:
            for n in (2, 3):
                step(At(pair, n), False)

    with nc.Block() as block:
        @block.sync
        def _(sp):
            sp.dma_start(wout[:, :, :], io["L1_gnn_W_out"].rearrange("(t p) n -> p t n", p=P)).then_inc(w_in, 16)
            sp.dma_start(bout[:, :], io["L1_gnn_b_out"].rearrange("(o d) -> o d", o=1).to_broadcast([P, D])).then_inc(w_in, 16)

            def step(it, first):
                b = it.par()
                if not first:
                    sp.wait_ge(normed, it.at(-1))
                sp.dma_start(hid[b][:, :, :], t["hidden"][it.rows(), :, :]).then_inc(hid_in[b], 16)
                if not first:
                    sp.wait_ge(y_out[b], 16 * it.half())
                sp.dma_start(x1[b][:, :], t["x1"][it.rows(), :]).then_inc(x_in[b], 16)
            steps(sp, step)

        @block.vector
        def _(dve):
            def norm(it, first):
                b = it.par()
                dve.wait_ge(hid_in[b], 16 * (it.half() + 1))
                dve.reciprocal(rz[b][:, :], hid[b][:, :, DH]).then_inc(inv, 1)
                dve.wait_ge(inv, it.at(1))
                if not first:
                    dve.wait_ge(turned, it.at(-1))
                dve.tensor_tensor(hn[b][:, :].rearrange("p (h d) -> p h d", h=HB), hid[b][:, :, 0:DH],
                                  rz[b][:, :, None].to_broadcast([P, HB, DH]), ALU.mult).then_inc(normed, 1)

            def finish(it, first):
                b = it.par()
                dve.wait_ge(proj, it.at(1))
                dve.wait_ge(w_in, 32)
                dve.tensor_tensor(v[b][:, :], ps[:, 2 + b, :], bout[:, :], ALU.add).then_inc(biased, 1)
                dve.wait_ge(biased, it.at(1))
                if not first:
                    dve.wait_ge(added, it.at(-1))
                dve.tensor_scalar(e[b][:, :], v[b][:, :], 0.0, None, ALU.min).then_inc(low, 1)
                dve.wait_ge(x_in[b], 16 * (it.half() + 1))
                dve.wait_ge(expd, it.at(1))
                dve.scalar_tensor_tensor(e[b][:, :], e[b][:, :], -1.0, x1[b][:, :], ALU.add, ALU.add).then_inc(added, 1)
                dve.wait_ge(added, it.at(1))
                dve.scalar_tensor_tensor(x1[b][:, :], v[b][:, :], 0.0, e[b][:, :], ALU.max, ALU.add).then_inc(done, 1)
            norm(At(0, 0), True)
            norm(At(0, 1), True)
            finish(At(0, 0), True)
            norm(At(0, 2), False)
            finish(At(0, 1), True)
            norm(At(0, 3), False)
            with dve.Fori(0, (NT - 4) // 2) as pair:
                for n in (2, 3):
                    finish(At(pair, n), False)
                    norm(At(pair, n + 2), False)
            for it in (NT - 2, NT - 1):
                finish(At(0, it), False)

        @block.tensor
        def _(pe):
            pe.wait_ge(w_in, 32)

            def turn(it, first):
                b = it.par()
                pe.wait_ge(normed, it.at(1))
                if not first:
                    pe.wait_ge(turned_out, it.at(-1))
                for k in range(KT):
                    last = pe.transpose(ps[:, b, k * P:(k + 1) * P], hn[b][:, k * P:(k + 1) * P], t["ident"][:, :])
                last.then_inc(turned, 1)

            def project(it, first):
                b = it.par()
                pe.wait_ge(turned_out, it.at(1))
                if not first:
                    pe.wait_ge(biased, it.at(-1))
                for k in range(KT):
                    last = pe.matmul(ps[:, 2 + b, :], hT[b][:, k, :], wout[:, k, :], start=(k == 0), stop=(k == KT - 1))
                last.then_inc(proj, 1)
            turn(At(0, 0), True)
            turn(At(0, 1), True)
            project(At(0, 0), True)
            turn(At(0, 2), False)
            project(At(0, 1), True)
            turn(At(0, 3), False)
            with pe.Fori(0, (NT - 4) // 2) as pair:
                for n in (2, 3):
                    project(At(pair, n), False)
                    turn(At(pair, n + 2), False)
            for it in (NT - 2, NT - 1):
                project(At(0, it), False)

        @block.scalar
        def _(act):
            def copy(it, first):
                b = it.par()
                act.wait_ge(turned, it.at(1))
                if not first:
                    act.wait_ge(proj, it.at(-1))
                act.activation(hT[b][:, :, :], ps[:, b, :].rearrange("p (k i) -> p k i", k=KT), ACT.Copy).then_inc(turned_out, 1)

            def exp(it):
                b = it.par()
                act.wait_ge(low, it.at(1))
                act.activation(e[b][:, :], e[b][:, :], ACT.Exp).then_inc(expd, 1)
            copy(At(0, 0), True)
            copy(At(0, 1), True)
            with act.Fori(0, (NT - 2) // 2) as pair:
                for n in (0, 1):
                    exp(At(pair, n))
                    copy(At(pair, n + 2), False)
            for it in (NT - 2, NT - 1):
                exp(At(0, it))

        @block.gpsimd
        def _(pool):
            with pool.Fori(0, NT // 2) as pair:
                for n in (0, 1):
                    it = At(pair, n)
                    pool.wait_ge(done, it.at(1))
                    pool.dma_start(out[it.rows(), :], x1[n][:, :]).then_inc(y_out[n], 16)
            for i in range(2):
                pool.wait_ge(y_out[i], 16 * NT // 2)


INS = ["x", "adj", "L0_gnn_rel_pair_index", "L0_gnn_Wq", "L0_gnn_bq", "L0_gnn_Wk", "L0_gnn_bk", "L1_gnn_W_seq",
       "L1_gnn_a1", "L1_gnn_a2", "L1_gnn_W_out", "L1_gnn_b_out"]


def build(nc, io, out, kind="Internal", upto=5):
    dram = lambda name, shape, dt=F32: nc.dram_tensor(name, shape, dt, kind=kind).ap()
    t = {
        "q_parts": dram("q_parts", [3, D, NE], BF16), "k_parts": dram("k_parts", [3, D, NE], BF16),
        "rel_table": [dram(f"rel_table{i}", [NE, NE], BF16) for i in range(2)], "x1": dram("x1", [N, D]),
        "s1_rows": dram("s1_rows", [HB, N]), "hidden": dram("hidden", [N, HB, DZ]),
    }
    with ExitStack() as c:
        t["ident"] = c.enter_context(nc.sbuf_tensor("ident", [P, P], F32))
        t["identb"] = c.enter_context(nc.sbuf_tensor("identb", [P, P], BF16))
        t["offdiag"] = c.enter_context(nc.sbuf_tensor("offdiag", [P, P], BF16))
        ps = c.enter_context(nc.psum_tensor("psum", [P, 8, 512], F32))
        s = {n: c.enter_context(nc.semaphore(n)) for n in ("zeroed", "const", "lasting")}
        make_constants(nc, t, s)
        with ExitStack() as first:
            t["h"] = first.enter_context(nc.sbuf_tensor("h", [P, NT, D], F32))
            with ExitStack() as part:
                stage1(nc, part, io, t, s, ps)
            if upto >= 2:
                with ExitStack() as part:
                    stage2(nc, part, io, t, s, ps)
        if upto >= 3:
            with ExitStack() as second:
                sb = lambda name, shape, dt=F32: second.enter_context(nc.sbuf_tensor(name, shape, dt))
                t["seq"] = sb("seq", [P, NT, D])
                t["adjT"] = sb("adjT", [P, NT, N], BF16)
                for name in ("ns2", "wa", "wb"):
                    t[name] = sb(name, [P, HB, NT])
                for name in ("ea", "eb"):
                    t[name] = sb(name, [P, NT, HB])
                t["lasting"] = s["lasting"]
                with ExitStack() as part:
                    stage3(nc, part, io, t, s, ps)
                if upto >= 4:
                    with ExitStack() as part:
                        stage4(nc, part, io, t, s, ps)
        if upto >= 5:
            with ExitStack() as part:
                stage5(nc, part, io, out, t, s, ps)


def kernel(**inputs):
    import numpy as np
    import concourse.bacc as bacc
    from concourse.bass_utils import run_bass_kernel_spmd as run

    nc = bacc.Bacc("TRN2", target_bir_lowering=False, num_devices=1)
    arrays, io = {}, {}
    for name in INS:
        a = np.ascontiguousarray(inputs[name])
        arrays[f"in_{name}"] = a
        io[name] = nc.dram_tensor(f"in_{name}", a.shape, mybir.dt.from_np(a.dtype), kind="ExternalInput").ap()
    out = nc.dram_tensor("out", [N, D], F32, kind="ExternalOutput").ap()
    build(nc, io, out)
    return run(nc, [arrays], core_ids=[0]).results[0]["out"]
```

```python
from contextlib import ExitStack

import concourse.bass as bass
from concourse import mybir

F32 = mybir.dt.float32
BF16 = mybir.dt.bfloat16
I32 = mybir.dt.int32
U32 = mybir.dt.uint32
U8 = mybir.dt.uint8
ALU = mybir.AluOpType
ACT = mybir.ActivationFunctionType
AX = mybir.AxisListType

P = 128
N = 2048
D = 512
NT = N // P
KT = D // P
EPS = 1e-5

NREL = 1500
ET = -(-NREL // P)
NE = ET * P
E = 10000
EP = 125
EC = E // EP
PLANES = 3
HA = 8
DK = D // HA
CH = NE // 512
BIG = float(2.0 ** 100)
MID, HI, LO = 0, 1, 2
DIAG = 1e-7

HB = 16
DH = D // HB
DZ = DH + 1
GH = 2
NG = HB // GH
SLOPE = 0.2
SHIFT = 40.0


def make_constants(nc, t, s):
    with nc.Block() as block:
        @block.gpsimd
        def _(pool):
            pool.memset(t["ident"][:, :], 0.0).then_inc(s["zeroed"], 1)
            pool.memset(t["identb"][:, :], 0.0).then_inc(s["zeroed"], 1)
            pool.memset(t["offdiag"][:, :], 1.0).then_inc(s["zeroed"], 1)
            pool.wait_ge(s["zeroed"], 3)
            for m, fill in ((t["ident"], 1.0), (t["identb"], 1.0), (t["offdiag"], 0.0)):
                pool.affine_select(out=m[:, :], in_=m[:, :], compare_op=ALU.not_equal, fill=fill, base=0,
                                   pattern=[[-1, P]], channel_multiplier=1).then_inc(s["const"], 1)


class At:

    def __init__(self, pair, n):
        self.pair, self.n = pair, n

    def at(self, off=0):
        return 2 * self.pair + (self.n + off)

    def half(self, off=0):
        return self.pair + (self.n + off) // 2

    def par(self, off=0):
        return (self.n + off) % 2

    def rows(self, off=0):
        return bass.ds(self.at(off) * P, P)


class FirstLayer:

    def __init__(self, nc, c):
        sb = lambda name, shape, dt=F32: c.enter_context(nc.sbuf_tensor(f"f_{name}", shape, dt))
        sem = lambda name: c.enter_context(nc.semaphore(f"f_{name}"))
        self.keys = sb("keys", [P, 2, HA, NE], BF16)
        self.k1, self.k2 = self.keys[:, 0, :, :], self.keys[:, 1, :, :]
        self.qs = [sb(f"q{i}", [P, 3, HA, P], BF16) for i in range(2)]
        self.adjn = sb("adj", [P, 4, N], BF16)
        self.rel = [sb(f"rel{i}", [P, PLANES, NE], U8) for i in range(2)]
        self.scored = sb("scored", [P, NE], BF16)
        self.low = [sb(f"low{i}", [P, NE], BF16) for i in range(2)]
        self.minus_big = sb("minus_big", [P, 1])
        self.q_in, self.rel_in, self.adj_in = ([sem(f"{n}{i}") for i in range(2)] for n in ("q_in", "rel_in", "adj_in"))
        self.mask_step, self.marked, self.scored_ready, self.low_ready, self.adjn_ready = (
            sem("mask_step"), sem("marked"), sem("scored_ready"), sem("low"), sem("adjn"))
        self.big_set = sem("big_set")

    def load_queries(self, sp, t, it):
        q = it.par()
        for lo, kind, part in ((0, 0, HI), (DK, 0, HI), (0, 1, MID), (DK, 1, MID), (0, 2, HI), (DK, 2, LO)):
            sp.dma_start(self.qs[q][lo:lo + DK, kind, :, :], head_rows(t["q_parts"], part)[:, :, it.rows()]
                         ).then_inc(self.q_in[q], 16)

    def load_related(self, sp, t, it):
        for i in range(PLANES):
            sp.dma_start(self.rel[it.par()][:, i, :], t["rel_planes"][i][it.rows(), :]).then_inc(self.rel_in[it.par()], 16)

    def load_adj(self, pool, io, it):
        pool.dma_start(self.adjn[:, it.at() % 4, :], io["adj"][it.rows(), :]).then_inc(self.adj_in[it.par()], 16)

    def make_masks(self, pool, t, it, related=True):
        adjn, cols, rel = self.adjn, it.rows(), self.rel[it.par()]
        pool.wait_ge(self.adj_in[it.par()], 16 * (it.half() + 1))
        last = pool.tensor_tensor(adjn[:, it.at() % 4, cols], adjn[:, it.at() % 4, cols], t["offdiag"][:, :], ALU.mult)
        if not related:
            last.then_inc(self.adjn_ready, 1)
            return
        last.then_inc(self.mask_step, 1)
        pool.wait_ge(self.rel_in[it.par()], 16 * PLANES * (it.half() + 1))
        for i in range(1, PLANES):
            if i > 1:
                pool.wait_ge(self.mask_step, PLANES * it.at() + i)
            pool.tensor_tensor(rel[:, 0, :].bitcast(I32), rel[:, 0, :].bitcast(I32), rel[:, i, :].bitcast(I32),
                               ALU.add).then_inc(self.mask_step, 1)
        pool.wait_ge(self.marked, it.at(1))
        pool.tensor_tensor(self.scored[:, :], self.scored[:, :], adjn[:, it.at(4) % 4, 0:NE], ALU.mult
                           ).then_inc(self.scored_ready, 1)
        pool.wait_ge(self.scored_ready, it.at(1))
        pool.tensor_tensor(adjn[:, it.at(8) % 4, 0:NE], adjn[:, it.at(8) % 4, 0:NE], self.scored[:, :],
                           ALU.subtract).then_inc(self.adjn_ready, 1)

    def mark_related(self, dve, it, first=False):
        if not first:
            dve.wait_ge(self.adjn_ready, it.at())
            dve.wait_ge(self.low_ready, it.at())
        dve.wait_ge(self.mask_step, PLANES * it.at(1))
        dve.tensor_scalar(self.scored[:, :], self.rel[it.par()][:, 0, :], 0.0, None, ALU.not_equal).then_inc(self.marked, 1)

    def make_low(self, act, it):
        act.wait_ge(self.scored_ready, it.at(1))
        act.activation(self.low[it.par()][:, :], self.scored[:, :], ACT.Identity, bias=self.minus_big[:, 0:1],
                       scale=BIG).then_inc(self.low_ready, 1)


def head_rows(parts, n):
    return parts[n, :, :].rearrange("(h p) j -> p h j", p=DK)


def stage1(nc, c, io, t, s, ps, f):
    sb = lambda name, shape, dt=F32: c.enter_context(nc.sbuf_tensor(name, shape, dt))
    sem = lambda name: c.enter_context(nc.semaphore(name))
    wnat = [sb(f"s1_w{i}", [P, KT, D]) for i in range(2)]
    wT = [sb(f"s1_wT{i}", [P, KT, D]) for i in range(2)]
    bias = sb("s1_bias", [P, 2, KT])
    bias8 = sb("s1_bias8", [P, KT])
    hT = sb("s1_hT", [P, KT, NE])
    stats = sb("s1_stats", [P, NT, 6])
    mv = sb("s1_mv", [P, NT, 2])
    std = sb("s1_std", [P, NT])
    rstd = sb("s1_rstd", [P, NT])
    nmr = sb("s1_nmr", [P, NT])
    full = sb("s1_full", [P, 2, 512])
    parts = sb("s1_parts", [P, 2, 3, 512], BF16)
    zero = sb("s1_zero", [P, NE // 4], I32)
    ones = sb("s1_ones", [P, 1], U8)
    rel = sb("s1_rel", [P, EC, 2], I32)
    flat = sb("s1_flat", [P, EC], U32)
    h = t["h"]

    CX = 4
    x_in = [sem(f"s1_x_in{i}") for i in range(NT // CX)]
    w_in = [sem(f"s1_w_in{i}") for i in range(2)]
    bias_in, rel_in = sem("s1_bias_in"), sem("s1_rel_in")
    zero_set, flat_ready = sem("s1_zero_set"), sem("s1_flat")
    plane_zero = [sem(f"s1_plane_zero{i}") for i in range(PLANES)]
    related = [sem(f"s1_related{i}") for i in range(PLANES)]
    stat, var_ready, std_ready, rstd_ready, norm_ready, h_ready = (
        sem("s1_stat"), sem("s1_var"), sem("s1_std"), sem("s1_rstd"), sem("s1_norm"), sem("s1_h"))
    turned, copied = sem("s1_turned"), sem("s1_copied")
    bias_ready, proj, full_ready, split_step, parts_ready = (sem("s1_b8"), sem("s1_proj"), sem("s1_full"),
                                                             sem("s1_split"), sem("s1_parts"))
    parts_out = [sem(f"s1_parts_out{i}") for i in range(2)]
    Q, K = 0, 1
    turns = [("w", K, k) for k in range(KT)] + [("h", 0, i) for i in range(ET)] + [("w", Q, k) for k in range(KT)]
    groups = [(w, dt, ch) for w, ch in ((K, 0), (K, 1), (K, 2), (Q, 0), (Q, 1), (Q, 2)) for dt in range(KT)]
    G = len(groups)
    k_all, q_first = 3 * KT, 4 * KT

    def stored(g):
        keys = len(range(g % 2, min(g, k_all), 2))
        return 16 * (4 * keys + g // 2 - keys)

    plane_of = [e % PLANES for e in range(EC)]

    with nc.Block() as block:
        @block.sync
        def _(sp):
            def load_x(i):
                sp.dma_start(h[:, CX * i:CX * (i + 1), :], io["x"][CX * P * i:CX * P * (i + 1), :]
                             .rearrange("(t p) k -> p t k", p=P)).then_inc(x_in[i], 16)

            def load_w(i, name):
                sp.dma_start(wnat[i][:, :, :], io[name].rearrange("(t p) k -> p t k", p=P)).then_inc(w_in[i], 16)
            load_x(0)
            load_w(K, "L0_gnn_Wk")
            load_x(1)
            load_x(2)
            for i in range(PLANES):
                sp.wait_ge(plane_zero[i], 16)
            load_w(Q, "L0_gnn_Wq")
            load_x(3)
            for g, (w, dt, ch) in enumerate(groups):
                sp.wait_ge(parts_ready, g + 1)
                nodes = slice(ch * 512, (ch + 1) * 512)
                if w == K:
                    for hh in range(2):
                        for half, first_part in ((0, HI), (1, MID)):
                            sp.dma_start(f.keys[half * DK:(half + 1) * DK, :, 2 * dt + hh, nodes],
                                         parts[hh * DK:(hh + 1) * DK, g % 2, first_part:first_part + 2, :]
                                         ).then_inc(parts_out[g % 2], 16)
                    continue
                sp.dma_start(t["q_parts"][:, dt * P:(dt + 1) * P, nodes].rearrange("s p i -> p s i"),
                             parts[:, g % 2, :, :]).then_inc(parts_out[g % 2], 16)
                if g == q_first + 1:
                    for i in range(2):
                        sp.wait_ge(parts_out[i], stored(q_first + i))
                    f.load_queries(sp, t, At(0, 0))
            for i in range(PLANES):
                sp.wait_ge(related[i], 16 * plane_of.count(i))
            f.load_related(sp, t, At(0, 0))
            for i in range(2):
                sp.wait_ge(parts_out[i], stored(G + i))

        @block.gpsimd
        def _(pool):
            pool.dma_start(rel[0:EP, :, :], io["L0_gnn_rel_pair_index"].rearrange("(p c) s -> p c s", p=EP)).then_inc(rel_in, 16)
            pool.memset(zero[:, :], 0).then_inc(zero_set, 1)
            pool.memset(ones[:, :], 1).then_inc(zero_set, 1)
            pool.memset(f.minus_big[:, :], -BIG).then_inc(f.big_set, 1)
            for i, b in enumerate((io["L0_gnn_bq"], io["L0_gnn_bk"])):
                pool.dma_start(bias[:, i, :], b.rearrange("(t p) -> p t", p=P),
                               allow_slow_non_contiguous=True).then_inc(bias_in, 16)
            pool.wait_ge(zero_set, 2)
            pool.wait_ge(x_in[0], 16)
            for i in range(PLANES):
                pool.dma_start(t["rel_planes"][i].rearrange("(t p) j -> p t j", p=P),
                               zero[:, None, :].bitcast(U8).to_broadcast([P, ET, NE])).then_inc(plane_zero[i], 16)
            f.load_adj(pool, io, At(0, 0))
            pool.wait_ge(flat_ready, 1)
            for e, plane in enumerate(plane_of):
                n = plane_of[:e].count(plane)
                if n:
                    pool.wait_ge(related[plane], 16 * n)
                else:
                    pool.wait_ge(plane_zero[plane], 16)
                pool.indirect_dma_start(t["rel_planes"][plane].rearrange("i (j o) -> (i j) o", o=1),
                                        bass.IndirectOffsetOnAxis(ap=flat[0:EP, e:e + 1], axis=0),
                                        ones[0:EP, 0:1], None).then_inc(related[plane], 16)
            f.make_masks(pool, t, At(0, 0))

        @block.vector
        def _(dve):
            dve.wait_ge(rel_in, 16)
            dve.scalar_tensor_tensor(flat[0:EP, :], rel[0:EP, :, 0], float(NE), rel[0:EP, :, 1], ALU.mult,
                                     ALU.add).then_inc(flat_ready, 1)

            def norm(i):
                js = slice(CX * i, CX * (i + 1))
                dve.wait_ge(x_in[i], 16)
                for j in range(CX * i, CX * (i + 1)):
                    dve.bn_stats(stats[:, j, :], h[:, j, :]).then_inc(stat, 1)
                dve.wait_ge(stat, 2 * CX * i + CX)
                for j in range(CX * i, CX * (i + 1)):
                    dve.bn_aggr(mv[:, j, :], stats[:, j, :]).then_inc(stat, 1)
                dve.wait_ge(stat, 2 * CX * (i + 1))
                dve.tensor_scalar(rstd[:, js], mv[:, js, 1], EPS, None, ALU.add).then_inc(var_ready, 1)
                dve.wait_ge(std_ready, i + 1)
                dve.reciprocal(rstd[:, js], std[:, js]).then_inc(rstd_ready, 1)
                dve.wait_ge(rstd_ready, i + 1)
                dve.scalar_tensor_tensor(nmr[:, js], mv[:, js, 0], -1.0, rstd[:, js], ALU.mult, ALU.mult).then_inc(norm_ready, 1)

            def copy(lo, hi):
                for n in range(lo, hi):
                    kind, w, k = turns[n]
                    dve.wait_ge(turned, n + 1)
                    if kind == "w":
                        dve.tensor_copy(wT[w][:, k, :], ps[:, n % 4, :]).then_inc(copied, 1)
                    else:
                        dve.tensor_copy(hT[:, :, k * P:(k + 1) * P],
                                        ps[:, n % 4, :].rearrange("p (k i) -> p k i", k=KT)).then_inc(copied, 1)

            def split(lo, hi):
                for g in range(lo, hi):
                    v, q = full[:, g % 2, :], parts[:, g % 2, :, :]
                    dve.wait_ge(full_ready, g + 1)
                    if g >= 2:
                        dve.wait_ge(parts_out[g % 2], stored(g))
                    dve.tensor_copy(q[:, HI, :], v).then_inc(split_step, 1)
                    dve.wait_ge(split_step, 3 * g + 1)
                    dve.tensor_tensor(v, v, q[:, HI, :], ALU.subtract).then_inc(split_step, 1)
                    dve.wait_ge(split_step, 3 * g + 2)
                    dve.tensor_copy(q[:, MID, :], v).then_inc(split_step, 1)
                    dve.wait_ge(split_step, 3 * g + 3)
                    dve.tensor_tensor(q[:, LO, :], v, q[:, MID, :], ALU.subtract).then_inc(parts_ready, 1)
            norm(0)
            copy(0, 8)
            dve.wait_ge(bias_in, 32)
            dve.tensor_scalar(bias8[:, :], bias[:, 0, :], DK ** -0.5, None, ALU.mult).then_inc(bias_ready, 1)
            norm(1)
            norm(2)
            copy(8, 12)
            split(0, 4)
            copy(12, 16)
            split(4, 8)
            norm(3)
            copy(16, 20)
            split(8, G)
            f.mark_related(dve, At(0, 0), first=True)

        @block.scalar
        def _(act):
            def norm(i):
                js = slice(CX * i, CX * (i + 1))
                act.wait_ge(var_ready, i + 1)
                act.activation(std[:, js], rstd[:, js], ACT.Sqrt).then_inc(std_ready, 1)
                act.wait_ge(norm_ready, i + 1)
                for j in range(CX * i, CX * (i + 1)):
                    act.activation(h[:, j, :], h[:, j, :], ACT.Relu, bias=nmr[:, j:j + 1],
                                   scale=rstd[:, j:j + 1]).then_inc(h_ready, 1)

            def biased(lo, hi):
                for g in range(lo, hi):
                    w, dt, ch = groups[g]
                    act.wait_ge(proj, g + 1)
                    if g >= 2:
                        act.wait_ge(parts_ready, g - 1)
                    act.activation(full[:, g % 2, :], ps[:, 4 + g % 4, :], ACT.Identity,
                                   bias=bias8[:, dt:dt + 1] if w == Q else bias[:, 1, dt:dt + 1],
                                   scale=DK ** -0.5 if w == Q else 1.0).then_inc(full_ready, 1)
            for i in range(3):
                norm(i)
            act.wait_ge(bias_ready, 1)
            biased(0, 8)
            norm(3)
            biased(8, G)
            act.wait_ge(f.big_set, 1)
            f.make_low(act, At(0, 0))

        @block.tensor
        def _(pe):
            def turn(lo, hi):
                for n in range(lo, hi):
                    kind, w, k = turns[n]
                    if kind == "w":
                        pe.wait_ge(w_in[w], 16)
                    else:
                        pe.wait_ge(h_ready, k + 1)
                    if n >= 4:
                        pe.wait_ge(copied, n - 3)
                    for b in range(4):
                        src = wnat[w][:, b, k * P:(k + 1) * P] if kind == "w" else h[:, k, b * P:(b + 1) * P]
                        last = pe.transpose(ps[:, n % 4, b * P:(b + 1) * P], src, t["ident"][:, :])
                    last.then_inc(turned, 1)

            def project(lo, hi, needs):
                pe.wait_ge(copied, needs)
                for g in range(lo, hi):
                    w, dt, ch = groups[g]
                    if g >= 4:
                        pe.wait_ge(full_ready, g - 3)
                    for k in range(KT):
                        last = pe.matmul(ps[:, 4 + g % 4, :], wT[w][:, k, dt * P:(dt + 1) * P],
                                         hT[:, k, ch * 512:(ch + 1) * 512], start=(k == 0), stop=(k == KT - 1))
                    last.then_inc(proj, 1)
            pe.wait_ge(s["const"], 3)
            turn(0, 8)
            project(0, 4, 8)
            turn(8, 12)
            project(4, 8, 12)
            turn(12, 16)
            project(8, 12, 16)
            turn(16, 20)
            project(12, G, 20)


def stage2(nc, c, io, t, s, ps, f):
    sb = lambda name, shape, dt=F32: c.enter_context(nc.sbuf_tensor(name, shape, dt))
    sem = lambda name: c.enter_context(nc.semaphore(name))
    h = t["h"]
    qs, adjn, low = f.qs, f.adjn, f.low
    ex = sb("s2_exp", [P, HA, NE])
    W = [sb(f"s2_W{i}", [P, N]) for i in range(2)]
    WT = [sb(f"s2_WT{i}", [P, 2, P]) for i in range(2)]
    xt = [sb(f"s2_x{i}", [P, D]) for i in range(2)]
    junkv = sb("s2_junkv", [P, NE], BF16)
    negm = sb("s2_negm", [P, 2, HA])
    negd = sb("s2_negd", [P, HA])
    zs = sb("s2_zs", [P, 2, HA])
    n0 = sb("s2_n0", [P, 2])
    e0 = sb("s2_e0", [P, 3, HA])
    e1 = sb("s2_e1", [P, 3, HA])
    z = sb("s2_z", [P, HA])
    rz = sb("s2_rz", [P, HA])
    r8 = sb("s2_r8", [P, HA])
    re = sb("s2_re", [P, 2, HA])
    cd = sb("s2_cd", [P, 2])
    diag = sb("s2_diag", [P, 1])
    stats = sb("s2_stats", [P, 6])

    x_in = [sem(f"s2_x_in{i}") for i in range(2)]
    y_out = [sem(f"s2_y_out{i}") for i in range(2)]
    consts, consts_e = sem("s2_consts"), sem("s2_consts_e")
    scores, negmax, exped, rowsum, efac = sem("s2_scores"), sem("s2_negmax"), sem("s2_exped"), sem("s2_rowsum"), sem("s2_efac")
    fac, added, tail, w_ready = sem("s2_fac"), sem("s2_added"), sem("s2_tail"), sem("s2_w_ready")
    turned, turned_out, agg, summed = sem("s2_turned"), sem("s2_turned_out"), sem("s2_agg"), sem("s2_summed")
    measured, kept = sem("s2_measured"), sem("s2_kept")

    def steps(eng, step):
        for it in (-1, 0, 1):
            step(At(0, it), lambda off, lo, hi, it=it: lo <= it + off < hi)
        with eng.Fori(0, (ET - 4) // 2) as pair:
            for n in (2, 3):
                step(At(pair, n), lambda off, lo, hi: True)
        for it in range(ET - 2, NT + 1):
            step(At(0, it), lambda off, lo, hi, it=it: lo <= it + off < hi)

    with nc.Block() as block:
        @block.sync
        def _(sp):
            def step(it, has):
                if has(2, 0, ET):
                    if has(0, 0, ET):
                        sp.wait_ge(scores, HA * it.at(1))
                    f.load_queries(sp, t, At(it.pair, it.n + 2))
                    f.load_related(sp, t, At(it.pair, it.n + 2))
                if has(-1, 0, NT):
                    b = it.par(-1)
                    if it.n != 1:
                        sp.wait_ge(measured, it.at(-1))
                    sp.wait_ge(y_out[b], 16 * (it.half(-1) + 1))
                    sp.dma_start(xt[b][:, :], io["x"][it.rows(-1), :]).then_inc(x_in[b], 16)
                    sp.wait_ge(summed, it.at(0))
                    sp.dma_start(t["x1"][it.rows(-1), :], xt[b][:, :]).then_inc(y_out[b], 16)
            for i in range(2):
                sp.sem_inc(y_out[i], 16)
            sp.sem_inc(measured, 1)
            steps(sp, step)
            for i in range(2):
                sp.wait_ge(y_out[i], 16 * (NT // 2 + 1))

        @block.gpsimd
        def _(pool):
            pool.memset(negd[:, :], -DIAG).then_inc(consts, 1)
            pool.memset(diag[:, :], DIAG).then_inc(consts, 1)

            def step(it, has):
                if not has(2, 0, NT):
                    return
                if has(-2, 0, NT):
                    pool.wait_ge(w_ready, it.at(-1))
                f.load_adj(pool, io, At(it.pair, it.n + 2))
                f.make_masks(pool, t, At(it.pair, it.n + 2), related=has(2, 0, ET))
            steps(pool, step)

        @block.tensor
        def _(pe):
            def turn(it, m):
                n = HA * it.at(-1) + m
                if m == 0:
                    pe.wait_ge(w_ready, it.at(0))
                if not (it.n == 1 and m == 0):
                    pe.wait_ge(turned_out, n)
                for b in range(2):
                    last = pe.transpose(ps[:, 6, b * P:(b + 1) * P],
                                        W[it.par(-1)][:, (2 * m + b) * P:(2 * m + b + 1) * P], t["ident"][:, :])
                last.then_inc(turned, 1)

            def aggregate(it, m, has):
                if m == 0 and has(-2, 0, NT):
                    pe.wait_ge(summed, it.at(-1))
                pe.wait_ge(turned_out, HA * it.at(-1) + m + 1)
                for b in range(2):
                    last = pe.matmul(ps[:, 7, :], WT[m % 2][:, b, :], h[:, 2 * m + b, :],
                                     start=(m == 0 and b == 0), stop=(m == HA - 1 and b == 1))
                last.then_inc(agg, 1)

            def step(it, has):
                nxt, prev = has(1, 0, ET), has(-1, 0, NT)
                for hd in range(HA):
                    if nxt:
                        q = it.par(1)
                        if hd == 0:
                            pe.wait_ge(f.q_in[q], 96 * (it.half(1) + 1))
                            pe.wait_ge(f.low_ready, it.at(2))
                        if not (it.n == -1 and hd < 2):
                            pe.wait_ge(exped, HA * it.at(1) + hd - 1)
                        for ch in range(CH):
                            cols = slice(ch * 512, ch * 512 + 512)
                            out = ps[:, 3 * (hd % 2) + ch, :]
                            pe.matmul(out, qs[q][:, 0, hd, :], f.k1[:, hd, cols], start=True, stop=False)
                            pe.matmul(out, qs[q][:, 1, hd, :], f.k1[:, hd, cols], start=False, stop=False)
                            pe.matmul(out, qs[q][:, 2, hd, :], f.k2[:, hd, cols], start=False, stop=False)
                            last = pe.matmul(out, t["identb"][:, :], low[q][:, cols], start=False, stop=True)
                        last.then_inc(scores, 1)
                    if prev:
                        turn(it, hd)
                        if hd:
                            aggregate(it, hd - 1, has)
                if prev:
                    aggregate(it, HA - 1, has)
            steps(pe, step)

        @block.scalar
        def _(act):
            act.wait_ge(consts, 2)
            act.activation(e0[:, 2, :], negd[:, :], ACT.Exp).then_inc(consts_e, 1)
            act.activation(e1[:, 2, :], negd[:, :], ACT.Exp, bias=diag[:, 0:1]).then_inc(consts_e, 1)

            def step(it, has):
                nxt, prev, b = has(1, 0, ET), has(-1, 0, NT), it.par(1)
                if has(1, 0, NT):
                    act.wait_ge(f.adjn_ready, it.at(2))
                    if has(-1, 0, NT):
                        act.wait_ge(fac, 6 * it.at(0))
                    act.activation(adjn[:, it.at(1) % 4, :], adjn[:, it.at(1) % 4, :], ACT.Copy,
                                   accum_out=n0[:, b:b + 1]).then_inc(rowsum, 1)
                for hd in range(HA):
                    if hd == 6 and has(2, 0, ET):
                        if has(0, 0, ET):
                            act.wait_ge(scores, HA * it.at(1))
                        f.make_low(act, At(it.pair, it.n + 2))
                    if prev:
                        n = HA * it.at(-1) + hd
                        act.wait_ge(turned, n + 1)
                        if not (it.n == 1 and hd < 2):
                            act.wait_ge(agg, n - 1)
                        act.activation(WT[hd % 2][:, :, :],
                                       ps[:, 6, 0:2 * P].rearrange("p (b i) -> p b i", b=2),
                                       ACT.Copy).then_inc(turned_out, 1)
                    if nxt:
                        act.wait_ge(negmax, HA * it.at(1) + hd + 1)
                        if has(0, 0, ET):
                            act.wait_ge(added, HA * it.at(0) + hd + 1)
                        act.activation(ex[:, hd, :], ps[:, 3 * (hd % 2):3 * (hd % 2) + 3, :].rearrange("p c j -> p (c j)"),
                                       ACT.Exp, bias=negm[:, b, hd:hd + 1], accum_out=zs[:, b, hd:hd + 1]).then_inc(exped, 1)
                if nxt:
                    act.activation(e0[:, b, :], negm[:, b, :], ACT.Exp).then_inc(efac, 1)
                    act.activation(e1[:, b, :], negm[:, b, :], ACT.Exp, bias=diag[:, 0:1]).then_inc(efac, 1)
            steps(act, step)

        @block.vector
        def _(dve):
            dve.wait_ge(consts_e, 2)

            dve.sem_inc(kept, 1)

            def measure(it):
                dve.wait_ge(summed, it.at(1))
                dve.wait_ge(kept, it.at(1))
                dve.bn_stats(stats[:, :], xt[it.par()][:, :]).then_inc(measured, 1)
                dve.wait_ge(measured, it.at(2))
                dve.tensor_copy(t["stats"][:, it.at(), :], stats[:, :]).then_inc(kept, 1)

            def step(it, has):
                nxt, cur, related, prev = has(1, 0, ET), has(0, 0, NT), has(0, 0, ET), has(-1, 0, NT)
                b, bn = it.par(0), it.par(1)
                w = W[b]
                if cur:
                    links = 6 * it.at(0)
                    k = b if related else 2
                    dve.wait_ge(rowsum, it.at(1))
                    if related:
                        dve.wait_ge(exped, HA * it.at(1))
                        dve.wait_ge(efac, 2 * it.at(1))
                        dve.scalar_tensor_tensor(z[:, :], e0[:, k, :], n0[:, b:b + 1], zs[:, b, :], ALU.mult,
                                                 ALU.add).then_inc(fac, 1)
                        dve.wait_ge(fac, links + 1)
                        dve.tensor_tensor(z[:, :], z[:, :], e1[:, k, :], ALU.add).then_inc(fac, 1)
                    else:
                        dve.scalar_tensor_tensor(z[:, :], e0[:, k, :], n0[:, b:b + 1], e1[:, k, :], ALU.mult,
                                                 ALU.add).then_inc(fac, 2)
                    dve.wait_ge(fac, links + 2)
                    dve.reciprocal(rz[:, :], z[:, :]).then_inc(fac, 1)
                    dve.wait_ge(fac, links + 3)
                    dve.tensor_scalar(r8[:, :], rz[:, :], 1.0 / HA, None, ALU.mult).then_inc(fac, 1)
                    dve.scalar_tensor_tensor(re[:, 0, :], rz[:, :], 1.0 / HA, e0[:, k, :], ALU.mult, ALU.mult,
                                             accum_out=cd[:, 0:1]).then_inc(fac, 1)
                    dve.scalar_tensor_tensor(re[:, 1, :], rz[:, :], 1.0 / HA, e1[:, k, :], ALU.mult, ALU.mult,
                                             accum_out=cd[:, 1:2]).then_inc(fac, 1)
                    if has(-2, 0, NT):
                        dve.wait_ge(turned, HA * it.at(-1))
                    dve.wait_ge(fac, links + 6)
                for hd in range(HA):
                    if hd == 2 and has(-2, 0, NT):
                        measure(At(it.pair, it.n - 2))
                    if hd == 4 and has(2, 0, ET):
                        f.mark_related(dve, At(it.pair, it.n + 2))
                    if nxt:
                        dve.wait_ge(scores, HA * it.at(1) + hd + 1)
                        if not (it.n == -1 and hd == 0):
                            dve.wait_ge(negmax, HA * it.at(1) + hd)
                        dve.tensor_scalar(junkv[:, :], ps[:, 3 * (hd % 2):3 * (hd % 2) + 3, :].rearrange("p c j -> p (c j)"),
                                          -1.0, -DIAG, ALU.mult, ALU.min,
                                          accum_out=negm[:, bn, hd:hd + 1]).then_inc(negmax, 1)
                    if related:
                        if hd == 0:
                            dve.tensor_scalar(w[:, 0:NE], ex[:, 0, :], r8[:, 0:1], None, ALU.mult).then_inc(added, 1)
                        else:
                            dve.wait_ge(added, HA * it.at(0) + hd)
                            dve.scalar_tensor_tensor(w[:, 0:NE], ex[:, hd, :], r8[:, hd:hd + 1], w[:, 0:NE], ALU.mult,
                                                     ALU.add).then_inc(added, 1)
                if cur:
                    nbr = adjn[:, it.at(0) % 4, :]
                    if related:
                        dve.wait_ge(added, HA * it.at(1))
                        dve.scalar_tensor_tensor(w[:, 0:NE], adjn[:, it.at(0) % 4, 0:NE], cd[:, 0:1], w[:, 0:NE], ALU.mult,
                                                 ALU.add).then_inc(tail, 1)
                        dve.tensor_scalar(w[:, NE:N], adjn[:, it.at(0) % 4, NE:N], cd[:, 0:1], None, ALU.mult).then_inc(tail, 1)
                    else:
                        dve.tensor_scalar(w[:, :], nbr, cd[:, 0:1], None, ALU.mult).then_inc(tail, 2)
                    dve.wait_ge(tail, 2 * it.at(1))
                    dve.scalar_tensor_tensor(w[:, it.rows()], t["ident"][:, :], cd[:, 1:2], w[:, it.rows()], ALU.mult,
                                             ALU.add).then_inc(w_ready, 1)
                if prev:
                    p = it.par(-1)
                    dve.wait_ge(agg, HA * it.at(0))
                    dve.wait_ge(x_in[p], 16 * (it.half(-1) + 1))
                    dve.tensor_tensor(xt[p][:, :], xt[p][:, :], ps[:, 7, :], ALU.add).then_inc(summed, 1)
            steps(dve, step)
            measure(At(0, NT - 1))


def stage3(nc, c, io, t, s, ps):
    sb = lambda name, shape, dt=F32: c.enter_context(nc.sbuf_tensor(name, shape, dt))
    sem = lambda name: c.enter_context(nc.semaphore(name))
    seq, adjT = t["seq"], t["adjT"]
    xs = sb("s3_x", [P, NT, D])
    wseq = sb("s3_w", [P, KT, D])
    mv = sb("s3_mv", [P, NT, 2])
    std = sb("s3_std", [P, NT])
    rstd = sb("s3_rstd", [P, NT])
    nmr = sb("s3_nmr", [P, NT])
    hb = [sb(f"s3_h{i}", [P, D]) for i in range(2)]
    hT = [sb(f"s3_hT{i}", [P, KT, P]) for i in range(2)]
    a12 = sb("s3_a", [P, 2, DH])
    prod = [sb(f"s3_prod{i}", [P, 2, D]) for i in range(2)]
    adjb = [sb(f"s3_adj{i}", [P, N], BF16) for i in range(2)]
    sc = sb("s3_sc", [P, 2, HB, NT])
    top = sb("s3_top", [P, HB])
    topa = sb("s3_topa", [P, HB])
    d = sb("s3_d", [P, HB, NT])
    u = sb("s3_u", [P, HB, NT])
    m = sb("s3_m", [P, HB, NT])
    shift = sb("s3_shift", [P, 1])
    s1T = sb("s3_s1T", [P, 2, P])

    chunks = ((0, 2), (2, 4), (4, 8), (8, 12), (12, NT))
    x_in = [sem(f"s3_x_in{i}") for i in range(len(chunks))]
    w_in, a_in = sem("s3_w_in"), sem("s3_a_in")
    adj_in = [sem(f"s3_adj_in{i}") for i in range(2)]
    consts, stat, var_ready, std_ready, norm_ready = (sem("s3_consts"), sem("s3_stat"), sem("s3_var"), sem("s3_std"),
                                                      sem("s3_norm"))
    h_ready, h_turned, hT_ready, adj_turned, adj_out_a, adj_out_v, seq_psum, seq_ready, prods, scored = (
        sem("s3_h"), sem("s3_h_turned"), sem("s3_hT"), sem("s3_adj_turned"), sem("s3_adj_out_a"), sem("s3_adj_out_v"),
        sem("s3_seq_psum"), sem("s3_seq"), sem("s3_prods"), sem("s3_scored"))
    topped, top_all, chain, expd, sT_psum, sT_ready, rows_out = (sem("s3_topped"), sem("s3_top_all"), sem("s3_chain"),
                                                                sem("s3_expd"), sem("s3_sT_psum"), sem("s3_sT"),
                                                                sem("s3_rows_out"))

    def steps(eng, step):
        for it in (0, 1):
            step(At(0, it), True)
        with eng.Fori(0, (NT - 2) // 2) as pair:
            for n in (2, 3):
                step(At(pair, n), False)

    with nc.Block() as block:
        @block.sync
        def _(sp):
            for i, (lo, hi) in enumerate(chunks):
                if i == 1:
                    sp.wait_ge(w_in, 16)
                sp.dma_start(xs[:, lo:hi, :], t["x1"][lo * P:hi * P, :].rearrange("(t p) k -> p t k", p=P)).then_inc(x_in[i], 16)
                if i == 0:
                    sp.dma_start(wseq[:, :, :], io["L1_gnn_W_seq"].rearrange("(t p) n -> p t n", p=P)).then_inc(w_in, 16)
                    for k, a in enumerate((io["L1_gnn_a1"], io["L1_gnn_a2"])):
                        sp.dma_start(a12[:, k, :], a.rearrange("(o d) -> o d", o=1).to_broadcast([P, DH])).then_inc(a_in, 16)
            sp.wait_ge(sT_ready, 2)
            for g in range(2):
                sp.dma_start(t["s1_rows"].rearrange("h (t i) -> (h t) i", i=P)[g * P:(g + 1) * P, :],
                             s1T[:, g, :]).then_inc(rows_out, 16)
            sp.wait_ge(rows_out, 32)

        @block.gpsimd
        def _(pool):
            pool.memset(shift[:, :], SHIFT).then_inc(consts, 1)
            for i in range(2):
                pool.wait_ge(*((x_in[0], 16), (w_in, 16))[i])
                pool.dma_start(adjb[i][:, :], io["adj"][i * P:(i + 1) * P, :]).then_inc(adj_in[i], 16)

            def load_adj(it):
                pool.wait_ge(adj_turned, 2 * it.at(-1))
                pool.dma_start(adjb[it.par()][:, :], io["adj"][it.rows(), :]).then_inc(adj_in[it.par()], 16)

            def products(it, first=False):
                b = it.par()
                pool.wait_ge(seq_ready, it.at(1))
                if not first:
                    pool.wait_ge(scored, 2 * it.at(-1))
                for i in range(2):
                    pool.tensor_tensor(prod[b][:, i, :].rearrange("p (h d) -> p h d", h=HB),
                                       seq[:, it.at(), :].rearrange("p (h d) -> p h d", h=HB),
                                       a12[:, i, None, :].to_broadcast([P, HB, DH]), ALU.mult).then_inc(prods, 1)
            pool.wait_ge(a_in, 32)
            for it in (0, 1):
                load_adj(At(0, it + 2))
                products(At(0, it), True)
            with pool.Fori(0, (NT - 4) // 2) as pair:
                for n in (2, 3):
                    load_adj(At(pair, n + 2))
                    products(At(pair, n))
            for it in (NT - 2, NT - 1):
                products(At(0, it))
            pool.wait_ge(topped, 1)
            pool.partition_all_reduce(topa[:, :], top[:, :], P, bass.bass_isa.ReduceOp.max).then_inc(top_all, 1)

        @block.vector
        def _(dve):
            for i in range(NT):
                dve.bn_aggr(mv[:, i, :], t["stats"][:, i, :]).then_inc(stat, 1)
            dve.wait_ge(stat, NT)
            dve.tensor_scalar(rstd[:, :], mv[:, :, 1], EPS, None, ALU.add).then_inc(var_ready, 1)
            dve.wait_ge(std_ready, 1)
            dve.reciprocal(rstd[:, :], std[:, :]).then_inc(var_ready, 1)
            dve.wait_ge(var_ready, 2)
            dve.scalar_tensor_tensor(nmr[:, :], mv[:, :, 0], -1.0, rstd[:, :], ALU.mult, ALU.mult).then_inc(norm_ready, 1)

            def turned_h(it, first=False):
                b = it.par()
                dve.wait_ge(h_turned, it.at(1))
                if not first:
                    dve.wait_ge(seq_psum, it.at(-1))
                dve.tensor_copy(hT[b][:, :, :], ps[:, b, :].rearrange("p (k i) -> p k i", k=KT)).then_inc(hT_ready, 1)

            def turned_adj(it):
                dve.wait_ge(adj_turned, 2 * it.at() + 2)
                dve.tensor_copy(adjT[:, 8:16, it.rows()],
                                ps[:, 3, :].bitcast(BF16).rearrange("p (j i) -> p j i", j=8)).then_inc(adj_out_v, 1)

            def score(it):
                for i in range(2):
                    dve.wait_ge(prods, 2 * it.at() + i + 1)
                    dve.reduce_sum(sc[:, i, :, it.at()], prod[it.par()][:, i, :].rearrange("p (h d) -> p h d", h=HB),
                                   AX.X).then_inc(scored, 1)
            turned_h(At(0, 0), True)
            turned_h(At(0, 1), True)
            turned_adj(At(0, 0))
            with dve.Fori(0, (NT - 2) // 2) as pair:
                for n in (2, 3):
                    turned_h(At(pair, n))
                    turned_adj(At(pair, n - 1))
                    score(At(pair, n - 2))
            score(At(0, NT - 2))
            turned_adj(At(0, NT - 1))
            score(At(0, NT - 1))

            steps_done = [0]

            def link(ins):
                steps_done[0] += 1
                ins.then_inc(chain, 1)
                dve.wait_ge(chain, steps_done[0])
            dve.wait_ge(scored, 2 * NT)
            s1, s2 = sc[:, 0, :, :], sc[:, 1, :, :]
            dve.reduce_max(top[:, :], s2, AX.X).then_inc(topped, 1)
            dve.tensor_scalar(t["ns2"][:, :, :], s2, -1.0, None, ALU.mult)\
                .then_inc(t["lasting"], 1)
            for g in range(2):
                dve.wait_ge(sT_psum, g + 1)
                dve.tensor_copy(s1T[:, g, :], ps[:, 6, g * P:(g + 1) * P]).then_inc(sT_ready, 1)
            dve.wait_ge(top_all, 1)
            tops = topa[:, :, None].to_broadcast([P, HB, NT])
            link(dve.tensor_tensor(d[:, :, :], s2, tops, ALU.subtract))
            link(dve.tensor_tensor(u[:, :, :], s1, tops, ALU.add))
            link(dve.scalar_tensor_tensor(m[:, :, :], u[:, :, :], SLOPE, u[:, :, :], ALU.mult, ALU.max))
            link(dve.scalar_tensor_tensor(t["wb"][:, :, :], u[:, :, :], SLOPE, m[:, :, :], ALU.mult, ALU.subtract))
            link(dve.tensor_tensor(t["wa"][:, :, :], u[:, :, :], m[:, :, :], ALU.subtract))

        @block.scalar
        def _(act):
            act.wait_ge(var_ready, 1)
            act.activation(std[:, :], rstd[:, :], ACT.Sqrt).then_inc(std_ready, 1)
            act.wait_ge(norm_ready, 1)

            def relu(it, first):
                if not first:
                    act.wait_ge(h_turned, it.at(-1))
                act.activation(hb[it.par()][:, :], xs[:, it.at(), :], ACT.Relu, bias=nmr[:, bass.ds(it.at(), 1)],
                               scale=rstd[:, bass.ds(it.at(), 1)]).then_inc(h_ready, 1)

            def turned_adj(it):
                act.wait_ge(adj_turned, 2 * it.at() + 1)
                act.activation(adjT[:, 0:8, it.rows()], ps[:, 2, :].bitcast(BF16).rearrange("p (j i) -> p j i", j=8),
                               ACT.Copy).then_inc(adj_out_a, 1)

            def projected(it):
                act.wait_ge(seq_psum, it.at(1))
                act.activation(seq[:, it.at(), :], ps[:, 4 + it.par(), :], ACT.Copy).then_inc(seq_ready, 1)
            act.wait_ge(x_in[0], 16)
            relu(At(0, 0), True)
            relu(At(0, 1), True)
            for i, (lo, hi) in list(enumerate(chunks))[1:]:
                act.wait_ge(x_in[i], 16)
                with act.Fori(lo // 2 - 1, hi // 2 - 1) as pair:
                    for n in (0, 1):
                        relu(At(pair, n + 2), False)
                        projected(At(pair, n))
                        turned_adj(At(pair, n))
            for it in (NT - 2, NT - 1):
                projected(At(0, it))
                turned_adj(At(0, it))
            act.wait_ge(consts, 1)
            act.wait_ge(chain, 1)
            act.activation(t["ea"][:, :, :].rearrange("p t h -> p h t"), d[:, :, :], ACT.Exp, bias=shift[:, 0:1]).then_inc(expd, 1)
            act.activation(t["eb"][:, :, :].rearrange("p t h -> p h t"), d[:, :, :], ACT.Exp, bias=shift[:, 0:1],
                           scale=SLOPE).then_inc(expd, 1)
            act.wait_ge(chain, 5)
            for w in ("wa", "wb"):
                act.activation(t[w][:, :, :], t[w][:, :, :], ACT.Exp).then_inc(expd, 1)

        @block.tensor
        def _(pe):
            def turn(it, first):
                b = it.par()
                pe.wait_ge(h_ready, it.at(1))
                if not first:
                    pe.wait_ge(hT_ready, it.at(-1))
                for k in range(KT):
                    last = pe.transpose(ps[:, b, k * P:(k + 1) * P], hb[b][:, k * P:(k + 1) * P], t["ident"][:, :])
                last.then_inc(h_turned, 1)

            def step(it, first, last_tile=False):
                b = it.par()
                if not last_tile:
                    turn(At(it.pair, it.n + 1), first and b == 0)
                if first and b == 0:
                    pe.wait_ge(w_in, 16)
                pe.wait_ge(hT_ready, it.at(1))
                if not first:
                    pe.wait_ge(seq_ready, it.at(-1))
                for k in range(KT):
                    last = pe.matmul(ps[:, 4 + b, :], hT[b][:, k, :], wseq[:, k, :], start=(k == 0), stop=(k == KT - 1))
                last.then_inc(seq_psum, 1)
                pe.wait_ge(adj_in[b], 16 * (it.half() + 1))
                for half, out in ((0, adj_out_a), (1, adj_out_v)):
                    if not (first and b == 0):
                        pe.wait_ge(out, it.at())
                    for j in range(8):
                        last = pe.transpose(ps[:, 2 + half, :].bitcast(BF16)[:, j * P:(j + 1) * P],
                                            adjb[b][:, (8 * half + j) * P:(8 * half + j + 1) * P], t["identb"][:, :])
                    last.then_inc(adj_turned, 1)
            turn(At(0, 0), True)
            step(At(0, 0), True)
            step(At(0, 1), True)
            with pe.Fori(0, (NT - 4) // 2) as pair:
                for n in (2, 3):
                    step(At(pair, n), False)
            step(At(0, NT - 2), False)
            step(At(0, NT - 1), False, last_tile=True)
            pe.wait_ge(scored, 2 * NT)
            for g in range(2):
                if g:
                    pe.wait_ge(sT_ready, g)
                pe.transpose(ps[:, 6, g * P:(g + 1) * P],
                             sc[:, 0, 8 * g:8 * g + 8, :].rearrange("p h t -> p (h t)"), t["ident"][:, :]).then_inc(sT_psum, 1)


RING = 16
HALF = N // 2
HT = HALF // P
VECTOR_ONLY = (5, 11)
NS = NT - len(VECTOR_ONLY)
UG = 2 * GH
VB = NT // UG
AT = NT // UG
HEAD_START = 6
BANK_START = 2


def stage4(nc, c, io, t, s, ps):
    sb = lambda name, shape, dt=F32: c.enter_context(nc.sbuf_tensor(f"s4_{name}", shape, dt))
    sem = lambda name: c.enter_context(nc.semaphore(f"s4_{name}"))
    seq, adjT = t["seq"], t["adjT"]
    GZ = GH * DZ
    V = sb("V", [P, 3, NT, 3, 2, GZ], BF16)
    A2 = sb("A2", [P, 3, NT, GZ])
    masks = sb("masks", [P, RING, HALF], BF16)
    s1b = [sb(f"s1b{i}", [P, HALF]) for i in range(2)]
    bs2 = [sb(f"bs2{i}", [P, NT]) for i in range(2)]
    tmp = [sb(f"tmp{i}", [P, VB, 2, GZ]) for i in range(2)]
    sums = [sb(f"sums{i}", [P, HT, 2, DZ]) for i in range(2)]
    hid = [sb(f"hid{i}", [P, HT, DZ]) for i in range(2)]

    value, hi_out, rest, mid_out, split = sem("value"), sem("hi"), sem("rest"), sem("mid"), sem("split")
    near_psum, near_out = sem("near_psum"), sem("near_out")
    s1_in = [sem(f"s1_in{i}") for i in range(2)]
    hid_out = [sem(f"hid_out{i}") for i in range(2)]
    bs2_ready, signs, mask_ready, mask_used = sem("bs2_ready"), sem("signs"), sem("mask"), sem("mask_used")
    bank_free, summed, sums_free, comb, hid_ready = (sem("bank_free"), sem("summed"), sem("sums_free"), sem("comb"),
                                                     sem("hid"))

    with nc.Block() as block:
        @block.sync
        def _(sp):
            def load(k, half):
                sp.dma_start(s1b[half][:, :],
                             t["s1_rows"][bass.ds(k, 1), half * HALF:(half + 1) * HALF].to_broadcast([P, HALF])
                             ).then_inc(s1_in[half], 16)

            def store(k, half):
                sp.wait_ge(hid_ready, 2 * k + half + 1)
                sp.dma_start(t["hidden"][half * HALF:(half + 1) * HALF, k, :].rearrange("(t p) d -> p t d", p=P),
                             hid[half][:, :, :]).then_inc(hid_out[half], 16)
            load(0, 0)
            load(0, 1)
            with sp.Fori(0, HB - 1) as k:
                for half in range(2):
                    sp.wait_ge(mask_ready, NT * (2 * k + half + 1))
                    load(k + 1, half)
                    if half:
                        store(k, 0)
                store(k, 1)
            for half in range(2):
                store(HB - 1, half)
            for half in range(2):
                sp.wait_ge(hid_out[half], 16 * (HB + 1))

        @block.gpsimd
        def _(pool):
            for half in range(2):
                pool.sem_inc(hid_out[half], 16)
            pool.sem_inc(sums_free, 2)

            def values(g, u, first=False):
                b, n = u % 2, UG * g + u
                js = slice(VB * u, VB * u + VB)
                if not first:
                    pool.wait_ge(split, n - 1)
                for k, e in enumerate((t["ea"], t["eb"])):
                    out = tmp[b][:, :, k, :].rearrange("p j (h z) -> p j h z", h=GH)
                    pool.tensor_tensor(out[:, :, :, 0:DH],
                                       seq[:, js, bass.ds(g * GH * DH, GH * DH)].rearrange("p j (h d) -> p j h d", h=GH),
                                       e[:, js, bass.ds(g * GH, GH), None].to_broadcast([P, VB, GH, DH]),
                                       ALU.mult).then_inc(value, 1)
                    pool.tensor_copy(out[:, :, :, DH], e[:, js, bass.ds(g * GH, GH)]).then_inc(value, 1)

            def combine(g, u):
                n, hh, half = UG * g + u, u // 2, u % 2
                q, out, rows = sums[half], hid[half], slice(half * HT, (half + 1) * HT)
                wa, wb = (t[w][:, GH * g + hh, rows].rearrange("p (t o) -> p t o", o=1).to_broadcast([P, HT, DZ])
                          for w in ("wa", "wb"))
                pool.wait_ge(summed, n + 1)
                pool.wait_ge(hid_out[half], 16 * (GH * g + hh + 1))
                pool.tensor_tensor(out[:, :, :], A2[:, g % 3, rows, hh * DZ:(hh + 1) * DZ], q[:, :, 1, :],
                                   ALU.subtract).then_inc(comb, 1)
                pool.tensor_tensor(q[:, :, 0, :], q[:, :, 0, :], wa, ALU.mult).then_inc(comb, 1)
                pool.wait_ge(comb, 3 * n + 1)
                pool.tensor_tensor(out[:, :, :], out[:, :, :], wb, ALU.mult).then_inc(comb, 1)
                pool.wait_ge(comb, 3 * n + 3)
                pool.tensor_tensor(out[:, :, :], out[:, :, :], q[:, :, 0, :], ALU.add).then_inc(hid_ready, 1)
                pool.wait_ge(hid_ready, n + 1)
                pool.sem_inc(sums_free, 1)
            for n in range(2 * UG):
                values(n // UG, n % UG, first=n < 2)
            with pool.Fori(0, NG - 2) as g:
                for u in range(UG):
                    values(g + 2, u)
                    combine(g, u)
            for g in (NG - 2, NG - 1):
                for u in range(UG):
                    combine(g, u)

        @block.scalar
        def _(act):
            def part(g, u, p):
                n = UG * g + u
                act.wait_ge(*((value, 4 * (n + 1)) if p == 0 else (rest, n + 1)))
                act.activation(V[:, g % 3, VB * u:VB * u + VB, p, :, :], tmp[u % 2][:, :, :, :],
                               ACT.Copy).then_inc(hi_out if p == 0 else mid_out, 1)

            def unit(g, u, build=True):
                n, half = UG * g + u, u % 2
                act.wait_ge(s1_in[half], 16 * (GH * g + u // 2 + 1))
                act.wait_ge(bs2_ready, n + 1)
                for j in range(NT):
                    if j not in VECTOR_ONLY:
                        act.wait_ge(mask_used, NT * n + j + 1)
                        act.activation(masks[:, j % RING, :], s1b[half][:, :], ACT.Relu,
                                       bias=bs2[half][:, j:j + 1], scale=BIG).then_inc(signs, 1)
                    if build and j == 13:
                        part(g + 2, u, 0)
                if build:
                    part(g + 2, u, 1)
            for n in range(2 * UG):
                part(n // UG, n % UG, 0)
                part(n // UG, n % UG, 1)
            with act.Fori(0, NG - 2) as g:
                for u in range(UG):
                    unit(g, u)
            for g in (NG - 2, NG - 1):
                for u in range(UG):
                    unit(g, u, build=False)

        @block.vector
        def _(dve):
            dve.sem_inc(bank_free, 1)

            def take_off(g, u, p):
                n = UG * g + u
                dve.wait_ge(hi_out if p == 0 else mid_out, n + 1)
                left = tmp[u % 2][:, :, :, :].rearrange("p j k c -> p j (k c)")
                js = slice(VB * u, VB * u + VB)
                out = left if p == 0 else V[:, g % 3, js, 2, :, :].rearrange("p j k c -> p j (k c)")
                dve.tensor_tensor(out, left, V[:, g % 3, js, p, :, :].rearrange("p j k c -> p j (k c)"),
                                  ALU.subtract).then_inc(rest if p == 0 else split, 1)

            def scaled_scores(g, u):
                n = UG * g + u
                head = GH * g + u // 2
                if not isinstance(n, int) or n:
                    dve.wait_ge(signs, NS * (n - 1) + 1)
                dve.tensor_scalar(bs2[u % 2][:, :], t["ns2"][:, head, :], -BIG, None, ALU.mult).then_inc(bs2_ready, 1)

            def mask(g, u, j):
                n, half = UG * g + u, u % 2
                out, near = masks[:, j % RING, :], adjT[:, j, half * HALF:(half + 1) * HALF]
                if j in VECTOR_ONLY:
                    dve.wait_ge(mask_used, NT * n + j + 1)
                    dve.wait_ge(s1_in[half], 16 * (GH * g + u // 2 + 1))
                    dve.scalar_tensor_tensor(out, s1b[half][:, :], t["ns2"][:, GH * g + u // 2, j:j + 1], near,
                                             ALU.is_gt, ALU.mult).then_inc(mask_ready, 1)
                else:
                    before = sum(x not in VECTOR_ONLY for x in range(j))
                    dve.wait_ge(signs, NS * n + before + 1)
                    dve.tensor_tensor(out, out, near, ALU.min).then_inc(mask_ready, 1)

            def mask_sums(g, u):
                n = UG * g + u
                dve.wait_ge(mask_used, RING + NT * (n + 1))
                dve.wait_ge(sums_free, n + 1)
                dve.reduce_sum(sums[u % 2][:, :, :, :].rearrange("p t k d -> p t (k d)"),
                               ps[:, 0:4, :].rearrange("p b (u c) -> p (b u) c", u=2)[:, :, 0:6 * DZ]
                               .rearrange("p t (s c) -> p t c s", s=3), AX.X).then_inc(summed, 1)
                dve.wait_ge(summed, n + 1)
                dve.sem_inc(bank_free, 1)

            def near_sums(g, u):
                n = UG * g + u
                dve.wait_ge(near_psum, n + 1)
                b = 4 + 2 * (u % 2)
                dve.reduce_sum(A2[:, g % 3, AT * u:AT * u + AT, :],
                               ps[:, b:b + 2, :].rearrange("p b (u c) -> p (b u) c", u=2)[:, :, 0:3 * GZ]
                               .rearrange("p t (s c) -> p t c s", s=3), AX.X).then_inc(near_out, 1)

            def unit(g, u, build=True, ahead=True, last=False):
                nxt = (g, u + 1) if u + 1 < UG else (g + 1, 0)
                for j in range(HEAD_START, NT):
                    if j == HEAD_START + 1 and not last:
                        scaled_scores(*nxt)
                    if build and j == 10:
                        take_off(g + 2, u, 0)
                    if build and j == 14:
                        take_off(g + 2, u, 1)
                    mask(g, u, j)
                if not last:
                    for j in range(BANK_START):
                        mask(*nxt, j)
                mask_sums(g, u)
                if not last:
                    for j in range(BANK_START, HEAD_START):
                        mask(*nxt, j)
                if ahead:
                    near_sums(g + 1, u)
            for n in range(2 * UG):
                for p in range(2):
                    take_off(n // UG, n % UG, p)
                if n == 0:
                    scaled_scores(0, 0)
                if n == UG + 1:
                    near_sums(0, 0)
            near_sums(0, 1)
            for j in range(HEAD_START):
                mask(0, 0, j)
                if j in (1, 4):
                    near_sums(0, 2 + j // 4)
            with dve.Fori(0, NG - 2) as g:
                for u in range(UG):
                    unit(g, u)
            for u in range(UG):
                unit(NG - 2, u, build=False)
            for u in range(UG):
                unit(NG - 1, u, build=False, ahead=False, last=u == UG - 1)

        @block.tensor
        def _(pe):
            pe.sem_inc(mask_used, RING)

            def near(g, u, first=False):
                n, b = UG * g + u, 4 + 2 * (u % 2)
                if not first:
                    pe.wait_ge(near_out, n - 1)
                for j in range(NT):
                    if j % VB == 0 and first:
                        pe.wait_ge(split, UG * g + j // VB + 1)
                    elif j == 0:
                        pe.wait_ge(split, UG * (g + 1))
                    for i in range(AT):
                        it = AT * u + i
                        last = pe.matmul(ps[:, b + i // 2, 256 * (i % 2):256 * (i % 2) + 3 * GZ]
                                         .rearrange("p (s c) -> p s c", s=3),
                                         adjT[:, j, it * P:(it + 1) * P], V[:, g % 3, j, :, 1, :],
                                         start=(j == 0 and i % 2 == 0), stop=(j == NT - 1), skip_group_check=True)
                last.then_inc(near_psum, 1)

            def unit(g, u, ahead=True):
                n = UG * g + u
                hh = u // 2
                pe.wait_ge(bank_free, n + 1)
                for j in range(NT):
                    pe.wait_ge(mask_ready, NT * n + j + 1)
                    for i in range(HT):
                        last = pe.matmul(ps[:, i // 2, 256 * (i % 2):256 * (i % 2) + 6 * DZ]
                                         .rearrange("p (s d) -> p s d", s=6),
                                         masks[:, j % RING, i * P:(i + 1) * P],
                                         V[:, g % 3, j, :, :, hh * DZ:(hh + 1) * DZ].rearrange("p s k d -> p (s k) d"),
                                         start=(j == 0 and i % 2 == 0), stop=(j == NT - 1), skip_group_check=True)
                    last.then_inc(mask_used, 1)
                if ahead:
                    near(g + 1, u)
            for u in range(UG):
                near(0, u, first=u < 2)
            with pe.Fori(0, NG - 1) as g:
                for u in range(UG):
                    unit(g, u)
            for u in range(UG):
                unit(NG - 1, u, ahead=False)


def stage5(nc, c, io, out, t, s, ps):
    sb = lambda name, shape, dt=F32: c.enter_context(nc.sbuf_tensor(name, shape, dt))
    sem = lambda name: c.enter_context(nc.semaphore(name))
    wout = sb("s5_w", [P, KT, D])
    bout = sb("s5_b", [P, D])
    hid = sb("s5_hid", [P, NT, HB, DZ])
    x1 = sb("s5_x", [P, NT, D])
    rz = [sb(f"s5_rz{i}", [P, HB]) for i in range(2)]
    hn = [sb(f"s5_hn{i}", [P, D]) for i in range(2)]
    hT = [sb(f"s5_hT{i}", [P, KT, P]) for i in range(2)]
    v = [sb(f"s5_v{i}", [P, D]) for i in range(2)]
    e = [sb(f"s5_e{i}", [P, D]) for i in range(2)]
    w_in = sem("s5_w_in")
    chunks = ((0, 2), (2, 4), (4, 8), (8, 12), (12, NT))
    hid_in = [sem(f"s5_hid_in{i}") for i in range(len(chunks))]
    x_in = [sem(f"s5_x_in{i}") for i in range(len(chunks))]
    y_out = sem("s5_y_out")
    inv, normed, turned, turned_out, proj, biased, low, expd, added, done = (
        sem("s5_inv"), sem("s5_normed"), sem("s5_turned"), sem("s5_turned_out"), sem("s5_proj"), sem("s5_biased"),
        sem("s5_low"), sem("s5_expd"), sem("s5_added"), sem("s5_done"))

    with nc.Block() as block:
        @block.sync
        def _(sp):
            for i, (lo, hi) in enumerate(chunks):
                ts, rows = slice(lo, hi), slice(P * lo, P * hi)
                if i == 1:
                    sp.wait_ge(w_in, 32)
                sp.dma_start(hid[:, ts, :, :], t["hidden"][rows, :, :].rearrange("(t p) h d -> p t h d", p=P)).then_inc(hid_in[i], 16)
                if i == 0:
                    sp.dma_start(wout[:, :, :], io["L1_gnn_W_out"].rearrange("(t p) n -> p t n", p=P)).then_inc(w_in, 16)
                    sp.dma_start(bout[:, :], io["L1_gnn_b_out"].rearrange("(o d) -> o d", o=1).to_broadcast([P, D])
                                 ).then_inc(w_in, 16)
                sp.dma_start(x1[:, ts, :], t["x1"][rows, :].rearrange("(t p) d -> p t d", p=P)).then_inc(x_in[i], 16)

        @block.vector
        def _(dve):
            def norm(it, first):
                b = it.par()
                dve.reciprocal(rz[b][:, :], hid[:, it.at(), :, DH]).then_inc(inv, 1)
                dve.wait_ge(inv, it.at(1))
                if not first:
                    dve.wait_ge(turned, it.at(-1))
                dve.tensor_tensor(hn[b][:, :].rearrange("p (h d) -> p h d", h=HB), hid[:, it.at(), :, 0:DH],
                                  rz[b][:, :, None].to_broadcast([P, HB, DH]), ALU.mult).then_inc(normed, 1)

            def begin(it, first):
                b = it.par()
                if not first:
                    dve.wait_ge(done, it.at(-1))
                dve.wait_ge(proj, it.at(1))
                dve.tensor_tensor(v[b][:, :], ps[:, 2 + b, :], bout[:, :], ALU.add).then_inc(biased, 1)
                dve.wait_ge(biased, it.at(1))
                if not first:
                    dve.wait_ge(added, it.at(-1))
                dve.tensor_scalar(e[b][:, :], v[b][:, :], 0.0, None, ALU.min).then_inc(low, 1)

            def finish(it):
                b = it.par()
                dve.wait_ge(expd, it.at(1))
                dve.scalar_tensor_tensor(e[b][:, :], e[b][:, :], -1.0, x1[:, it.at(), :], ALU.add, ALU.add).then_inc(added, 1)
                dve.wait_ge(added, it.at(1))
                dve.scalar_tensor_tensor(x1[:, it.at(), :], v[b][:, :], 0.0, e[b][:, :], ALU.max, ALU.add).then_inc(done, 1)
            dve.wait_ge(hid_in[0], 16)
            norm(At(0, 0), True)
            norm(At(0, 1), True)
            dve.wait_ge(w_in, 32)
            dve.wait_ge(x_in[0], 16)
            dve.wait_ge(hid_in[1], 16)
            for n in (0, 1):
                norm(At(0, n + 2), False)
                begin(At(0, n), True)
            finish(At(0, 0))
            dve.wait_ge(x_in[1], 16)
            for i, (lo, hi) in list(enumerate(chunks))[2:]:
                dve.wait_ge(hid_in[i], 16)
                dve.wait_ge(x_in[i], 16)
                with dve.Fori(lo // 2 - 1, hi // 2 - 1) as pair:
                    for n in (0, 1):
                        norm(At(pair, n + 2), False)
                        begin(At(pair, n), False)
                        finish(At(pair, n - 1))
            for it in (NT - 2, NT - 1):
                begin(At(0, it), False)
                finish(At(0, it - 1))
            finish(At(0, NT - 1))

        @block.tensor
        def _(pe):
            def turn(it, first):
                b = it.par()
                pe.wait_ge(normed, it.at(1))
                if not first:
                    pe.wait_ge(turned_out, it.at(-1))
                for k in range(KT):
                    last = pe.transpose(ps[:, b, k * P:(k + 1) * P], hn[b][:, k * P:(k + 1) * P], t["ident"][:, :])
                last.then_inc(turned, 1)

            def project(it, first):
                b = it.par()
                pe.wait_ge(turned_out, it.at(1))
                if not first:
                    pe.wait_ge(biased, it.at(-1))
                for k in range(KT):
                    last = pe.matmul(ps[:, 2 + b, :], hT[b][:, k, :], wout[:, k, :], start=(k == 0), stop=(k == KT - 1))
                last.then_inc(proj, 1)
            turn(At(0, 0), True)
            turn(At(0, 1), True)
            pe.wait_ge(w_in, 32)
            project(At(0, 0), True)
            turn(At(0, 2), False)
            project(At(0, 1), True)
            turn(At(0, 3), False)
            with pe.Fori(0, (NT - 4) // 2) as pair:
                for n in (2, 3):
                    project(At(pair, n), False)
                    turn(At(pair, n + 2), False)
            for it in (NT - 2, NT - 1):
                project(At(0, it), False)

        @block.scalar
        def _(act):
            def copy(it, first):
                b = it.par()
                act.wait_ge(turned, it.at(1))
                if not first:
                    act.wait_ge(proj, it.at(-1))
                act.activation(hT[b][:, :, :], ps[:, b, :].rearrange("p (k i) -> p k i", k=KT), ACT.Copy).then_inc(turned_out, 1)

            def exp(it):
                b = it.par()
                act.wait_ge(low, it.at(1))
                act.activation(e[b][:, :], e[b][:, :], ACT.Exp).then_inc(expd, 1)
            copy(At(0, 0), True)
            copy(At(0, 1), True)
            with act.Fori(0, (NT - 2) // 2) as pair:
                for n in (0, 1):
                    exp(At(pair, n))
                    copy(At(pair, n + 2), False)
            for it in (NT - 2, NT - 1):
                exp(At(0, it))

        @block.gpsimd
        def _(pool):
            with pool.Fori(0, NT // 2) as pair:
                for n in (0, 1):
                    it = At(pair, n)
                    pool.wait_ge(done, it.at(1))
                    pool.dma_start(out[it.rows(), :], x1[:, it.at(), :]).then_inc(y_out, 16)
            pool.wait_ge(y_out, 16 * NT)


INS = ["x", "adj", "L0_gnn_rel_pair_index", "L0_gnn_Wq", "L0_gnn_bq", "L0_gnn_Wk", "L0_gnn_bk", "L1_gnn_W_seq",
       "L1_gnn_a1", "L1_gnn_a2", "L1_gnn_W_out", "L1_gnn_b_out"]


def build(nc, io, out, kind="Internal", upto=5):
    dram = lambda name, shape, dt=F32: nc.dram_tensor(name, shape, dt, kind=kind).ap()
    t = {
        "q_parts": dram("q_parts", [3, D, NE], BF16),
        "rel_planes": [dram(f"rel_planes{i}", [NE, NE], U8) for i in range(PLANES)], "x1": dram("x1", [N, D]),
        "s1_rows": dram("s1_rows", [HB, N]), "hidden": dram("hidden", [N, HB, DZ]),
    }
    with ExitStack() as c:
        t["ident"] = c.enter_context(nc.sbuf_tensor("ident", [P, P], F32))
        t["identb"] = c.enter_context(nc.sbuf_tensor("identb", [P, P], BF16))
        t["offdiag"] = c.enter_context(nc.sbuf_tensor("offdiag", [P, P], BF16))
        ps = c.enter_context(nc.psum_tensor("psum", [P, 8, 512], F32))
        s = {n: c.enter_context(nc.semaphore(n)) for n in ("zeroed", "const", "lasting")}
        t["stats"] = c.enter_context(nc.sbuf_tensor("stats", [P, NT, 6], F32))
        make_constants(nc, t, s)
        with ExitStack() as first:
            t["h"] = first.enter_context(nc.sbuf_tensor("h", [P, NT, D], F32))
            f = FirstLayer(nc, first)
            with ExitStack() as part:
                stage1(nc, part, io, t, s, ps, f)
            if upto >= 2:
                with ExitStack() as part:
                    stage2(nc, part, io, t, s, ps, f)
        if upto >= 3:
            with ExitStack() as second:
                sb = lambda name, shape, dt=F32: second.enter_context(nc.sbuf_tensor(name, shape, dt))
                t["seq"] = sb("seq", [P, NT, D])
                t["adjT"] = sb("adjT", [P, NT, N], BF16)
                for name in ("ns2", "wa", "wb"):
                    t[name] = sb(name, [P, HB, NT])
                for name in ("ea", "eb"):
                    t[name] = sb(name, [P, NT, HB])
                t["lasting"] = s["lasting"]
                with ExitStack() as part:
                    stage3(nc, part, io, t, s, ps)
                if upto >= 4:
                    with ExitStack() as part:
                        stage4(nc, part, io, t, s, ps)
        if upto >= 5:
            with ExitStack() as part:
                stage5(nc, part, io, out, t, s, ps)


def kernel(**inputs):
    import numpy as np
    import concourse.bacc as bacc
    from concourse.bass_utils import run_bass_kernel_spmd as run

    nc = bacc.Bacc("TRN2", target_bir_lowering=False, num_devices=1)
    arrays, io = {}, {}
    for name in INS:
        a = np.ascontiguousarray(inputs[name])
        arrays[f"in_{name}"] = a
        io[name] = nc.dram_tensor(f"in_{name}", a.shape, mybir.dt.from_np(a.dtype), kind="ExternalInput").ap()
    out = nc.dram_tensor("out", [N, D], F32, kind="ExternalOutput").ap()
    build(nc, io, out)
    return run(nc, [arrays], core_ids=[0]).results[0]["out"]
```
